# Optimizing a Trainium2 kernel written in Bass

```python
import numpy as np
import jax
import jax.numpy as jnp

def _softmax(x, axis=-1):
    return jax.nn.softmax(x, axis=axis)

def _gelu(x):
    return jax.nn.gelu(x, approximate=True)

def _silu(x):
    return jax.nn.silu(x)

def _sigmoid(x):
    return jax.nn.sigmoid(x)

def _layernorm(x, axis=-1, eps=1e-05):
    m = jnp.mean(x, axis=axis, keepdims=True)
    v = jnp.var(x, axis=axis, keepdims=True)
    return (x - m) / jnp.sqrt(v + eps)

def _scatter_add(tgt, idx, src, axis=0):
    return tgt.at[idx].add(src)

def _segment_sum(src, seg, n):
    return jax.ops.segment_sum(src, seg, n)
kernel_name = 'mk_decoder_postln_d1_seqx_r8_eb86b8'

def setup_inputs(seed: int=0):
    np.random.seed(seed)
    _w = jnp.asarray

    def _rec_inputs():
        import jax
        import jax.numpy as jnp
        _rk = jax.random.key(seed)
        x = -0.0002928 + 1 * jax.random.normal(jax.random.fold_in(_rk, 1), (8, 128, 512), jnp.float32)
        _lenS = 128 - jax.random.randint(jax.random.fold_in(_rk, 7), (8,), 0, max(1, 128 // 4) + 1, jnp.int32)
        _lenS2 = 128 - jax.random.randint(jax.random.fold_in(_rk, 8), (8,), 0, max(1, 128 // 4) + 1, jnp.int32)
        _ctx_4096P = jax.random.normal(jax.random.fold_in(_rk, 11), (8, 16, 512), jnp.float32)
        _ctx_4096c = jax.random.dirichlet(jax.random.fold_in(_rk, 511), 0.3 * jnp.ones((16,), jnp.float32), (8, 128))
        _ctx_4096t = jnp.einsum('bsk,bkd->bsd', _ctx_4096c, _ctx_4096P)
        _ctx_4096t = _ctx_4096t * jax.lax.rsqrt(jnp.mean(jnp.square(_ctx_4096t)) + 1e-12) * 0.953939
        ctx_4096 = -2.8382e-05 + 0.999851 * (_ctx_4096t + 0.3 * jax.random.normal(jax.random.fold_in(_rk, 611), (8, 128, 512), jnp.float32))
        _validS = jnp.arange(128)[None, :] < _lenS[:, None]
        _validS2 = jnp.arange(128)[None, :] < _lenS2[:, None]
        _causal = jnp.tril(jnp.ones((128, 128), dtype=bool))
        mask_1x1xSxS2_ff0 = jnp.where(jnp.ones((1, 1, 128, 128), dtype=bool), 0.0, -1000000000.0).astype(jnp.float32)
        return (x, ctx_4096, mask_1x1xSxS2_ff0)
    x, ctx_4096, mask_1x1xSxS2_ff0 = _rec_inputs()

    def _L0_attn_setup():
        import jax, jax.numpy as jnp
        import numpy as np
        D_MODEL = 512
        D_XB = 128
        D_INNER = 512
        HEADDIM = 128
        DSTATE = 128
        NHEADS = D_INNER // HEADDIM
        DCONV = 4
        INTER = 1792
        EPS = 1e-05
        CHUNK = 128

        def rmsnorm(x, w):
            return x * jax.lax.rsqrt(jnp.mean(x * x, axis=-1, keepdims=True) + EPS) * w

        def silu(x):
            return x * jax.nn.sigmoid(x)

        def mamba2(x, w_in, conv_w, conv_b, A_log, D, dt_bias, w_out):
            B, L, _ = x.shape
            H, P, N = (NHEADS, HEADDIM, DSTATE)
            G = D_XB // P
            rep = H // G
            zxbcdt = x @ w_in.T
            z, xs, Bs, Cs, dt = jnp.split(zxbcdt, [D_INNER, D_INNER + D_XB, D_INNER + 2 * D_XB, 2 * D_INNER + 2 * D_XB], axis=-1)
            xBC = jnp.concatenate([xs, Bs, Cs], axis=-1)
            conv = jax.lax.conv_general_dilated(xBC.transpose(0, 2, 1), conv_w[:, None, :], (1,), [(DCONV - 1, 0)], feature_group_count=conv_w.shape[0])
            xBC = silu(conv.transpose(0, 2, 1) + conv_b)
            xs, Bs, Cs = jnp.split(xBC, [D_XB, 2 * D_XB], axis=-1)
            dt = jax.nn.softplus(dt + dt_bias)
            A = -jnp.exp(A_log)
            xh = jnp.repeat(xs.reshape(B, L, G, P), rep, axis=2)
            Bh = jnp.repeat(Bs.reshape(B, L, G, N), rep, axis=2)
            Ch = Cs.reshape(B, L, H, N)
            c, Q = (L // CHUNK, CHUNK)
            a = (dt * A).reshape(B, c, Q, H).transpose(0, 1, 3, 2)
            dtc = dt.reshape(B, c, Q, H).transpose(0, 1, 3, 2)
            Xc = xh.reshape(B, c, Q, H, P).transpose(0, 1, 3, 2, 4)
            Bc = Bh.reshape(B, c, Q, H, N).transpose(0, 1, 3, 2, 4)
            Cc = Ch.reshape(B, c, Q, H, N).transpose(0, 1, 3, 2, 4)
            cs = jnp.cumsum(a, axis=-1)
            tri = jnp.tril(jnp.ones((Q, Q), bool))
            Ldec = jnp.where(tri, jnp.exp(cs[..., :, None] - cs[..., None, :]), 0.0)
            Xdt = Xc * dtc[..., None]
            att = jnp.einsum('bchqn,bchkn->bchqk', Cc, Bc) * Ldec
            Yd = jnp.einsum('bchqk,bchkp->bchqp', att, Xdt)
            dec_end = jnp.exp(cs[..., -1:] - cs)
            states = jnp.einsum('bchq,bchqn,bchqp->bchpn', dec_end, Bc, Xdt)
            g = jnp.exp(cs[..., -1])

            def step(S, inp):
                gk, st = inp
                return (gk[:, :, None, None] * S + st, S)
            S0 = jnp.zeros((B, H, P, N), x.dtype)
            _, prev = jax.lax.scan(step, S0, (g.transpose(1, 0, 2), states.transpose(1, 0, 2, 3, 4)))
            prev = prev.transpose(1, 0, 2, 3, 4)
            Yo = jnp.einsum('bchqn,bchpn,bchq->bchqp', Cc, prev, jnp.exp(cs))
            Y = (Yd + Yo).transpose(0, 1, 3, 2, 4).reshape(B, L, H, P)
            Y = Y + D[:, None] * xh
            y = Y.reshape(B, L, D_INNER) * silu(z)
            return y @ w_out.T
        key = jax.random.key(seed)
        ks = jax.random.split(key, 10)
        B, L = (2, 256)
        proj_out = 2 * D_INNER + 2 * D_XB + NHEADS
        conv_dim = 2 * D_XB + D_INNER
        return {'hidden_states': jax.random.normal(ks[0], (B, L, D_MODEL), jnp.float32), 'w_in': jax.random.normal(ks[1], (proj_out, D_MODEL), jnp.float32) * 0.02, 'conv_w': jax.random.normal(ks[2], (conv_dim, DCONV), jnp.float32) * 0.1, 'conv_b': jnp.zeros((conv_dim,), jnp.float32), 'A_log': jnp.log(jnp.arange(1, NHEADS + 1, dtype=jnp.float32)), 'D': jnp.ones((NHEADS,), jnp.float32), 'dt_bias': jax.random.normal(ks[3], (NHEADS,), jnp.float32) * 0.1, 'w_out': jax.random.normal(ks[4], (D_MODEL, D_INNER), jnp.float32) * 0.02, 'ln1_w': jnp.ones((D_MODEL,), jnp.float32), 'ln2_w': jnp.ones((D_MODEL,), jnp.float32), 'gate_w': jax.random.normal(ks[5], (INTER, D_MODEL), jnp.float32) * 0.02, 'up_w': jax.random.normal(ks[6], (INTER, D_MODEL), jnp.float32) * 0.02, 'down_w': jax.random.normal(ks[7], (D_MODEL, INTER), jnp.float32) * 0.02}
    _L0_attn_all = _L0_attn_setup()
    _L0_attn_in = {k: v for k, v in _L0_attn_all.items() if k in ('w_in', 'conv_w', 'conv_b', 'A_log', 'D', 'dt_bias', 'w_out', 'ln1_w', 'ln2_w', 'gate_w', 'up_w', 'down_w')}
    del _L0_attn_all

    def _L0_xattn_setup():
        import jax, jax.numpy as jnp
        import numpy as np
        B, Q, K, D = (1, 128, 6404, 512)
        H, KVH, HD = (32, 8, 128)
        GROUPS = H // KVH
        EPS = 1e-05

        def _rmsnorm(x, w):
            xf = x.astype(jnp.float32)
            var = jnp.mean(xf * xf, axis=-1, keepdims=True)
            return (xf * jax.lax.rsqrt(var + EPS)).astype(x.dtype) * w
        key = jax.random.key(seed)
        ks = jax.random.split(key, 8)
        s = 0.02
        return {'hidden_states': jax.random.normal(ks[0], (B, Q, D), jnp.float32), 'cross_attention_states': jax.random.normal(ks[1], (B, K, D), jnp.float32), 'attention_mask': jnp.zeros((B, 1, Q, K), jnp.float32), 'Wq': jax.random.normal(ks[2], (H * HD, D), jnp.float32) * s, 'Wk': jax.random.normal(ks[3], (KVH * HD, D), jnp.float32) * s, 'Wv': jax.random.normal(ks[4], (KVH * HD, D), jnp.float32) * s, 'Wo': jax.random.normal(ks[5], (D, H * HD), jnp.float32) * s, 'q_norm_w': jnp.ones((HD,), jnp.float32), 'k_norm_w': jnp.ones((HD,), jnp.float32)}
    _L0_xattn_all = _L0_xattn_setup()
    _L0_xattn_in = {k: v for k, v in _L0_xattn_all.items() if k in ('Wq', 'Wk', 'Wv', 'Wo', 'q_norm_w', 'k_norm_w')}
    del _L0_xattn_all

    def _L0_ffn_setup():
        import jax, jax.numpy as jnp
        import numpy as np
        LORA_SCALE = 16.0 / jnp.sqrt(16.0)
        TOP_K = 2
        key = jax.random.key(seed)
        k1, k2, k3, k4 = jax.random.split(key, 4)
        B_, S, D, O, E, R = (4, 256, 512, 512, 4, 16)
        x = jax.random.normal(k1, (B_, S, D), dtype=jnp.float32)
        router_w = jax.random.normal(k2, (E, D), dtype=jnp.float32) * 0.02
        A = jax.random.normal(k3, (E, R, D), dtype=jnp.float32) * 0.02
        B = jax.random.normal(k4, (O,), dtype=jnp.float32)
        B = jax.random.normal(k4, (E, O, R), dtype=jnp.float32) * 0.02
        return {'x': x, 'router_w': router_w, 'A': A, 'B': B}
    _L0_ffn_all = _L0_ffn_setup()
    _L0_ffn_in = {k: v for k, v in _L0_ffn_all.items() if k in ('router_w', 'A', 'B')}
    del _L0_ffn_all
    return {'x': x, 'ctx_4096': ctx_4096, 'mask_1x1xSxS2_ff0': mask_1x1xSxS2_ff0, 'L0_attn_w_in': _L0_attn_in['w_in'], 'L0_attn_conv_w': _L0_attn_in['conv_w'], 'L0_attn_conv_b': _L0_attn_in['conv_b'], 'L0_attn_A_log': _L0_attn_in['A_log'], 'L0_attn_D': _L0_attn_in['D'], 'L0_attn_dt_bias': _L0_attn_in['dt_bias'], 'L0_attn_w_out': _L0_attn_in['w_out'], 'L0_attn_ln1_w': _L0_attn_in['ln1_w'], 'L0_attn_ln2_w': _L0_attn_in['ln2_w'], 'L0_attn_gate_w': _L0_attn_in['gate_w'], 'L0_attn_up_w': _L0_attn_in['up_w'], 'L0_attn_down_w': _L0_attn_in['down_w'], 'L0_xattn_Wq': _L0_xattn_in['Wq'], 'L0_xattn_Wk': _L0_xattn_in['Wk'], 'L0_xattn_Wv': _L0_xattn_in['Wv'], 'L0_xattn_Wo': _L0_xattn_in['Wo'], 'L0_xattn_q_norm_w': _L0_xattn_in['q_norm_w'], 'L0_xattn_k_norm_w': _L0_xattn_in['k_norm_w'], 'L0_ffn_router_w': _L0_ffn_in['router_w'], 'L0_ffn_A': _L0_ffn_in['A'], 'L0_ffn_B': _L0_ffn_in['B']}

def reference(x, ctx_4096, mask_1x1xSxS2_ff0, L0_attn_w_in, L0_attn_conv_w, L0_attn_conv_b, L0_attn_A_log, L0_attn_D, L0_attn_dt_bias, L0_attn_w_out, L0_attn_ln1_w, L0_attn_ln2_w, L0_attn_gate_w, L0_attn_up_w, L0_attn_down_w, L0_xattn_Wq, L0_xattn_Wk, L0_xattn_Wv, L0_xattn_Wo, L0_xattn_q_norm_w, L0_xattn_k_norm_w, L0_ffn_router_w, L0_ffn_A, L0_ffn_B):
    import jax
    import jax.numpy as jnp

    def _L0_attn_ref(hidden_states, w_in, conv_w, conv_b, A_log, D, dt_bias, w_out, ln1_w, ln2_w, gate_w, up_w, down_w):
        import jax, jax.numpy as jnp
        import numpy as np
        D_MODEL = 512
        D_XB = 128
        D_INNER = 512
        HEADDIM = 128
        DSTATE = 128
        NHEADS = D_INNER // HEADDIM
        DCONV = 4
        INTER = 1792
        EPS = 1e-05
        CHUNK = 128

        def rmsnorm(x, w):
            return x * jax.lax.rsqrt(jnp.mean(x * x, axis=-1, keepdims=True) + EPS) * w

        def silu(x):
            return x * jax.nn.sigmoid(x)

        def mamba2(x, w_in, conv_w, conv_b, A_log, D, dt_bias, w_out):
            B, L, _ = x.shape
            H, P, N = (NHEADS, HEADDIM, DSTATE)
            G = D_XB // P
            rep = H // G
            zxbcdt = x @ w_in.T
            z, xs, Bs, Cs, dt = jnp.split(zxbcdt, [D_INNER, D_INNER + D_XB, D_INNER + 2 * D_XB, 2 * D_INNER + 2 * D_XB], axis=-1)
            xBC = jnp.concatenate([xs, Bs, Cs], axis=-1)
            conv = jax.lax.conv_general_dilated(xBC.transpose(0, 2, 1), conv_w[:, None, :], (1,), [(DCONV - 1, 0)], feature_group_count=conv_w.shape[0])
            xBC = silu(conv.transpose(0, 2, 1) + conv_b)
            xs, Bs, Cs = jnp.split(xBC, [D_XB, 2 * D_XB], axis=-1)
            dt = jax.nn.softplus(dt + dt_bias)
            A = -jnp.exp(A_log)
            xh = jnp.repeat(xs.reshape(B, L, G, P), rep, axis=2)
            Bh = jnp.repeat(Bs.reshape(B, L, G, N), rep, axis=2)
            Ch = Cs.reshape(B, L, H, N)
            c, Q = (L // CHUNK, CHUNK)
            a = (dt * A).reshape(B, c, Q, H).transpose(0, 1, 3, 2)
            dtc = dt.reshape(B, c, Q, H).transpose(0, 1, 3, 2)
            Xc = xh.reshape(B, c, Q, H, P).transpose(0, 1, 3, 2, 4)
            Bc = Bh.reshape(B, c, Q, H, N).transpose(0, 1, 3, 2, 4)
            Cc = Ch.reshape(B, c, Q, H, N).transpose(0, 1, 3, 2, 4)
            cs = jnp.cumsum(a, axis=-1)
            tri = jnp.tril(jnp.ones((Q, Q), bool))
            Ldec = jnp.where(tri, jnp.exp(cs[..., :, None] - cs[..., None, :]), 0.0)
            Xdt = Xc * dtc[..., None]
            att = jnp.einsum('bchqn,bchkn->bchqk', Cc, Bc) * Ldec
            Yd = jnp.einsum('bchqk,bchkp->bchqp', att, Xdt)
            dec_end = jnp.exp(cs[..., -1:] - cs)
            states = jnp.einsum('bchq,bchqn,bchqp->bchpn', dec_end, Bc, Xdt)
            g = jnp.exp(cs[..., -1])

            def step(S, inp):
                gk, st = inp
                return (gk[:, :, None, None] * S + st, S)
            S0 = jnp.zeros((B, H, P, N), x.dtype)
            _, prev = jax.lax.scan(step, S0, (g.transpose(1, 0, 2), states.transpose(1, 0, 2, 3, 4)))
            prev = prev.transpose(1, 0, 2, 3, 4)
            Yo = jnp.einsum('bchqn,bchpn,bchq->bchqp', Cc, prev, jnp.exp(cs))
            Y = (Yd + Yo).transpose(0, 1, 3, 2, 4).reshape(B, L, H, P)
            Y = Y + D[:, None] * xh
            y = Y.reshape(B, L, D_INNER) * silu(z)
            return y @ w_out.T
        res = hidden_states
        h = rmsnorm(hidden_states, ln1_w)
        h = res + mamba2(h, w_in, conv_w, conv_b, A_log, D, dt_bias, w_out)
        res = h
        h2 = rmsnorm(h, ln2_w)
        mlp = silu(h2 @ gate_w.T) * (h2 @ up_w.T) @ down_w.T
        return res + mlp

    def _L0_xattn_ref(hidden_states, cross_attention_states, attention_mask, Wq, Wk, Wv, Wo, q_norm_w, k_norm_w):
        import jax, jax.numpy as jnp
        import numpy as np
        B, Q, K, D = (1, 128, 6404, 512)
        H, KVH, HD = (32, 8, 128)
        GROUPS = H // KVH
        EPS = 1e-05

        def _rmsnorm(x, w):
            xf = x.astype(jnp.float32)
            var = jnp.mean(xf * xf, axis=-1, keepdims=True)
            return (xf * jax.lax.rsqrt(var + EPS)).astype(x.dtype) * w
        bsz, q_len, _ = hidden_states.shape
        kv_len = cross_attention_states.shape[1]
        q = (hidden_states @ Wq.T).reshape(bsz, q_len, H, HD).transpose(0, 2, 1, 3)
        k = (cross_attention_states @ Wk.T).reshape(bsz, kv_len, KVH, HD).transpose(0, 2, 1, 3)
        v = (cross_attention_states @ Wv.T).reshape(bsz, kv_len, KVH, HD).transpose(0, 2, 1, 3)
        q = _rmsnorm(q, q_norm_w)
        k = jnp.repeat(k, GROUPS, axis=1)
        v = jnp.repeat(v, GROUPS, axis=1)
        k = _rmsnorm(k, k_norm_w)
        scale = 1.0 / np.sqrt(HD)
        scores = jnp.einsum('bhqd,bhkd->bhqk', q, k) * scale
        scores = scores + attention_mask[:, :, :, :kv_len]
        probs = jax.nn.softmax(scores.astype(jnp.float32), axis=-1).astype(q.dtype)
        out = jnp.einsum('bhqk,bhkd->bhqd', probs, v)
        out = out.transpose(0, 2, 1, 3).reshape(bsz, q_len, H * HD)
        return out @ Wo.T

    def _L0_ffn_ref(x, router_w, A, B):
        import jax, jax.numpy as jnp
        import numpy as np
        LORA_SCALE = 16.0 / jnp.sqrt(16.0)
        TOP_K = 2
        D = x.shape[-1]
        flat = x.reshape(-1, D)
        logits = flat @ router_w.T
        topk_vals, topk_idx = jax.lax.top_k(logits, TOP_K)
        sparse = jnp.full_like(logits, -jnp.inf)
        rows = jnp.arange(logits.shape[0])[:, None]
        sparse = sparse.at[rows, topk_idx].set(topk_vals)
        gates = jax.nn.softmax(sparse, axis=-1)
        mid = jnp.einsum('tf,erf->ter', flat, A)
        all_deltas = jnp.einsum('ter,eor->teo', mid, B) * LORA_SCALE
        delta = jnp.einsum('te,teo->to', gates, all_deltas)
        return delta.reshape(*x.shape[:-1], -1)
    x = _layernorm(x + _L0_attn_ref(x, L0_attn_w_in, L0_attn_conv_w, L0_attn_conv_b, L0_attn_A_log, L0_attn_D, L0_attn_dt_bias, L0_attn_w_out, L0_attn_ln1_w, L0_attn_ln2_w, L0_attn_gate_w, L0_attn_up_w, L0_attn_down_w), axis=-1)
    x = _layernorm(x + _L0_xattn_ref(x, ctx_4096, mask_1x1xSxS2_ff0, L0_xattn_Wq, L0_xattn_Wk, L0_xattn_Wv, L0_xattn_Wo, L0_xattn_q_norm_w, L0_xattn_k_norm_w), axis=-1)
    x = _layernorm(x + _L0_ffn_ref(x, L0_ffn_router_w, L0_ffn_A, L0_ffn_B), axis=-1)
    return x

_drawn_inputs = setup_inputs


def setup_inputs(seed=0):
    import zlib

    import numpy as np

    out = dict(_drawn_inputs(seed))
    spreads = {'L0_attn_conv_b': (0.0, 0.8),
     'L0_attn_D': (1.0, 0.6),
     'L0_attn_ln1_w': (1.0, 0.6),
     'L0_attn_ln2_w': (1.0, 0.6),
     'L0_xattn_q_norm_w': (1.0, 0.6),
     'L0_xattn_k_norm_w': (1.0, 0.6)}
    factors = {'L0_attn_w_in': 6.654,
     'L0_attn_conv_w': 8.0,
     'L0_attn_A_log': 8.0,
     'L0_attn_dt_bias': 8.0,
     'L0_attn_w_out': 6.49,
     'L0_attn_gate_w': 64.0,
     'L0_attn_up_w': 64.0,
     'L0_attn_down_w': 64.0}
    for name, (base, spread) in spreads.items():
        noise = np.random.default_rng([zlib.crc32(name.encode()), seed]).standard_normal(out[name].shape)
        drawn = base * np.exp(spread * noise) if base else spread * noise
        out[name] = jnp.asarray(drawn.astype(out[name].dtype))
    for name, factor in factors.items():
        out[name] = (out[name] * factor).astype(out[name].dtype)
    return out
```

```python
from contextlib import ExitStack

import concourse.bass as bass
from concourse import mybir

B, L, DM = 8, 128, 512
P = 128
KT = DM // P
HALF = 4
NTOK = HALF * L
NH, DSTATE, DCONV = 4, 128, 4
NCONV = 6
NPIECE = NCONV + NH
INTER = 1792
MLP_IT = INTER // (2 * P)
GROUPS, GH, HD = 8, 4, 128
NE, RANK = 4, 16
EPS = 1e-5
LORA_SCALE = 4.0
ATANH_TERMS = 8


def build_program(nc, x, ctx_t, mask, consts, chan, rows, w_dt, w_in, w_out, w_gu, w_dn,
                  w_q, w_kv, w_o, w_ra, w_b, out):
    fp32 = mybir.dt.float32
    f32r = mybir.dt.float32r
    bf16 = mybir.dt.bfloat16
    ALU = mybir.AluOpType
    ACT = mybir.ActivationFunctionType
    X = mybir.AxisListType.X

    ctx = ExitStack()
    with ctx:
        def sb(where, name, shape, dt=fp32):
            return where.enter_context(nc.sbuf_tensor(name, shape, dt))

        def sem(name):
            return ctx.enter_context(nc.semaphore(name))

        def f32(ap):
            return ap.bitcast(fp32)

        act_hi = sb(ctx, "act_hi", [P, KT, B * L], f32r)
        act_lo = sb(ctx, "act_lo", [P, KT, B * L], f32r)
        res = sb(ctx, "res", [P, B, DM])
        w_hi = sb(ctx, "w_hi", [P, 5120], f32r)
        w_lo = sb(ctx, "w_lo", [P, 5120], f32r)
        raw_a = sb(ctx, "raw_a", [P, 2048])
        raw_b = sb(ctx, "raw_b", [P, 2048])
        cst = sb(ctx, "cst", [P, 3 * P])
        ident, tri_half, strict = cst[:, 0:P], cst[:, P:2 * P], cst[:, 2 * P:3 * P]
        mask_sb = sb(ctx, "mask_sb", [P, L])
        chan_sb = sb(ctx, "chan_sb", [P, NCONV * DCONV + NCONV + 2])
        ones = sb(ctx, "ones", [P, 1])
        qk_w = sb(ctx, "qk_w", [P, 1])
        pow_m = sb(ctx, "pow_m", [P, 16])
        xn = sb(ctx, "xn", [P, 2, DM])
        junk = sb(ctx, "junk", [P, 2, DM], bf16)
        stat = sb(ctx, "stat", [P, 32])
        var = sb(ctx, "var", [P, 48])
        rstd = sb(ctx, "rstd", [P, 48])
        bst = sb(ctx, "bst", [P, 2, 6])
        mv = sb(ctx, "mv", [P, 48, 2])

        with ExitStack() as m:
            row_sb = sb(m, "row_sb", [P, 2 * DM + 3 * NH])
            wdt_raw = sb(m, "wdt_raw", [P, KT * NH])
            wdt_hi = sb(m, "wdt_hi", [P, KT * NH], f32r)
            wdt_lo = sb(m, "wdt_lo", [P, KT * NH], f32r)
            cw = sb(m, "cw", [P, NCONV * DCONV + NCONV])
            a2 = sb(m, "a2", [P, NH])
            d2 = sb(m, "d2", [P, NH])
            dt_sb = sb(m, "dt_sb", [P, B * NH])
            sp = sb(m, "sp", [P, 7, HALF * NH])
            pre = sb(m, "pre", [P, 2, HALF, L + DCONV - 1])
            cbuf = sb(m, "cbuf", [P, 2, NTOK])
            th = sb(m, "th", [P, 2, NTOK])
            xbc = sb(m, "xbc", [P, NCONV, NTOK])
            zt = sb(m, "zt", [P, NH, B * L])
            xtok = sb(m, "xtok", [P, 2, P])
            md = sb(m, "md", [P, 2, NH, L])
            em = sb(m, "em", [P, 2, NH, L])
            att = sb(m, "att", [P, NH, L])
            yb = sb(m, "yb", [P, 2, NH, L])
            y_hi = sb(m, "y_hi", [P, 4, NH, L], f32r)
            y_lo = sb(m, "y_lo", [P, 4, NH, L], f32r)

        ctx_hi = sb(ctx, "ctx_hi", [P, KT, B * L], f32r)
        ctx_lo = sb(ctx, "ctx_lo", [P, KT, B * L], f32r)
        with ExitStack() as m:
            h_hi = sb(m, "h_hi", [P, 2, B * L], f32r)
            h_lo = sb(m, "h_lo", [P, 2, B * L], f32r)
            sg = sb(m, "sg", [P, 2, NTOK])
            hb = sb(m, "hb", [P, 2, NTOK])
            xre = sb(m, "xre", [P, 2, DM])

        with ExitStack() as m:
            q_hi = sb(m, "q_hi", [P, 2, GH, NTOK], f32r)
            q_lo = sb(m, "q_lo", [P, 2, GH, NTOK], f32r)
            k_hi = sb(m, "k_hi", [P, 2, NTOK], f32r)
            k_lo = sb(m, "k_lo", [P, 2, NTOK], f32r)
            v_hi = sb(m, "v_hi", [P, 2, HALF, HD], f32r)
            v_lo = sb(m, "v_lo", [P, 2, HALF, HD], f32r)
            kraw = sb(m, "kraw", [P, HALF, HD])
            qsq = xn[:, 0, :]
            qv = sb(m, "qv", [P, 2 * GH, HALF])
            qr = sb(m, "qr", [P, 2 * GH, HALF])
            kv = sb(m, "kv", [P, 3, HALF])
            pb = sb(m, "pb", [P, 2, GH, L])
            nmax = sb(m, "nmax", [P, 2, GH])
            psum_ = sb(m, "psum_", [P, 2, GH])
            prec = sb(m, "prec", [P, 2, GH])
            pt_hi = sb(m, "pt_hi", [P, GH * L], f32r)
            pt_lo = sb(m, "pt_lo", [P, GH * L], f32r)
            ot_hi = sb(m, "ot_hi", [P, GH * L], f32r)
            ot_lo = sb(m, "ot_lo", [P, GH * L], f32r)

        with ExitStack() as m:
            x2t = sb(m, "x2t", [P, B, KT, P])
            ra_sb = sb(m, "ra_sb", [P, KT, NE + NE * RANK])
            bl_sb = sb(m, "bl_sb", [NE * RANK, DM])
            cmp_m = sb(m, "cmp_m", [P, 2, NE, NE])
            lg = sb(m, "lg", [P, B, NE])
            c1 = sb(m, "c1", [P, B, NE, NE])
            c2 = sb(m, "c2", [P, B, NE, NE])
            rank_t = sb(m, "rank_t", [P, B, NE])
            lmax = sb(m, "lmax", [P, B])
            ge = sb(m, "ge", [P, B, NE])
            gsum = sb(m, "gsum", [P, B])
            mid = sb(m, "mid", [P, B, NE, RANK])
            midt = sb(m, "midt", [NE * RANK, 2, P])

        bank = [ctx.enter_context(nc.psum_tensor(f"bank{i}", [P, 512], fp32)) for i in range(8)]

        ld_x = [sem(f"ld_x{b}") for b in range(B)]
        ld_small = [sem(f"ld_small{i}") for i in range(5)]
        ld_win = [sem(f"ld_win{i}") for i in range(8)]
        ld_wout = sem("ld_wout")
        ld_gu = sem("ld_gu")
        ld_dn = sem("ld_dn")
        ld_ctx = [sem("ld_ctx0"), sem("ld_ctx1")]
        ld_xre = [sem("ld_xre0"), sem("ld_xre1")]
        ld_q = sem("ld_q")
        ld_kv = sem("ld_kv")
        ld_o = sem("ld_o")
        ld_lora = [sem("ld_lora0"), sem("ld_lora1")]
        st_out = sem("st_out")

        n_ssq, n_var, n_rstd, n_x = sem("n_ssq"), sem("n_var"), sem("n_rstd"), sem("n_x")
        n_t, n_hi, n_lo, n_bn, n_mv = sem("n_t"), sem("n_hi"), sem("n_lo"), sem("n_bn"), sem("n_mv")
        res_x, vlo_done = sem("res_x"), sem("vlo_done")
        x_add = sem("x_add")

        dt_w = sem("dt_w")
        win_h, win_l = sem("win_h"), sem("win_l")
        wout_h, wout_l = sem("wout_h"), sem("wout_l")
        gu_h, gu_l = sem("gu_h"), sem("gu_l")
        dn_h, dn_l = sem("dn_h"), sem("dn_l")
        cx_h, cx_l = sem("cx_h"), sem("cx_l")
        wq_h, wq_l = sem("wq_h"), sem("wq_l")
        wkv_h, wkv_l = sem("wkv_h"), sem("wkv_l")
        wo_h, wo_l = sem("wo_h"), sem("wo_l")

        setup_v, setup_a, setup_p = sem("setup_v"), sem("setup_a"), sem("setup_p")
        in_mm, conv_ev, conv_c, conv_th, conv_out = (sem("in_mm"), sem("conv_ev"), sem("conv_c"),
                                                     sem("conv_th"), sem("conv_out"))
        z_th, z_out = sem("z_th"), sem("z_out")
        dt_mm, dt_a, dt_done = sem("dt_mm"), sem("dt_a"), sem("dt_done")
        md_done, xt_mm, xt_ev, cum_mm, exp_done = (sem("md_done"), sem("xt_mm"), sem("xt_ev"),
                                                   sem("cum_mm"), sem("exp_done"))
        em_done, sc_mm, att_done, y_mm, y1_done = (sem("em_done"), sem("sc_mm"), sem("att_done"),
                                                   sem("y_mm"), sem("y1_done"))
        yz_done, yhi_done, ylo_done = sem("yz_done"), sem("yhi_done"), sem("ylo_done")
        o_mm, o_add = sem("o_mm"), sem("o_add")
        vch = sem("vch")
        gu_mm, silu_done, h_done, hhi_done, hlo_done = (sem("gu_mm"), sem("silu_done"), sem("h_done"),
                                                        sem("hhi_done"), sem("hlo_done"))
        q_mm, qhi_done, qsq_done, qlo_done = sem("q_mm"), sem("qhi_done"), sem("qsq_done"), sem("qlo_done")
        ss_mm, qv_done, qr_done = sem("ss_mm"), sem("qv_done"), sem("qr_done")
        kv_mm, ksq_done, vhi_done, kraw_done = sem("kv_mm"), sem("ksq_done"), sem("vhi_done"), sem("kraw_done")
        kvar_done, kr_done, kn_done = sem("kvar_done"), sem("kr_done"), sem("kn_done")
        kt_mm, khi_done, klo_done = sem("kt_mm"), sem("khi_done"), sem("klo_done")
        s_mm, s_done, max_done, p_exp, p_rec, p_norm = (sem("s_mm"), sem("s_done"), sem("max_done"),
                                                        sem("p_exp"), sem("p_rec"), sem("p_norm"))
        pt_mm, pthi_done, ptlo_done = sem("pt_mm"), sem("pthi_done"), sem("ptlo_done")
        pv_mm, othi_done, otlo_done = sem("pv_mm"), sem("othi_done"), sem("otlo_done")
        d_mm, d_add = sem("d_mm"), sem("d_add")
        f_x2t, ra_mm, lg_done, f_exp, mid_done = (sem("f_x2t"), sem("ra_mm"), sem("lg_done"),
                                                  sem("f_exp"), sem("mid_done"))
        mt_mm, mt_ev, dl_mm, dl_add = sem("mt_mm"), sem("mt_ev"), sem("dl_mm"), sem("dl_add")

        block = ctx.enter_context(nc.Block())

        OUT_COL = 3072
        GU_COL, DN_COL = 0, 2048
        WQ_COL, WKV_COL = 0, 3072
        WO_COL = [2048, 2560, 4096, 4608]

        def mamba_raw(p):
            return raw_b[:, (p - 4) * 512:(p - 3) * 512] if 4 <= p < 8 else raw_a[:, p % 8 * 512:(p % 8 + 1) * 512]

        @block.sync
        def _(sp_eng):
            def load_x(b):
                sp_eng.dma_start(res[:, b, :], x[b]).then_inc(ld_x[b], 16)

            def load_win(p):
                if p >= 8:
                    sp_eng.wait_ge(win_l, p - 7)
                sp_eng.dma_start(mamba_raw(p), w_in[p]).then_inc(ld_win[p % 8], 16)

            load_x(0)
            sp_eng.dma_start(cst[:, :], consts).then_inc(ld_small[0], 16)
            sp_eng.dma_start(row_sb[:, :], rows.partition_broadcast(P)).then_inc(ld_small[1], 16)
            load_win(0)
            load_x(1)
            sp_eng.dma_start(chan_sb[:, :], chan).then_inc(ld_small[2], 16)
            sp_eng.dma_start(wdt_raw[:, :], w_dt).then_inc(ld_small[3], 16)
            load_x(2)
            load_win(1)
            load_x(3)
            load_win(2)
            load_win(3)
            sp_eng.dma_start(mask_sb[:, :], mask).then_inc(ld_small[4], 16)
            for b in range(4, 8):
                load_win(b)
                load_x(b)
            load_win(8)
            load_win(9)
            sp_eng.wait_ge(win_l, 8)
            sp_eng.dma_start(raw_b[:, :], w_out).then_inc(ld_wout, 16)
            sp_eng.wait_ge(win_l, 10)
            sp_eng.dma_start(raw_a[:, :], w_gu[0]).then_inc(ld_gu, 16)
            sp_eng.wait_ge(wout_l, 4)
            sp_eng.dma_start(raw_b[:, 0:1024], w_dn[0]).then_inc(ld_dn, 16)

            def load_ctx(i):
                if i >= 2:
                    sp_eng.wait_ge(cx_l, i - 1)
                sp_eng.dma_start(raw_b[:, 1024 + i % 2 * 512:1536 + i % 2 * 512],
                                 ctx_t[i // 2, :, i % 2 * 512:(i % 2 + 1) * 512]).then_inc(ld_ctx[i % 2], 16)

            load_ctx(0)
            load_ctx(1)

            def next_mlp(c):
                sp_eng.wait_ge(dn_l, 2 * c + 2)
                sp_eng.dma_start(raw_b[:, 0:1024], w_dn[bass.ds(c + 1, 1)].rearrange("a p n -> (a p) n"))\
                    .then_inc(ld_dn, 16)
                sp_eng.wait_ge(gu_l, 4 * c + 4)
                sp_eng.dma_start(raw_a[:, :], w_gu[bass.ds(c + 1, 1)].rearrange("a p n -> (a p) n"))\
                    .then_inc(ld_gu, 16)

            sp_eng.wait_ge(gu_l, 4)
            sp_eng.dma_start(raw_a[:, :], w_gu[1]).then_inc(ld_gu, 16)
            for i in range(2, 8):
                load_ctx(i)
            sp_eng.wait_ge(dn_l, 2)
            sp_eng.dma_start(raw_b[:, 0:1024], w_dn[1]).then_inc(ld_dn, 16)
            with sp_eng.Fori(1, MLP_IT - 1) as c:
                next_mlp(c)
            sp_eng.wait_ge(cx_l, 8)
            sp_eng.wait_ge(dn_l, 2 * MLP_IT)
            sp_eng.dma_start(raw_b[:, 0:1024], w_kv[0]).then_inc(ld_kv, 16)
            sp_eng.wait_ge(gu_l, 4 * MLP_IT)
            sp_eng.dma_start(raw_a[:, :], w_q[0]).then_inc(ld_q, 16)
            for b in range(B):
                if b >= 2:
                    sp_eng.wait_ge(x_add, b - 1)
                sp_eng.dma_start(xre[:, b % 2, :], x[b]).then_inc(ld_xre[b % 2], 16)
            sp_eng.wait_ge(wkv_l, 2)
            sp_eng.dma_start(raw_b[:, :], w_o[0]).then_inc(ld_o, 16)

            def next_group(g):
                sp_eng.wait_ge(wq_l, 4 * g + 4)
                sp_eng.dma_start(raw_a[:, :], w_q[bass.ds(g + 1, 1)].rearrange("a p n -> (a p) n"))\
                    .then_inc(ld_q, 16)
                sp_eng.wait_ge(wo_l, 4 * g + 4)
                sp_eng.dma_start(raw_b[:, 0:1024], w_kv[bass.ds(g + 1, 1)].rearrange("a p n -> (a p) n"))\
                    .then_inc(ld_kv, 16)
                sp_eng.wait_ge(wkv_l, 2 * g + 4)
                sp_eng.dma_start(raw_b[:, :], w_o[bass.ds(g + 1, 1)].rearrange("a p n -> (a p) n"))\
                    .then_inc(ld_o, 16)

            with sp_eng.Fori(0, GROUPS - 1) as g:
                next_group(g)
            sp_eng.wait_ge(d_add, 64)
            sp_eng.dma_start(ra_sb[:, :, :], w_ra).then_inc(ld_lora[0], 16)
            sp_eng.dma_start(bl_sb[:, :], w_b).then_inc(ld_lora[1], 16)
            for b in range(B):
                sp_eng.wait_ge(n_x, 33 + b)
                sp_eng.dma_start(out[b], x2t[:, b, :, :].rearrange("p k n -> p (k n)")).then_inc(st_out, 16)
            sp_eng.wait_ge(st_out, 16 * B)

        @block.tensor
        def _(pe):
            mm = nc.tensor.matmul

            def mm3(o, l_hi, l_lo, r_hi, r_lo, first, last):
                mm(o, l_hi, r_hi, start=first, stop=False)
                mm(o, l_hi, r_lo, start=False, stop=False)
                return mm(o, l_lo, r_hi, start=False, stop=last)

            def norm_t(i, banks):
                pe.wait_ge(n_x, i + 1)
                if i >= 2:
                    pe.wait_ge(n_lo, i - 1)
                for k in range(KT):
                    t = nc.tensor.transpose(banks[i % 2][:, k * P:(k + 1) * P],
                                            xn[:, i % 2, k * P:(k + 1) * P], ident)
                t.then_inc(n_t, 1)

            order = [(0, p) for p in range(NPIECE)] + [(1, p) for p in (6, 7, 8, 9, 0, 1, 2, 3, 4, 5)]

            def in_step(f):
                n, p = order[f]
                pe.wait_ge(win_l, p + 1)
                pe.wait_ge(n_lo, 4 * n + 4)
                if f >= 2:
                    pn, pp = order[f - 2]
                    if pp < NCONV:
                        pe.wait_ge(conv_ev, NCONV * pn + pp + 1)
                    else:
                        pe.wait_ge(z_out, NH * pn + pp - NCONV + 1)
                for k in range(KT):
                    c0 = p * 512 + k * P
                    tok = slice(n * NTOK, (n + 1) * NTOK)
                    t = mm3(bank[f % 2][:, :], w_hi[:, c0:c0 + P], w_lo[:, c0:c0 + P],
                            act_hi[:, k, tok], act_lo[:, k, tok], k == 0, k == KT - 1)
                t.then_inc(in_mm, 1)

            def dt_step(n):
                pe.wait_ge(dt_w, 2)
                pe.wait_ge(n_lo, 4 * n + 4)
                if n:
                    pe.wait_ge(dt_a, 1)
                for b in range(HALF):
                    tok = slice((4 * n + b) * L, (4 * n + b + 1) * L)
                    for k in range(KT):
                        t = mm3(bank[7][:, b * NH:(b + 1) * NH], act_hi[:, k, tok], act_lo[:, k, tok],
                                wdt_hi[:, k * NH:(k + 1) * NH], wdt_lo[:, k * NH:(k + 1) * NH],
                                k == 0, k == KT - 1)
                t.then_inc(dt_mm, 1)

            def ssm1(b):
                n, tok = b // HALF, slice(b % HALF * L, (b % HALF + 1) * L)
                pe.wait_ge(conv_out, NCONV * n + NCONV)
                if b:
                    pe.wait_ge(xt_ev, b)
                nc.tensor.transpose(bank[5][:, 0:P], xbc[:, 0, tok], ident).then_inc(xt_mm, 1)
                pe.wait_ge(md_done, b + 1)
                if b:
                    pe.wait_ge(exp_done, b)
                mm(bank[2][:, :], strict, md[:, b % 2, :, :], start=True, stop=True).then_inc(cum_mm, 1)
                if b:
                    pe.wait_ge(att_done, b)
                mm(bank[3][:, :], xbc[:, 1, tok], xbc[:, 2:6, tok], start=True, stop=True).then_inc(sc_mm, 1)

            def ssm2(b):
                pe.wait_ge(att_done, b + 1)
                pe.wait_ge(xt_ev, b + 1)
                if b:
                    pe.wait_ge(y1_done, b)
                mm(bank[4][:, :], xtok[:, b % 2, :], att[:, :, :], start=True, stop=True).then_inc(y_mm, 1)

            def out_step(b):
                pe.wait_ge(wout_l, 4)
                pe.wait_ge(ylo_done, b + 1)
                if b >= 2:
                    pe.wait_ge(o_add, b - 1)
                for k in range(NH):
                    c0 = OUT_COL + k * 512
                    t = mm3(bank[6 + b % 2][:, :], y_hi[:, b % 4, k, :], y_lo[:, b % 4, k, :],
                            w_hi[:, c0:c0 + 512], w_lo[:, c0:c0 + 512], k == 0, k == NH - 1)
                t.then_inc(o_mm, 1)

            pe.wait_ge(ld_small[0], 16)
            for i in range(4):
                norm_t(i, (bank[2], bank[3]))
            in_step(0)
            dt_step(0)
            for f in range(1, 6):
                in_step(f)
            for i in range(4, 8):
                norm_t(i, (bank[2], bank[3]))
            for f in range(6, 10):
                in_step(f)
            dt_step(1)
            pe.wait_ge(n_lo, 8)
            in_step(10)
            in_step(11)
            ssm1(0)
            in_step(12)
            ssm2(0)
            ssm1(1)
            in_step(13)
            ssm2(1)
            ssm1(2)
            in_step(14)
            ssm2(2)
            ssm1(3)
            in_step(15)
            ssm2(3)
            for f in range(16, 20):
                in_step(f)
            pe.wait_ge(dt_a, 2)
            out_step(0)
            ssm1(4)
            out_step(1)
            ssm2(4)
            ssm1(5)
            out_step(2)
            ssm2(5)
            ssm1(6)
            out_step(3)
            ssm2(6)
            ssm1(7)
            out_step(4)
            ssm2(7)
            tb = (bank[0], bank[1])
            pe.wait_ge(conv_ev, 12)
            pe.wait_ge(z_out, 8)
            out_step(5)
            norm_t(8, tb)
            norm_t(9, tb)
            out_step(6)
            norm_t(10, tb)
            norm_t(11, tb)
            out_step(7)
            norm_t(12, tb)
            pe.wait_ge(y1_done, 8)
            pe.wait_ge(xt_ev, 8)
            pe.wait_ge(exp_done, 8)

            def gu_step(c, k, n):
                m_i = 2 * n + k
                pe.wait_ge(gu_l, 4 * c + 2 * k + 2)
                pe.wait_ge(h_done, 4 * c + m_i - 1) if not (isinstance(c, int) and 4 * c + m_i < 2) else None
                tok = slice(n * NTOK, (n + 1) * NTOK)
                for which in range(2):
                    o = bank[(2, 4)[m_i % 2] + which]
                    for kk in range(KT):
                        c0 = GU_COL + (2 * k + which) * 512 + kk * P
                        t = mm3(o[:, :], w_hi[:, c0:c0 + P], w_lo[:, c0:c0 + P],
                                act_hi[:, kk, tok], act_lo[:, kk, tok], kk == 0, kk == KT - 1)
                t.then_inc(gu_mm, 1)

            def dn_step(c, b):
                pe.wait_ge(hlo_done, 4 * c + 2 * (b // HALF) + 2)
                if b == 0:
                    pe.wait_ge(dn_l, 2 * c + 2)
                pe.wait_ge(o_add, 8 + 8 * c + b - 1)
                tok = slice(b * L, (b + 1) * L)
                for k in range(2):
                    c0 = DN_COL + k * 512
                    t = mm3(bank[6 + b % 2][:, :], h_hi[:, k, tok], h_lo[:, k, tok],
                            w_hi[:, c0:c0 + 512], w_lo[:, c0:c0 + 512], k == 0, k == 1)
                t.then_inc(o_mm, 1)

            def mlp_step(c):
                if isinstance(c, int) and c == 0:
                    pe.wait_ge(n_lo, 12)
                    gu_step(c, 0, 0)
                    for i in range(13, 16):
                        norm_t(i, tb)
                    gu_step(c, 1, 0)
                    pe.wait_ge(n_lo, 16)
                else:
                    gu_step(c, 0, 0)
                    gu_step(c, 1, 0)
                gu_step(c, 0, 1)
                gu_step(c, 1, 1)
                for b in range(B):
                    dn_step(c, b)

            mlp_step(0)
            with pe.Fori(1, MLP_IT - 1) as c:
                mlp_step(c)
            mlp_step(MLP_IT - 1)

            def q_step(u, h):
                g, n = u
                hh = h
                pe.wait_ge(wq_l, 4 * g + hh + 1)
                r = 5 * n + hh
                wait_bank(g, r)
                tok = slice(n * NTOK, (n + 1) * NTOK)
                for k in range(KT):
                    c0 = WQ_COL + hh * 512 + k * P
                    t = mm3(bank[r % 2][:, :], w_hi[:, c0:c0 + P], w_lo[:, c0:c0 + P],
                            act_hi[:, k, tok], act_lo[:, k, tok], k == 0, k == KT - 1)
                t.then_inc(q_mm, 1)

            def wait_bank(g, r):
                pr = (r - 2) % 10
                gg = g if r >= 2 else g - 1
                if isinstance(gg, int) and gg < 0:
                    return
                n, hh = pr // 5, pr % 5
                if hh < 4:
                    pe.wait_ge(qlo_done, 8 * gg + 4 * n + hh + 1)
                else:
                    pe.wait_ge(klo_done, 2 * gg + n + 1)

            def ss_step(g, n, h):
                i = 8 * g + 4 * n + h
                pe.wait_ge(qsq_done, i + 1)
                if not (isinstance(g, int) and i == 0):
                    pe.wait_ge(qv_done, i)
                for j in range(HALF):
                    t = mm(bank[7][:, j:j + 1], qsq[:, j * L:(j + 1) * L], ones[:, :], start=True, stop=True)
                t.then_inc(ss_mm, 1)

            def kv_step(g, n, j):
                i = 8 * g + 4 * n + j
                pe.wait_ge(wkv_l, 2 * g + 2)
                if not (isinstance(g, int) and i == 0):
                    pe.wait_ge(kraw_done, i)
                tok = slice((4 * n + j) * L, (4 * n + j + 1) * L)
                for k in range(KT):
                    c0 = WKV_COL + k * 256
                    t = mm3(bank[2][:, 0:256], ctx_hi[:, k, tok], ctx_lo[:, k, tok],
                            w_hi[:, c0:c0 + 256], w_lo[:, c0:c0 + 256], k == 0, k == KT - 1)
                t.then_inc(kv_mm, 1)

            def kt_step(g, n):
                pe.wait_ge(kn_done, 2 * g + n + 1)
                wait_bank(g, 5 * n + 4)
                for j in range(HALF):
                    t = nc.tensor.transpose(bank[(5 * n + 4) % 2][:, j * P:(j + 1) * P], kraw[:, j, :], ident)
                t.then_inc(kt_mm, 1)

            def s_step(g, jj):
                n, j = jj // HALF, jj % HALF
                t_i = 8 * g + jj
                pe.wait_ge(qlo_done, 8 * g + 4 * n + 4)
                pe.wait_ge(klo_done, 2 * g + n + 1)
                if not (isinstance(g, int) and t_i == 0):
                    pe.wait_ge(s_done, t_i)
                tok = slice(j * L, (j + 1) * L)
                for h in range(GH):
                    t = mm3(bank[3][:, h * L:(h + 1) * L], q_hi[:, n, h, tok], q_lo[:, n, h, tok],
                            k_hi[:, n, tok], k_lo[:, n, tok], True, True)
                t.then_inc(s_mm, 1)

            def pt_step(g, jj):
                t_i = 8 * g + jj
                pe.wait_ge(p_norm, t_i + 1)
                if not (isinstance(g, int) and t_i == 0):
                    pe.wait_ge(ptlo_done, t_i)
                for h in range(GH):
                    t = nc.tensor.transpose(bank[4][:, h * L:(h + 1) * L], pb[:, jj % 2, h, :], ident)
                t.then_inc(pt_mm, 1)

            def pv_step(g, jj):
                t_i = 8 * g + jj
                pe.wait_ge(ptlo_done, t_i + 1)
                if not (isinstance(g, int) and t_i == 0):
                    pe.wait_ge(otlo_done, t_i)
                n, j = jj // HALF, jj % HALF
                mm3(bank[5][:, :], v_hi[:, n, j, :], v_lo[:, n, j, :], pt_hi[:, :], pt_lo[:, :], True, True)\
                    .then_inc(pv_mm, 1)

            def d_step(g, jj):
                t_i = 8 * g + jj
                pe.wait_ge(otlo_done, t_i + 1)
                if jj == 0:
                    pe.wait_ge(wo_l, 4 * g + 4)
                if not (isinstance(g, int) and t_i == 0):
                    pe.wait_ge(d_add, t_i)
                for h in range(GH):
                    hs = slice(h * L, (h + 1) * L)
                    c0 = WO_COL[h]
                    t = mm3(bank[6][:, :], ot_hi[:, hs], ot_lo[:, hs], w_hi[:, c0:c0 + 512],
                            w_lo[:, c0:c0 + 512], h == 0, h == GH - 1)
                t.then_inc(d_mm, 1)

            def slot(g, jj, produce, before=True):
                n, j = jj // HALF, jj % HALF
                pg, pn = (g, 1) if n == 0 else (g + 1, 0)
                if j < 3:
                    s_step(g, jj + 1)
                if produce:
                    q_step((pg, pn), j)
                    if j == 0:
                        kv_step(pg, pn, 0)
                        kv_step(pg, pn, 1)
                    elif j < 3:
                        kv_step(pg, pn, j + 1)
                    else:
                        kt_step(pg, pn)
                pt_step(g, jj)
                if before:
                    d_step(*((g, jj - 1) if jj else (g - 1, 7)))
                if produce:
                    ss_step(pg, pn, j)
                pv_step(g, jj)
                if j == 3 and produce:
                    s_step(pg, 4 * pn)

            pe.wait_ge(o_add, 8 + 8 * MLP_IT)
            for j in range(HALF):
                kv_step(0, 0, j)
            for i in range(16, 24):
                norm_t(i, tb)
            pe.wait_ge(n_lo, 24)
            for h in range(GH):
                q_step((0, 0), h)
                if h:
                    ss_step(0, 0, h - 1)
            kt_step(0, 0)
            ss_step(0, 0, 3)
            s_step(0, 0)
            slot(0, 0, True, before=False)
            with pe.Fori(0, GROUPS - 1) as g:
                for jj in range(1, 8):
                    slot(g, jj, True)
                slot(g + 1, 0, True)
            for jj in range(1, 8):
                slot(GROUPS - 1, jj, jj < 4)
            d_step(GROUPS - 1, 7)

            def lora_in(b):
                if b == 0:
                    pe.wait_ge(ld_lora[0], 16)
                pe.wait_ge(f_x2t, b + 1)
                for k in range(KT):
                    t = mm(bank[2 + b // 4][:, b % 4 * 68:(b % 4 + 1) * 68], x2t[:, b, k, :], ra_sb[:, k, :],
                           start=(k == 0), stop=(k == KT - 1))
                t.then_inc(ra_mm, 1)

            def f_norm_t(i):
                pe.wait_ge(n_x, i + 1)
                if i >= 26:
                    pe.wait_ge(f_x2t, i - 25)
                for k in range(KT):
                    t = nc.tensor.transpose(tb[i % 2][:, k * P:(k + 1) * P], res[:, i - 24, k * P:(k + 1) * P],
                                            ident)
                t.then_inc(n_t, 1)

            pe.wait_ge(s_done, 64)
            pe.wait_ge(otlo_done, 64)
            for b in range(B):
                f_norm_t(24 + b)
                if b:
                    lora_in(b - 1)
            lora_in(7)

            def mt_step(b):
                pe.wait_ge(mid_done, b // 4 + 1)
                if b >= 2:
                    pe.wait_ge(mt_ev, b - 1)
                nc.tensor.transpose(bank[4 + b % 2][0:NE * RANK, 0:P],
                                    mid[:, b, :, :].rearrange("p e r -> p (e r)"), ident).then_inc(mt_mm, 1)

            def dl_step(b):
                if b == 0:
                    pe.wait_ge(ld_lora[1], 16)
                    pe.wait_ge(d_add, 64)
                    pe.wait_ge(qv_done, 64)
                pe.wait_ge(mt_ev, b + 1)
                if b >= 2:
                    pe.wait_ge(dl_add, b - 1)
                mm(bank[6 + b % 2][:, :], midt[:, b % 2, :], bl_sb[:, :], start=True, stop=True)\
                    .then_inc(dl_mm, 1)

            mt_step(0)
            for b in range(B):
                if b + 1 < B:
                    mt_step(b + 1)
                dl_step(b)

        @block.scalar
        def _(act):
            A = nc.scalar.activation

            def square(i):
                if i < 8:
                    act.wait_ge(ld_x[i], 16)
                else:
                    act.wait_ge(o_add, i - 7)
                if i >= 2:
                    act.wait_ge(n_ssq, i - 1)
                A(junk[:, i % 2, :], res[:, i % 8, :], ACT.Square, accum_out=stat[:, i:i + 1]).then_inc(n_ssq, 1)

            def norm_hi(i, banks):
                act.wait_ge(n_t, i + 1)
                b = i % 8
                A(act_hi[:, :, b * L:(b + 1) * L], banks[i % 2][:, :].rearrange("p (k n) -> p k n", k=KT),
                  ACT.Copy).then_inc(n_hi, 1)

            def win_hi(p):
                act.wait_ge(ld_win[p % 8], 16 * (p // 8 + 1))
                A(w_hi[:, p * 512:(p + 1) * 512], mamba_raw(p), ACT.Copy).then_inc(win_h, 1)

            nb = (bank[2], bank[3])
            square(0)
            act.wait_ge(ld_small[3], 16)
            A(wdt_hi[:, :], wdt_raw[:, :], ACT.Copy).then_inc(dt_w, 1)
            win_hi(0)
            square(1)
            act.wait_ge(ld_small[1], 16)
            A(a2[:, :], row_sb[:, 2 * DM:2 * DM + NH], ACT.Exp).then_inc(setup_a, 1)
            norm_hi(0, nb)
            square(2)
            norm_hi(1, nb)
            win_hi(1)
            square(3)
            norm_hi(2, nb)
            win_hi(2)
            norm_hi(3, nb)
            win_hi(3)
            win_hi(4)

            order = [(0, p) for p in range(NPIECE)] + [(1, p) for p in (6, 7, 8, 9, 0, 1, 2, 3, 4, 5)]

            def in_evac(f):
                n, p = order[f]
                act.wait_ge(in_mm, f + 1)
                if p < NCONV:
                    q = NCONV * n + p
                    if q == 0:
                        act.wait_ge(setup_v, 1)
                    if q >= 2:
                        act.wait_ge(conv_c, q - 1)
                    A(pre[:, q % 2, :, DCONV - 1:], bank[f % 2][:, :].rearrange("p (s n) -> p s n", s=HALF),
                      ACT.Copy).then_inc(conv_ev, 1)
                else:
                    i = NH * n + p - NCONV
                    if i >= 1:
                        act.wait_ge(z_out, i)
                    A(th[:, 0, :], bank[f % 2][:, :], ACT.Tanh, scale=0.5).then_inc(z_th, 1)

            def conv_tanh(q):
                act.wait_ge(conv_c, q + 1)
                if q >= 1:
                    act.wait_ge(conv_out, q)
                A(th[:, 1, :], cbuf[:, q % 2, :], ACT.Tanh).then_inc(conv_th, 1)

            def dt_exp(n):
                act.wait_ge(dt_a, n + 1)
                A(sp[:, 2, :], sp[:, 1, :], ACT.Exp).then_inc(dt_done, 1)

            def x_evac(b):
                act.wait_ge(xt_mm, b + 1)
                if b >= 2:
                    act.wait_ge(y_mm, b - 1)
                A(xtok[:, b % 2, :], bank[5][:, 0:P], ACT.Copy).then_inc(xt_ev, 1)

            def decay(b):
                act.wait_ge(cum_mm, b + 1)
                if b == 0:
                    act.wait_ge(setup_v, 3)
                if b >= 2:
                    act.wait_ge(att_done, b - 1)
                for h in range(NH):
                    t = A(em[:, b % 2, h, :], bank[2][:, h * L:(h + 1) * L], ACT.Exp, scale=a2[:, h:h + 1])
                t.then_inc(exp_done, 1)

            def y_split(b):
                act.wait_ge(yz_done, b + 1)
                if b >= 4:
                    act.wait_ge(o_mm, b - 3)
                A(y_hi[:, b % 4, :, :], yb[:, b % 2, :, :], ACT.Copy).then_inc(yhi_done, 1)

            in_evac(0)
            win_hi(5)
            in_evac(1)
            conv_tanh(0)
            dt_exp(0)
            square(4)
            win_hi(6)
            in_evac(2)
            conv_tanh(1)
            square(5)
            win_hi(7)
            in_evac(3)
            conv_tanh(2)
            square(6)
            win_hi(8)
            in_evac(4)
            conv_tanh(3)
            square(7)
            win_hi(9)
            in_evac(5)
            conv_tanh(4)
            for i in range(4, 8):
                norm_hi(i, nb)
            in_evac(6)
            conv_tanh(5)
            for f in range(7, 10):
                in_evac(f)
            in_evac(10)
            dt_exp(1)
            in_evac(11)
            x_evac(0)
            decay(0)
            in_evac(12)
            x_evac(1)
            decay(1)
            in_evac(13)
            y_split(0)
            x_evac(2)
            decay(2)
            in_evac(14)
            y_split(1)
            x_evac(3)
            decay(3)
            in_evac(15)
            y_split(2)

            def wout_hi(k):
                if k == 0:
                    act.wait_ge(ld_wout, 16)
                    act.wait_ge(in_mm, 14)
                A(w_hi[:, OUT_COL + k * 512:OUT_COL + (k + 1) * 512], raw_b[:, k * 512:(k + 1) * 512],
                  ACT.Copy).then_inc(wout_h, 1)

            in_evac(16)
            wout_hi(0)
            wout_hi(1)
            y_split(3)
            conv_tanh(6)
            in_evac(17)
            wout_hi(2)
            wout_hi(3)
            conv_tanh(7)
            in_evac(18)
            conv_tanh(8)
            in_evac(19)
            conv_tanh(9)
            conv_tanh(10)
            conv_tanh(11)
            tb = (bank[0], bank[1])

            def gu_hi(c, i):
                act.wait_ge(ld_gu, 16 * c + 16)
                if isinstance(c, int) and c == 0:
                    act.wait_ge(in_mm, 20)
                else:
                    act.wait_ge(gu_mm, 4 * c)
                A(w_hi[:, GU_COL + i * 512:GU_COL + (i + 1) * 512], raw_a[:, i * 512:(i + 1) * 512],
                  ACT.Copy).then_inc(gu_h, 1)

            def dn_hi(c, i):
                act.wait_ge(ld_dn, 16 * c + 16)
                if isinstance(c, int) and c == 0:
                    act.wait_ge(in_mm, 20)
                else:
                    act.wait_ge(o_mm, 8 + 8 * c)
                A(w_hi[:, DN_COL + i * 512:DN_COL + (i + 1) * 512], raw_b[:, i * 512:(i + 1) * 512],
                  ACT.Copy).then_inc(dn_h, 1)

            gu_split = 0
            for b in range(4, 8):
                x_evac(b)
                decay(b)
                gu_hi(0, gu_split)
                gu_split += 1
                square(4 + b)
                y_split(b)
            for b in range(4):
                norm_hi(8 + b, tb)
                square(12 + b)
            for i in range(12, 16):
                norm_hi(i, tb)

            def silu(c, m_i):
                act.wait_ge(gu_mm, 4 * c + m_i + 1)
                if not (isinstance(c, int) and 4 * c + m_i < 2):
                    act.wait_ge(h_done, 4 * c + m_i - 1)
                A(sg[:, m_i % 2, :], bank[(2, 4)[m_i % 2]][:, :], ACT.Silu).then_inc(silu_done, 1)

            def h_split(c, m_i):
                act.wait_ge(h_done, 4 * c + m_i + 1)
                if not (isinstance(c, int) and c == 0):
                    act.wait_ge(o_mm, 8 + 8 * c - 4 + 4 * (m_i // 2))
                k, n = m_i % 2, m_i // 2
                A(h_hi[:, k, n * NTOK:(n + 1) * NTOK], hb[:, m_i % 2, :], ACT.Copy).then_inc(hhi_done, 1)

            def ctx_split(i):
                act.wait_ge(ld_ctx[i % 2], 16 * (i // 2 + 1))
                if i == 0:
                    act.wait_ge(o_mm, 8)
                A(ctx_hi[:, i // 2, i % 2 * 512:(i % 2 + 1) * 512],
                  raw_b[:, 1024 + i % 2 * 512:1536 + i % 2 * 512], ACT.Copy).then_inc(cx_h, 1)

            def mlp_step(c):
                first = isinstance(c, int) and c == 0
                for m_i in range(4):
                    silu(c, m_i)
                    h_split(c, m_i)
                    if m_i == 0:
                        dn_hi(c, 0)
                        dn_hi(c, 1)
                    if first:
                        ctx_split(2 * m_i)
                        ctx_split(2 * m_i + 1)
                if not (isinstance(c, int) and c == MLP_IT - 1):
                    for i in range(4):
                        gu_hi(c + 1, i)

            mlp_step(0)
            with act.Fori(1, MLP_IT - 1) as c:
                mlp_step(c)
            mlp_step(MLP_IT - 1)

            def wkv_hi(g, i):
                act.wait_ge(ld_kv, 16 * g + 16)
                if isinstance(g, int) and g == 0:
                    act.wait_ge(o_mm, 8)
                else:
                    act.wait_ge(kv_mm, 8 * g)
                A(w_hi[:, WKV_COL + i * 512:WKV_COL + (i + 1) * 512], raw_b[:, i * 512:(i + 1) * 512],
                  ACT.Copy).then_inc(wkv_h, 1)

            def wq_hi(g, h):
                act.wait_ge(ld_q, 16 * g + 16)
                if isinstance(g, int) and g == 0:
                    act.wait_ge(gu_mm, 4 * MLP_IT)
                else:
                    act.wait_ge(q_mm, 8 * g - 4 + h + 1)
                A(w_hi[:, WQ_COL + h * 512:WQ_COL + (h + 1) * 512], raw_a[:, h * 512:(h + 1) * 512],
                  ACT.Copy).then_inc(wq_h, 1)

            def wo_hi(g, h):
                act.wait_ge(ld_o, 16 * g + 16)
                if isinstance(g, int) and g == 0:
                    act.wait_ge(o_mm, 8 + 8 * MLP_IT)
                else:
                    act.wait_ge(d_mm, 8 * g)
                A(w_hi[:, WO_COL[h]:WO_COL[h] + 512], raw_b[:, h * 512:(h + 1) * 512], ACT.Copy)\
                    .then_inc(wo_h, 1)

            def q_evac(g, n, h):
                i = 8 * g + 4 * n + h
                act.wait_ge(q_mm, i + 1)
                if not (isinstance(g, int) and 8 * g + 4 * n < 8):
                    act.wait_ge(s_mm, 8 * g + 4 * n - 4)
                A(q_hi[:, n, h, :], bank[(5 * n + h) % 2][:, :], ACT.Copy).then_inc(qhi_done, 1)
                if not (isinstance(g, int) and i == 0):
                    act.wait_ge(ss_mm, i)
                A(qsq[:, :], bank[(5 * n + h) % 2][:, :], ACT.Square).then_inc(qsq_done, 1)

            def kv_evac(g, n, j):
                i = 8 * g + 4 * n + j
                act.wait_ge(kv_mm, i + 1)
                if not (isinstance(g, int) and i == 0):
                    act.wait_ge(ksq_done, i)
                if j == 0 and not (isinstance(g, int) and 2 * g + n == 0):
                    act.wait_ge(kvar_done, 2 * g + n)
                A(junk[:, 0, 0:HD], bank[2][:, 0:HD], ACT.Square, accum_out=kv[:, 0, j:j + 1])\
                    .then_inc(ksq_done, 1)
                if not (isinstance(g, int) and 8 * g + 4 * n < 8):
                    act.wait_ge(pv_mm, 8 * g + 4 * n - 4)
                A(v_hi[:, n, j, :], bank[2][:, HD:2 * HD], ACT.Copy).then_inc(vhi_done, 1)

            def kt_evac(g, n):
                u = 2 * g + n
                act.wait_ge(kt_mm, u + 1)
                if isinstance(g, int) and u == 0:
                    act.wait_ge(setup_p, 1)
                if not (isinstance(g, int) and u < 2):
                    act.wait_ge(s_mm, 8 * g + 4 * n - 4)
                A(k_hi[:, n, :], bank[(5 * n + 4) % 2][:, :], ACT.Copy, scale=qk_w[:, 0:1]).then_inc(khi_done, 1)

            def softmax_exp(g, jj):
                t_i = 8 * g + jj
                act.wait_ge(max_done, t_i + 1)
                for h in range(GH):
                    t = A(pb[:, jj % 2, h, :], pb[:, jj % 2, h, :], ACT.Exp, bias=nmax[:, jj % 2, h:h + 1],
                          accum_out=psum_[:, jj % 2, h:h + 1])
                t.then_inc(p_exp, 1)

            def pt_evac(g, jj):
                act.wait_ge(pt_mm, 8 * g + jj + 1)
                if not (isinstance(g, int) and 8 * g + jj == 0):
                    act.wait_ge(pv_mm, 8 * g + jj)
                A(pt_hi[:, :], bank[4][:, :], ACT.Copy).then_inc(pthi_done, 1)

            def ot_evac(g, jj):
                act.wait_ge(pv_mm, 8 * g + jj + 1)
                if not (isinstance(g, int) and 8 * g + jj == 0):
                    act.wait_ge(d_mm, 8 * g + jj)
                A(ot_hi[:, :], bank[5][:, :], ACT.Copy).then_inc(othi_done, 1)

            def slot(g, jj, produce, refill=True):
                n, j = jj // HALF, jj % HALF
                pg, pn = (g, 1) if n == 0 else (g + 1, 0)
                if j < 3:
                    softmax_exp(g, jj + 1)
                if produce:
                    q_evac(pg, pn, j)
                    if j == 0:
                        kv_evac(pg, pn, 0)
                        kv_evac(pg, pn, 1)
                    elif j < 3:
                        kv_evac(pg, pn, j + 1)
                    else:
                        kt_evac(pg, pn)
                if refill and 1 <= jj <= 4:
                    wq_hi(g + 1, jj - 1)
                pt_evac(g, jj)
                if jj == 0 and not (isinstance(g, int) and g == 0):
                    for h in range(GH):
                        wo_hi(g, h)
                if refill and jj == 3:
                    wkv_hi(g + 1, 0)
                    wkv_hi(g + 1, 1)
                ot_evac(g, jj)
                if j == 3 and produce:
                    softmax_exp(pg, 4 * pn)

            wkv_hi(0, 0)
            wkv_hi(0, 1)
            for h in range(GH):
                wq_hi(0, h)
            for j in range(HALF):
                kv_evac(0, 0, j)
            for i in range(16, 24):
                norm_hi(i, tb)
            for h in range(GH):
                wo_hi(0, h)
                q_evac(0, 0, h)
            kt_evac(0, 0)
            softmax_exp(0, 0)
            slot(0, 0, True)
            with act.Fori(0, GROUPS - 1) as g:
                for jj in range(1, 8):
                    slot(g, jj, True)
                slot(g + 1, 0, True, refill=False)
            for jj in range(1, 8):
                slot(GROUPS - 1, jj, jj < 4, refill=False)

            def x2_evac(b):
                act.wait_ge(n_t, 25 + b)
                if b == 0:
                    act.wait_ge(otlo_done, 64)
                    act.wait_ge(d_mm, 64)
                A(x2t[:, b, :, :], tb[b % 2][:, :].rearrange("p (k n) -> p k n", k=KT), ACT.Copy)\
                    .then_inc(f_x2t, 1)

            def gate_exp(i):
                act.wait_ge(lg_done, i + 1)
                A(ge[:, 4 * i:4 * i + 4, :], ge[:, 4 * i:4 * i + 4, :], ACT.Exp).then_inc(f_exp, 1)

            def mt_evac(b):
                act.wait_ge(mt_mm, b + 1)
                if b >= 2:
                    act.wait_ge(dl_mm, b - 1)
                A(midt[:, b % 2, :], bank[4 + b % 2][0:NE * RANK, 0:P], ACT.Copy).then_inc(mt_ev, 1)

            for b in range(B):
                x2_evac(b)
                if b == 6:
                    gate_exp(0)
            gate_exp(1)
            for b in range(B):
                mt_evac(b)

        @block.gpsimd
        def _(pool):
            TT = nc.gpsimd.tensor_tensor

            def lo(dst, src, hi, done):
                TT(dst, src, f32(hi), ALU.subtract).then_inc(done, 1)

            def rsqrt(i):
                pool.wait_ge(n_var, i + 1)
                TT(rstd[:, i:i + 1], var[:, i:i + 1], pow_m[:, 0:1], ALU.pow).then_inc(n_rstd, 1)

            pool.wait_ge(setup_v, 2)
            for i in range(4):
                rsqrt(i)

            def decay_in(b):
                pool.wait_ge(dt_done, 2 * (b // HALF) + 2)
                if b == 0:
                    pool.wait_ge(ld_small[0], 16)
                if b >= 2:
                    pool.wait_ge(em_done, b - 1)
                    pool.wait_ge(cum_mm, b - 1)
                TT(md[:, b % 2, :, :], dt_sb[:, b * NH:(b + 1) * NH].unsqueeze(2).to_broadcast([P, NH, L]),
                   tri_half.unsqueeze(1).to_broadcast([P, NH, L]), ALU.mult).then_inc(md_done, 1)

            def decay_out(b):
                pool.wait_ge(exp_done, b + 1)
                TT(em[:, b % 2, :, :], em[:, b % 2, :, :], md[:, b % 2, :, :], ALU.mult).then_inc(em_done, 1)

            def y_rest(b):
                pool.wait_ge(yhi_done, b + 1)
                lo(y_lo[:, b % 4, :, :], yb[:, b % 2, :, :], y_hi[:, b % 4, :, :], ylo_done)

            for i in range(4, 8):
                rsqrt(i)
            decay_in(0)
            decay_in(1)
            for b in range(4):
                decay_out(b)
                if b < 2:
                    decay_in(b + 2)
                if b:
                    y_rest(b - 1)
            for k in range(4):
                pool.wait_ge(wout_h, k + 1)
                lo(w_lo[:, OUT_COL + k * 512:OUT_COL + (k + 1) * 512], raw_b[:, k * 512:(k + 1) * 512],
                   w_hi[:, OUT_COL + k * 512:OUT_COL + (k + 1) * 512], wout_l)
                if k == 0:
                    y_rest(3)
            decay_in(4)
            decay_in(5)

            def gu_rest(c, i):
                pool.wait_ge(gu_h, 4 * c + i + 1)
                s = slice(GU_COL + i * 512, GU_COL + (i + 1) * 512)
                lo(w_lo[:, s], raw_a[:, i * 512:(i + 1) * 512], w_hi[:, s], gu_l)

            def dn_rest(c, i):
                pool.wait_ge(dn_h, 2 * c + i + 1)
                s = slice(DN_COL + i * 512, DN_COL + (i + 1) * 512)
                lo(w_lo[:, s], raw_b[:, i * 512:(i + 1) * 512], w_hi[:, s], dn_l)

            for b in range(4, 8):
                decay_out(b)
                if b < 6:
                    decay_in(b + 2)
                gu_rest(0, b - 4)
                y_rest(b)
                rsqrt(8 + b - 4)
            for i in range(12, 16):
                rsqrt(i)

            def mlp_step(c):
                first = isinstance(c, int) and c == 0
                for m_i in range(4):
                    k, n = m_i % 2, m_i // 2
                    pool.wait_ge(hhi_done, 4 * c + m_i + 1)
                    tok = slice(n * NTOK, (n + 1) * NTOK)
                    lo(h_lo[:, k, tok], hb[:, m_i % 2, :], h_hi[:, k, tok], hlo_done)
                    if m_i == 0:
                        dn_rest(c, 0)
                        dn_rest(c, 1)
                    if first:
                        for i in (2 * m_i, 2 * m_i + 1):
                            pool.wait_ge(cx_h, i + 1)
                            cs = slice(i % 2 * 512, (i % 2 + 1) * 512)
                            lo(ctx_lo[:, i // 2, cs], raw_b[:, 1024 + i % 2 * 512:1536 + i % 2 * 512],
                               ctx_hi[:, i // 2, cs], cx_l)
                if not (isinstance(c, int) and c == MLP_IT - 1):
                    for i in range(4):
                        gu_rest(c + 1, i)

            mlp_step(0)
            with pool.Fori(1, MLP_IT - 1) as c:
                mlp_step(c)
            mlp_step(MLP_IT - 1)

            def wkv_rest(g, i):
                pool.wait_ge(wkv_h, 2 * g + i + 1)
                s = slice(WKV_COL + i * 512, WKV_COL + (i + 1) * 512)
                lo(w_lo[:, s], raw_b[:, i * 512:(i + 1) * 512], w_hi[:, s], wkv_l)

            def wq_rest(g, h):
                pool.wait_ge(wq_h, 4 * g + h + 1)
                s = slice(WQ_COL + h * 512, WQ_COL + (h + 1) * 512)
                lo(w_lo[:, s], raw_a[:, h * 512:(h + 1) * 512], w_hi[:, s], wq_l)

            def wo_rest(g, h):
                pool.wait_ge(wo_h, 4 * g + h + 1)
                s = slice(WO_COL[h], WO_COL[h] + 512)
                lo(w_lo[:, s], raw_b[:, h * 512:(h + 1) * 512], w_hi[:, s], wo_l)

            def q_rsqrt(g, n, h):
                i = 8 * g + 4 * n + h
                pool.wait_ge(qv_done, i + 1)
                if not (isinstance(g, int) and 8 * g + 4 * n < 8):
                    pool.wait_ge(s_done, 8 * g + 4 * n - 4)
                TT(qr[:, 4 * n + h, :], qv[:, 4 * n + h, :], pow_m[:, 0:HALF], ALU.pow).then_inc(qr_done, 1)

            def k_rsqrt(g, n):
                pool.wait_ge(kvar_done, 2 * g + n + 1)
                if not (isinstance(g, int) and 2 * g + n == 0):
                    pool.wait_ge(kn_done, 2 * g + n)
                TT(kv[:, 2, :], kv[:, 1, :], pow_m[:, 0:HALF], ALU.pow).then_inc(kr_done, 1)

            def p_scale(g, jj):
                pool.wait_ge(p_rec, 8 * g + jj + 1)
                TT(pb[:, jj % 2, :, :], pb[:, jj % 2, :, :],
                   prec[:, jj % 2, :].unsqueeze(2).to_broadcast([P, GH, L]), ALU.mult).then_inc(p_norm, 1)

            def slot(g, jj, produce, refill=True):
                n, j = jj // HALF, jj % HALF
                pg, pn = (g, 1) if n == 0 else (g + 1, 0)
                if j == 0:
                    p_scale(g, jj)
                if j < 3:
                    p_scale(g, jj + 1)
                if produce and j == 2:
                    k_rsqrt(pg, pn)
                if refill and 1 <= jj <= 4:
                    wq_rest(g + 1, jj - 1)
                if jj == 0 and not (isinstance(g, int) and g == 0):
                    for h in range(GH):
                        wo_rest(g, h)
                if refill and jj == 3:
                    wkv_rest(g + 1, 0)
                    wkv_rest(g + 1, 1)
                if produce:
                    q_rsqrt(pg, pn, j)

            pool.wait_ge(setup_v, 2)
            pool.wait_ge(ld_small[2], 16)
            nq = NCONV * DCONV + NCONV
            TT(qk_w[:, :], chan_sb[:, nq:nq + 1], chan_sb[:, nq + 1:nq + 2], ALU.mult).then_inc(setup_p, 1)
            wkv_rest(0, 0)
            wkv_rest(0, 1)
            for h in range(GH):
                wq_rest(0, h)
            k_rsqrt(0, 0)
            for i in range(16, 24):
                rsqrt(i)
            for h in range(GH):
                wo_rest(0, h)
                q_rsqrt(0, 0, h)
            slot(0, 0, True)
            with pool.Fori(0, GROUPS - 1) as g:
                for jj in range(1, 8):
                    slot(g, jj, True)
                slot(g + 1, 0, True, refill=False)
            for jj in range(1, 8):
                slot(GROUPS - 1, jj, jj < 4, refill=False)
            for i in range(24, 40):
                rsqrt(i)

        @block.vector
        def _(dve):
            V = nc.vector
            TT, STT, TS = V.tensor_tensor, V.scalar_tensor_tensor, V.tensor_scalar
            count = [0]

            def link(ins):
                count[0] += 1
                ins.then_inc(vch, 1)
                dve.wait_ge(vch, count[0])

            def lo(dst, src, hi, done):
                TT(dst, src, f32(hi), ALU.subtract).then_inc(done, 1)

            def rms_var(i):
                dve.wait_ge(n_ssq, i + 1)
                TS(var[:, i:i + 1], stat[:, i:i + 1], 1.0 / DM, EPS, ALU.mult, ALU.add).then_inc(n_var, 1)

            def rms_x(i):
                dve.wait_ge(n_rstd, i + 1)
                if i == 0:
                    dve.wait_ge(ld_small[1], 16)
                if i >= 2:
                    dve.wait_ge(n_t, i - 1)
                STT(xn[:, i % 2, :], res[:, i % 8, :], rstd[:, i:i + 1],
                    row_sb[:, i // 8 * DM:(i // 8 + 1) * DM], ALU.mult, ALU.mult).then_inc(n_x, 1)

            def norm_lo(i, banks):
                dve.wait_ge(n_hi, i + 1)
                b = i % 8
                lo(act_lo[:, :, b * L:(b + 1) * L], banks[i % 2][:, :].rearrange("p (k n) -> p k n", k=KT),
                   act_hi[:, :, b * L:(b + 1) * L], n_lo)

            def win_lo(p):
                dve.wait_ge(win_h, p + 1)
                lo(w_lo[:, p * 512:(p + 1) * 512], mamba_raw(p), w_hi[:, p * 512:(p + 1) * 512], win_l)

            nb = (bank[2], bank[3])
            V.memset(ones[:, :], 1.0)
            V.memset(pre[:, :, :, :], 0.0).then_inc(setup_v, 1)
            V.memset(pow_m[:, :], -0.5).then_inc(setup_v, 1)
            rms_var(0)
            dve.wait_ge(dt_w, 1)
            TT(wdt_lo[:, :], wdt_raw[:, :], f32(wdt_hi[:, :]), ALU.subtract).then_inc(dt_w, 1)
            rms_x(0)
            win_lo(0)
            rms_var(1)
            rms_x(1)
            norm_lo(0, nb)
            rms_var(2)
            rms_x(2)
            norm_lo(1, nb)
            win_lo(1)
            rms_var(3)
            rms_x(3)
            norm_lo(2, nb)
            win_lo(2)
            norm_lo(3, nb)
            dve.wait_ge(setup_a, 1)
            dve.wait_ge(ld_small[2], 16)
            link(TS(a2[:, :], a2[:, :], -2.0, None, ALU.mult))
            TS(cw[:, :], chan_sb[:, 0:NCONV * DCONV + NCONV], 0.5, None, ALU.mult)
            link(TS(d2[:, :], row_sb[:, 2 * DM + NH:2 * DM + 2 * NH], 0.5, None, ALU.mult))
            V.tensor_copy(sp[:, 6, 0:NH], row_sb[:, 2 * DM + 2 * NH:2 * DM + 3 * NH]).then_inc(setup_v, 1)
            win_lo(3)
            win_lo(4)

            def conv(q):
                p = q % NCONV
                dve.wait_ge(conv_ev, q + 1)
                if q >= 2:
                    dve.wait_ge(conv_out, q - 1)
                c = cbuf[:, q % 2, :].rearrange("p (s n) -> p s n", s=HALF)

                def tap(k):
                    return pre[:, q % 2, :, k:k + L], cw[:, p * DCONV + k:p * DCONV + k + 1]
                v, w = tap(3)
                link(TS(c, v, w, cw[:, NCONV * DCONV + p:NCONV * DCONV + p + 1], ALU.mult, ALU.add))
                for k in (2, 1):
                    v, w = tap(k)
                    link(STT(c, v, w, c, ALU.mult, ALU.add))
                v, w = tap(0)
                STT(c, v, w, c, ALU.mult, ALU.add).then_inc(conv_c, 1)

            def conv_silu(q):
                dve.wait_ge(conv_th, q + 1)
                STT(xbc[:, q % NCONV, :], th[:, 1, :], 1.0, cbuf[:, q % 2, :], ALU.add, ALU.mult)\
                    .then_inc(conv_out, 1)

            def z_silu(i):
                n, h = i // NH, i % NH
                f = 6 + h if n == 0 else 10 + h
                dve.wait_ge(z_th, i + 1)
                STT(zt[:, h, n * NTOK:(n + 1) * NTOK], th[:, 0, :], 1.0, bank[f % 2][:, :], ALU.add, ALU.mult)\
                    .then_inc(z_out, 1)

            def dt_in(n):
                dve.wait_ge(dt_mm, n + 1)
                bias = sp[:, 6, 0:NH].unsqueeze(1).to_broadcast([P, HALF, NH])
                link(TT(sp[:, 0, :].rearrange("p (b h) -> p b h", h=NH),
                        bank[7][:, 0:HALF * NH].rearrange("p (b h) -> p b h", h=NH), bias, ALU.add))
                link(TS(sp[:, 1, :], sp[:, 0, :], 0.0, None, ALU.min))
                link(TS(sp[:, 0, :], sp[:, 0, :], 0.0, None, ALU.max))
                link(TT(sp[:, 3, :], sp[:, 1, :], sp[:, 0, :], ALU.subtract))
                V.tensor_copy(sp[:, 1, :], sp[:, 3, :]).then_inc(dt_a, 1)

            def dt_out(n):
                dve.wait_ge(dt_done, 2 * n + 1)
                link(TS(sp[:, 3, :], sp[:, 2, :], 2.0, None, ALU.add))
                link(V.reciprocal(sp[:, 4, :], sp[:, 3, :]))
                link(TT(sp[:, 3, :], sp[:, 2, :], sp[:, 4, :], ALU.mult))
                link(TT(sp[:, 4, :], sp[:, 3, :], sp[:, 3, :], ALU.mult))
                link(TS(sp[:, 5, :], sp[:, 4, :], 2.0 / (2 * ATANH_TERMS + 1), None, ALU.mult))
                for k in range(ATANH_TERMS - 1, 0, -1):
                    link(STT(sp[:, 5, :], sp[:, 5, :], 2.0 / (2 * k + 1), sp[:, 4, :], ALU.add, ALU.mult))
                link(STT(sp[:, 5, :], sp[:, 5, :], 2.0, sp[:, 3, :], ALU.add, ALU.mult))
                TT(dt_sb[:, n * HALF * NH:(n + 1) * HALF * NH], sp[:, 5, :], sp[:, 0, :], ALU.add)\
                    .then_inc(dt_done, 1)

            def att_mul(b):
                dve.wait_ge(em_done, b + 1)
                dve.wait_ge(sc_mm, b + 1)
                if b:
                    dve.wait_ge(y_mm, b)
                TT(att[:, :, :], em[:, b % 2, :, :], bank[3][:, :].rearrange("p (h n) -> p h n", h=NH), ALU.mult)\
                    .then_inc(att_done, 1)

            def y_out(b):
                dve.wait_ge(y_mm, b + 1)
                if b >= 2:
                    dve.wait_ge(ylo_done, b - 1)
                tok = slice(b % HALF * L, (b % HALF + 1) * L)
                for h in range(NH):
                    t = STT(yb[:, b % 2, h, :], xbc[:, 0, tok], d2[:, h:h + 1], bank[4][:, h * L:(h + 1) * L],
                            ALU.mult, ALU.add)
                t.then_inc(y1_done, 1)
                dve.wait_ge(y1_done, b + 1)
                dve.wait_ge(z_out, NH * (b // HALF) + NH)
                TT(yb[:, b % 2, :, :], yb[:, b % 2, :, :], zt[:, :, b * L:(b + 1) * L], ALU.mult)\
                    .then_inc(yz_done, 1)

            def add_res(i, b):
                dve.wait_ge(o_mm, i + 1)
                TT(res[:, b, :], res[:, b, :], bank[6 + b % 2][:, :], ALU.add).then_inc(o_add, 1)

            conv(0)
            dt_in(0)
            conv_silu(0)
            conv(1)
            dt_out(0)
            rms_var(4)
            rms_x(4)
            conv_silu(1)
            win_lo(5)
            conv(2)
            rms_var(5)
            rms_x(5)
            conv_silu(2)
            win_lo(6)
            conv(3)
            conv_silu(3)
            win_lo(7)
            rms_var(6)
            conv(4)
            conv_silu(4)
            win_lo(8)
            rms_var(7)
            win_lo(9)
            norm_lo(4, nb)
            rms_x(6)
            norm_lo(5, nb)
            rms_x(7)
            norm_lo(6, nb)
            conv(5)
            norm_lo(7, nb)
            conv_silu(5)
            for i in range(4):
                z_silu(i)
            dt_in(1)
            z_silu(4)
            dt_out(1)
            z_silu(5)
            att_mul(0)
            z_silu(6)
            y_out(0)
            att_mul(1)
            z_silu(7)
            y_out(1)
            att_mul(2)
            y_out(2)
            att_mul(3)
            y_out(3)
            for q in range(6, 12):
                conv(q)
                dve.wait_ge(sc_mm, 4)
                dve.wait_ge(xt_mm, 4)
                conv_silu(q)
            tb = (bank[0], bank[1])
            add_res(0, 0)
            rms_var(8)
            att_mul(4)
            add_res(1, 1)
            y_out(4)
            rms_var(9)
            att_mul(5)
            add_res(2, 2)
            y_out(5)
            rms_var(10)
            att_mul(6)
            add_res(3, 3)
            y_out(6)
            rms_var(11)
            att_mul(7)
            add_res(4, 4)
            y_out(7)
            rms_x(8)
            add_res(5, 5)
            rms_x(9)
            rms_var(12)
            norm_lo(8, tb)
            rms_x(10)
            norm_lo(9, tb)
            rms_x(11)
            rms_var(13)
            add_res(6, 6)
            norm_lo(10, tb)
            rms_x(12)
            norm_lo(11, tb)
            rms_var(14)
            add_res(7, 7)
            rms_x(13)
            norm_lo(12, tb)
            rms_var(15)
            rms_x(14)
            norm_lo(13, tb)
            rms_x(15)
            norm_lo(14, tb)
            norm_lo(15, tb)

            def mlp_step(c):
                for m_i in range(4):
                    dve.wait_ge(silu_done, 4 * c + m_i + 1)
                    dve.wait_ge(gu_mm, 4 * c + m_i + 1)
                    if not (isinstance(c, int) and 4 * c + m_i < 2):
                        dve.wait_ge(hlo_done, 4 * c + m_i - 1)
                    TT(hb[:, m_i % 2, :], sg[:, m_i % 2, :], bank[(3, 5)[m_i % 2]][:, :], ALU.mult)\
                        .then_inc(h_done, 1)
                for b in range(B):
                    add_res(8 + 8 * c + b, b)

            mlp_step(0)
            with dve.Fori(1, MLP_IT - 1) as c:
                mlp_step(c)
            mlp_step(MLP_IT - 1)

            def ln_stats(i):
                b = i % 8
                if i >= 18:
                    dve.wait_ge(n_mv, i - 17)
                V.bn_stats(bst[:, i % 2, :], res[:, b, :]).then_inc(n_bn, 1)
                dve.wait_ge(n_bn, i - 15)
                V.bn_aggr(mv[:, i, :], bst[:, i % 2, :]).then_inc(n_mv, 1)
                dve.wait_ge(n_mv, i - 15)
                TS(var[:, i:i + 1], mv[:, i, 1:2], EPS, None, ALU.add).then_inc(n_var, 1)

            def add_x(b):
                dve.wait_ge(ld_xre[b % 2], 16 * (b // 2 + 1))
                dve.wait_ge(o_add, 8 + 8 * MLP_IT)
                TT(res[:, b, :], res[:, b, :], xre[:, b % 2, :], ALU.add).then_inc(x_add, 1)
                dve.wait_ge(x_add, b + 1)

            def ln_x(i):
                b = i % 8
                dve.wait_ge(n_rstd, i + 1)
                dve.wait_ge(n_t, i - 1)
                TS(xn[:, i % 2, :], res[:, b, :], mv[:, i, 0:1], rstd[:, i:i + 1], ALU.subtract, ALU.mult)\
                    .then_inc(n_x, 1)
                dve.wait_ge(n_x, i + 1)
                V.tensor_copy(res[:, b, :], xn[:, i % 2, :]).then_inc(res_x, 1)

            def v_rest(g, n, j):
                i = 8 * g + 4 * n + j
                dve.wait_ge(vhi_done, i + 1)
                lo(v_lo[:, n, j, :], bank[2][:, HD:2 * HD], v_hi[:, n, j, :], vlo_done)
                if j == 0 and not (isinstance(g, int) and 2 * g + n == 0):
                    dve.wait_ge(kt_mm, 2 * g + n)
                V.tensor_copy(kraw[:, j, :], bank[2][:, 0:HD]).then_inc(kraw_done, 1)

            def k_norm(g, n):
                u = 2 * g + n
                dve.wait_ge(ksq_done, 4 * u + 4) if isinstance(u, int) else dve.wait_ge(ksq_done, 8 * g + 4 * n + 4)
                if not (isinstance(g, int) and u == 0):
                    dve.wait_ge(kr_done, 2 * g + n)
                TS(kv[:, 1, :], kv[:, 0, :], 1.0 / HD, EPS, ALU.mult, ALU.add).then_inc(kvar_done, 1)
                dve.wait_ge(kr_done, 2 * g + n + 1)
                dve.wait_ge(kraw_done, 8 * g + 4 * n + 4)
                TT(kraw[:, :, :], kraw[:, :, :], kv[:, 2, :].unsqueeze(2).to_broadcast([P, HALF, HD]), ALU.mult)\
                    .then_inc(kn_done, 1)

            def k_rest(g, n):
                u = 2 * g + n
                dve.wait_ge(khi_done, 2 * g + n + 1)
                STT(k_lo[:, n, :], bank[(5 * n + 4) % 2][:, :], qk_w[:, 0:1], f32(k_hi[:, n, :]), ALU.mult,
                    ALU.subtract).then_inc(klo_done, 1)

            def q_rest(g, n, h):
                i = 8 * g + 4 * n + h
                dve.wait_ge(qsq_done, i + 1)
                lo(q_lo[:, n, h, :], bank[(5 * n + h) % 2][:, :], q_hi[:, n, h, :], qlo_done)

            def q_var(g, n, h):
                i = 8 * g + 4 * n + h
                dve.wait_ge(ss_mm, i + 1)
                if not (isinstance(g, int) and 8 * g + 4 * n < 8):
                    dve.wait_ge(qr_done, 8 * g + 4 * n - 4)
                TS(qv[:, 4 * n + h, :], bank[7][:, 0:HALF], HD * EPS, None, ALU.add).then_inc(qv_done, 1)

            def softmax_max(g, jj):
                n, j = jj // HALF, jj % HALF
                t_i = 8 * g + jj
                dve.wait_ge(s_mm, t_i + 1)
                dve.wait_ge(qr_done, 8 * g + 4 * n + 4)
                if not (isinstance(g, int) and t_i < 2):
                    dve.wait_ge(pt_mm, t_i - 1)
                for h in range(GH):
                    t = STT(pb[:, jj % 2, h, :], bank[3][:, h * L:(h + 1) * L], qr[:, 4 * n + h, j:j + 1],
                            mask_sb[:, :], ALU.mult, ALU.add)
                t.then_inc(s_done, 1)
                dve.wait_ge(s_done, t_i + 1)
                V.tensor_reduce(nmax[:, jj % 2, :], pb[:, jj % 2, :, :], X, ALU.max, negate=True)\
                    .then_inc(max_done, 1)

            def softmax_rec(g, jj):
                dve.wait_ge(p_exp, 8 * g + jj + 1)
                V.reciprocal(prec[:, jj % 2, :], psum_[:, jj % 2, :]).then_inc(p_rec, 1)

            def pt_rest(g, jj):
                dve.wait_ge(pthi_done, 8 * g + jj + 1)
                lo(pt_lo[:, :], bank[4][:, :], pt_hi[:, :], ptlo_done)

            def ot_rest(g, jj):
                dve.wait_ge(othi_done, 8 * g + jj + 1)
                lo(ot_lo[:, :], bank[5][:, :], ot_hi[:, :], otlo_done)

            def add_out(g, jj):
                t_i = 8 * g + jj
                dve.wait_ge(d_mm, t_i + 1)
                TT(res[:, jj, :], res[:, jj, :], bank[6][:, :], ALU.add).then_inc(d_add, 1)

            def slot(g, jj, produce, before=True):
                n, j = jj // HALF, jj % HALF
                pg, pn = (g, 1) if n == 0 else (g + 1, 0)
                if j == 0:
                    softmax_rec(g, jj)
                if j < 3:
                    softmax_max(g, jj + 1)
                if produce:
                    q_rest(pg, pn, j)
                if j < 3:
                    softmax_rec(g, jj + 1)
                if produce:
                    if j == 0:
                        v_rest(pg, pn, 0)
                        v_rest(pg, pn, 1)
                    elif j < 3:
                        v_rest(pg, pn, j + 1)
                        if j == 2:
                            k_norm(pg, pn)
                    else:
                        k_rest(pg, pn)
                pt_rest(g, jj)
                if before:
                    add_out(*((g, jj - 1) if jj else (g - 1, 7)))
                if produce:
                    q_var(pg, pn, j)
                ot_rest(g, jj)
                if j == 3 and produce:
                    softmax_max(pg, 4 * pn)

            add_x(0)
            ln_stats(16)
            for j in range(HALF):
                v_rest(0, 0, j)
            k_norm(0, 0)
            for b in range(1, B):
                add_x(b)
                ln_stats(16 + b)
                ln_x(15 + b)
                norm_lo(15 + b, tb)
            ln_x(23)
            norm_lo(23, tb)
            for h in range(GH):
                q_rest(0, 0, h)
                if h:
                    q_var(0, 0, h - 1)
            k_rest(0, 0)
            q_var(0, 0, 3)
            dve.wait_ge(res_x, 8)
            softmax_max(0, 0)
            slot(0, 0, True, before=False)
            with dve.Fori(0, GROUPS - 1) as g:
                for jj in range(1, 8):
                    slot(g, jj, True)
                slot(g + 1, 0, True)
            for jj in range(1, 8):
                slot(GROUPS - 1, jj, jj < 4)
            add_out(GROUPS - 1, 7)

            def ln2(i):
                b = i % 8
                dve.wait_ge(n_rstd, i + 1)
                dst = res[:, b, :] if i < 32 else x2t[:, b, :, :].rearrange("p k n -> p (k n)")
                TS(dst, res[:, b, :], mv[:, i, 0:1], rstd[:, i:i + 1], ALU.subtract, ALU.mult).then_inc(n_x, 1)

            dve.wait_ge(d_add, 64)
            for b in range(B):
                ln_stats(24 + b)
                if b:
                    ln2(23 + b)
            ln2(31)
            dve.wait_ge(d_mm, 64)
            for e in range(NE):
                V.memset(cmp_m[:, 0, e, :], 0.0)
                t = V.memset(cmp_m[:, 1, e, :], 0.0)
            link(t)
            for e in range(NE):
                if e:
                    t = V.memset(cmp_m[:, 0, e, 0:e], 1.0)
                if e < NE - 1:
                    t = V.memset(cmp_m[:, 1, e, e + 1:NE], 1.0)
            link(t)

            def gates_rank(i):
                tl = slice(4 * i, 4 * i + 4)
                ps = bank[2 + i][:, 0:4 * 68].rearrange("p (b c) -> p b c", b=4)
                dve.wait_ge(ra_mm, 4 * i + 4)
                link(V.tensor_copy(lg[:, tl, :], ps[:, :, 0:NE]))
                flat = lg[:, tl, :].rearrange("p b e -> p (b e)")
                own = flat.unsqueeze(2).to_broadcast([P, 4 * NE, NE])
                for b in range(4):
                    o = lg[:, 4 * i + b, :]
                    own = o.unsqueeze(2).to_broadcast([P, NE, NE])
                    other = o.unsqueeze(1).to_broadcast([P, NE, NE])
                    TT(c1[:, 4 * i + b, :, :], other, own, ALU.is_ge)
                    t = TT(c2[:, 4 * i + b, :, :], other, own, ALU.is_gt)
                link(t)
                for b in range(4):
                    TT(c1[:, 4 * i + b, :, :], c1[:, 4 * i + b, :, :], cmp_m[:, 0, :, :], ALU.mult)
                    t = TT(c2[:, 4 * i + b, :, :], c2[:, 4 * i + b, :, :], cmp_m[:, 1, :, :], ALU.mult)
                link(t)
                link(TT(c1[:, tl, :, :].rearrange("p b e f -> p (b e f)"), c1[:, tl, :, :].rearrange("p b e f -> p (b e f)"),
                        c2[:, tl, :, :].rearrange("p b e f -> p (b e f)"), ALU.add))
                V.tensor_reduce(rank_t[:, tl, :].rearrange("p b e -> p (b e)"),
                                c1[:, tl, :, :].rearrange("p b e f -> p (b e) f"), X, ALU.add)
                link(V.tensor_reduce(lmax[:, tl], lg[:, tl, :], X, ALU.max))
                TT(ge[:, tl, :], lg[:, tl, :], lmax[:, tl].unsqueeze(2).to_broadcast([P, 4, NE]), ALU.subtract)\
                    .then_inc(lg_done, 1)

            def gates_mid(i):
                tl = slice(4 * i, 4 * i + 4)
                ps = bank[2 + i][:, 0:4 * 68].rearrange("p (b c) -> p b c", b=4)
                dve.wait_ge(f_exp, i + 1)
                fl = ge[:, tl, :].rearrange("p b e -> p (b e)")
                link(STT(fl, rank_t[:, tl, :].rearrange("p b e -> p (b e)"), 1.5, fl, ALU.is_lt, ALU.mult))
                link(V.tensor_reduce(gsum[:, tl], ge[:, tl, :], X, ALU.add))
                link(V.reciprocal(gsum[:, tl], gsum[:, tl]))
                link(TS(gsum[:, tl], gsum[:, tl], LORA_SCALE, None, ALU.mult))
                link(TT(ge[:, tl, :], ge[:, tl, :], gsum[:, tl].unsqueeze(2).to_broadcast([P, 4, NE]), ALU.mult))
                for b in range(4):
                    t = TT(mid[:, 4 * i + b, :, :], ps[:, b, NE:].rearrange("p (e r) -> p e r", e=NE),
                           ge[:, 4 * i + b, :].unsqueeze(2).to_broadcast([P, NE, RANK]), ALU.mult)
                t.then_inc(mid_done, 1)

            def add_delta(b):
                dve.wait_ge(dl_mm, b + 1)
                TT(res[:, b, :], res[:, b, :], bank[6 + b % 2][:, :], ALU.add).then_inc(dl_add, 1)
                dve.wait_ge(dl_add, b + 1)

            gates_rank(0)
            gates_mid(0)
            gates_rank(1)
            gates_mid(1)
            for b in range(B):
                add_delta(b)
                ln_stats(32 + b)
                if b:
                    ln2(31 + b)
            ln2(39)


_OUT = ((B, L, DM), "float32")


def kernel(x, ctx_4096, mask_1x1xSxS2_ff0, L0_attn_w_in, L0_attn_conv_w, L0_attn_conv_b, L0_attn_A_log,
           L0_attn_D, L0_attn_dt_bias, L0_attn_w_out, L0_attn_ln1_w, L0_attn_ln2_w, L0_attn_gate_w,
           L0_attn_up_w, L0_attn_down_w, L0_xattn_Wq, L0_xattn_Wk, L0_xattn_Wv, L0_xattn_Wo,
           L0_xattn_q_norm_w, L0_xattn_k_norm_w, L0_ffn_router_w, L0_ffn_A, L0_ffn_B):
    import numpy as np
    import concourse.bacc as bacc
    from concourse.bass_utils import run_bass_kernel_spmd

    a = np.asarray

    def pieces(w, cols):
        n = w.shape[0] // cols
        return a(w).reshape(n, cols, KT, P).transpose(0, 3, 2, 1).reshape(n, P, KT * cols)

    w_in = a(L0_attn_w_in)
    cut = [0, 512, 1280, 1284]
    z, xbc, dt = (w_in[cut[i]:cut[i + 1]] for i in range(3))
    gate, up = pieces(L0_attn_gate_w, P), pieces(L0_attn_up_w, P)
    w_gu = np.stack([gate.reshape(MLP_IT, 2, P, 512), up.reshape(MLP_IT, 2, P, 512)], 2)
    w_q = pieces(L0_xattn_Wq, P).reshape(GROUPS, GH, P, 512).transpose(0, 2, 1, 3).reshape(GROUPS, P, 2048)
    wk, wv = (a(w).reshape(GROUPS, HD, KT, P).transpose(0, 3, 2, 1) for w in (L0_xattn_Wk, L0_xattn_Wv))
    w_o = a(L0_xattn_Wo).T.reshape(GROUPS, GH, HD, DM).transpose(0, 2, 1, 3).reshape(GROUPS, P, 2048)
    idx = np.arange(P)
    tri = (idx[:, None] <= idx[None, :]).astype(np.float32) * np.float32(0.5)
    strict = (idx[:, None] > idx[None, :]).astype(np.float32)
    arrays = {
        "x": a(x),
        "ctx_t": a(ctx_4096).reshape(B * L, KT, P).transpose(1, 2, 0),
        "mask": a(mask_1x1xSxS2_ff0).reshape(L, L),
        "consts": np.concatenate([np.eye(P, dtype=np.float32), tri, strict], 1),
        "chan": np.concatenate([a(L0_attn_conv_w).reshape(NCONV, P, DCONV).transpose(1, 0, 2).reshape(P, -1),
                                a(L0_attn_conv_b).reshape(NCONV, P).T,
                                a(L0_xattn_q_norm_w)[:, None], a(L0_xattn_k_norm_w)[:, None]], 1),
        "rows": np.concatenate([a(L0_attn_ln1_w), a(L0_attn_ln2_w), a(L0_attn_A_log), a(L0_attn_D),
                                a(L0_attn_dt_bias)]),
        "w_dt": dt.reshape(NH, KT, P).transpose(2, 1, 0).reshape(P, KT * NH),
        "w_in": pieces(np.concatenate([xbc, z], 0), P),
        "w_out": a(L0_attn_w_out).T.reshape(NH, P, DM).transpose(1, 0, 2).reshape(P, NH * DM),
        "w_gu": w_gu.transpose(0, 3, 1, 2, 4).reshape(MLP_IT, P, 2048),
        "w_dn": a(L0_attn_down_w).T.reshape(MLP_IT, 2, P, DM).transpose(0, 2, 1, 3).reshape(MLP_IT, P, 1024),
        "w_q": w_q,
        "w_kv": np.concatenate([wk, wv], 3).reshape(GROUPS, P, 1024),
        "w_o": w_o,
        "w_ra": np.concatenate([a(L0_ffn_router_w), a(L0_ffn_A).reshape(NE * RANK, DM)], 0)
                  .reshape(NE + NE * RANK, KT, P).transpose(2, 1, 0),
        "w_b": a(L0_ffn_B).transpose(0, 2, 1).reshape(NE * RANK, DM),
    }
    arrays = {k: np.ascontiguousarray(v) for k, v in arrays.items()}
    nc = bacc.Bacc("TRN2", target_bir_lowering=False, num_devices=1)
    args = {k: nc.dram_tensor(f"in_{k}", v.shape, mybir.dt.from_np(v.dtype), kind="ExternalInput").ap()
            for k, v in arrays.items()}
    o = nc.dram_tensor("out_0", _OUT[0], mybir.dt.float32, kind="ExternalOutput").ap()
    build_program(nc, **args, out=o)
    r = run_bass_kernel_spmd(nc, [{f"in_{k}": v for k, v in arrays.items()}], core_ids=[0])
    return r.results[0]["out_0"]
```

```python
from contextlib import ExitStack

import concourse.bass as bass
from concourse import mybir

B, L, DM = 8, 128, 512
P = 128
KT = DM // P
HALF = 4
NTOK = HALF * L
NH, DSTATE, DCONV = 4, 128, 4
NCONV = 6
NPIECE = NCONV + NH
INTER = 1792
MLP_IT = INTER // (2 * P)
GROUPS, GH, HD = 8, 4, 128
NE, RANK = 4, 16
EPS = 1e-5
LORA_SCALE = 4.0
ATANH_TERMS = 8


def build_program(nc, x, ctx_t, mask, consts, chan, rows, w_dt, w_in, w_out, w_gu, w_dn,
                  w_q, w_kv, w_o, w_ra, w_b, out):
    fp32 = mybir.dt.float32
    f32r = mybir.dt.float32r
    bf16 = mybir.dt.bfloat16
    ALU = mybir.AluOpType
    ACT = mybir.ActivationFunctionType
    X = mybir.AxisListType.X

    ctx = ExitStack()
    with ctx:
        def sb(where, name, shape, dt=fp32):
            return where.enter_context(nc.sbuf_tensor(name, shape, dt))

        def sem(name):
            return ctx.enter_context(nc.semaphore(name))

        def f32(ap):
            return ap.bitcast(fp32)

        act_hi = sb(ctx, "act_hi", [P, KT, B * L], f32r)
        act_lo = sb(ctx, "act_lo", [P, KT, B * L], f32r)
        res = sb(ctx, "res", [P, B, DM])
        w_hi = sb(ctx, "w_hi", [P, 5120], f32r)
        w_lo = sb(ctx, "w_lo", [P, 5120], f32r)
        raw_a = sb(ctx, "raw_a", [P, 2048])
        raw_b = sb(ctx, "raw_b", [P, 2048])
        cst = sb(ctx, "cst", [P, 3 * P])
        ident, tri_half, strict = cst[:, 0:P], cst[:, P:2 * P], cst[:, 2 * P:3 * P]
        chan_sb = sb(ctx, "chan_sb", [P, NCONV * DCONV + NCONV + 2])
        ones = sb(ctx, "ones", [P, 1])
        qk_w = sb(ctx, "qk_w", [P, 1])
        pow_m = sb(ctx, "pow_m", [P, 16])
        xn = sb(ctx, "xn", [P, 2, DM])
        junk = sb(ctx, "junk", [P, DM], bf16)
        stat = sb(ctx, "stat", [P, 32])
        var = sb(ctx, "var", [P, 48])
        rstd = sb(ctx, "rstd", [P, 48])
        bst = sb(ctx, "bst", [P, 2, 6])
        mv = sb(ctx, "mv", [P, 48, 2])

        with ExitStack() as m:
            row_sb = sb(m, "row_sb", [P, 2 * DM + 3 * NH])
            wdt_raw = sb(m, "wdt_raw", [P, KT * NH])
            wdt_hi = sb(m, "wdt_hi", [P, KT * NH], f32r)
            wdt_lo = sb(m, "wdt_lo", [P, KT * NH], f32r)
            cw = sb(m, "cw", [P, NCONV * DCONV + NCONV])
            a2 = sb(m, "a2", [P, NH])
            d2 = sb(m, "d2", [P, NH])
            dt_sb = sb(m, "dt_sb", [P, B * NH])
            sp = sb(m, "sp", [P, 7, HALF * NH])
            pre = sb(m, "pre", [P, 2, HALF, L + DCONV - 1])
            cbuf = sb(m, "cbuf", [P, 3, NTOK])
            th = sb(m, "th", [P, 3, NTOK])
            xbc = sb(m, "xbc", [P, 2, NCONV, NTOK])
            dt_row = sb(m, "dt_row", [NH, NTOK])
            diag_d = sb(m, "diag_d", [P, NH, L])
            zt = sb(m, "zt", [P, NH, B * L])
            xtok = sb(m, "xtok", [P, 2, P])
            md = sb(m, "md", [P, 2, NH, L])
            em = sb(m, "em", [P, 2, NH, L])
            att = sb(m, "att", [P, NH, L])
            yb = sb(m, "yb", [P, 2, NH, L])
            y_hi = sb(m, "y_hi", [P, 4, NH, L], f32r)
            y_lo = sb(m, "y_lo", [P, 4, NH, L], f32r)

        ctx_hi = sb(ctx, "ctx_hi", [P, KT, B * L], f32r)
        ctx_lo = sb(ctx, "ctx_lo", [P, KT, B * L], f32r)
        with ExitStack() as m:
            h_hi = sb(m, "h_hi", [P, 2, B * L], f32r)
            h_lo = sb(m, "h_lo", [P, 2, B * L], f32r)
            sg = sb(m, "sg", [P, 2, NTOK])
            hb = sb(m, "hb", [P, 2, NTOK])
            xre = sb(m, "xre", [P, 2, DM])

        with ExitStack() as m:
            mask_sb = sb(m, "mask_sb", [P, L])
            q_t = sb(m, "q_t", [P, 2, GH, NTOK])
            k_t = sb(m, "k_t", [P, 2, NTOK])
            v_hi = sb(m, "v_hi", [P, 2, HALF, HD], f32r)
            v_lo = sb(m, "v_lo", [P, 2, HALF, HD], f32r)
            kraw = sb(m, "kraw", [P, HALF, HD])
            qsq = xn[:, 0, :]
            qv = sb(m, "qv", [P, 2 * GH, HALF])
            qr = sb(m, "qr", [P, 2 * GH, HALF])
            kv = sb(m, "kv", [P, 3, HALF])
            pb = sb(m, "pb", [P, 2, GH, L])
            nmax = sb(m, "nmax", [P, 2, GH])
            psum_ = sb(m, "psum_", [P, 2, GH])
            prec = sb(m, "prec", [P, 2, GH])
            pt_hi = sb(m, "pt_hi", [P, GH * L], f32r)
            pt_lo = sb(m, "pt_lo", [P, GH * L], f32r)
            ot_hi = sb(m, "ot_hi", [P, GH * L], f32r)
            ot_lo = sb(m, "ot_lo", [P, GH * L], f32r)

            x2t = sb(m, "x2t", [P, 2, KT, P])
            ra_sb = sb(m, "ra_sb", [P, KT, NE + NE * RANK])
            bl_sb = sb(m, "bl_sb", [NE * RANK, DM])
            cmp_m = sb(m, "cmp_m", [P, 2, NE, NE])
            lg = sb(m, "lg", [P, B, NE])
            c1 = sb(m, "c1", [P, B, NE, NE])
            c2 = sb(m, "c2", [P, B, NE, NE])
            rank_t = sb(m, "rank_t", [P, B, NE])
            lmax = sb(m, "lmax", [P, B])
            ge = sb(m, "ge", [P, B, NE])
            gsum = sb(m, "gsum", [P, B])
            mid = sb(m, "mid", [P, B, NE, RANK])
            midt = sb(m, "midt", [NE * RANK, B, P])

        bank = [ctx.enter_context(nc.psum_tensor(f"bank{i}", [P, 512], fp32)) for i in range(8)]

        ld_x = [sem(f"ld_x{b}") for b in range(B)]
        ld_small = [sem(f"ld_small{i}") for i in range(5)]
        ld_win = [sem(f"ld_win{i}") for i in range(8)]
        ld_wout = sem("ld_wout")
        ld_gu = sem("ld_gu")
        ld_dn = sem("ld_dn")
        ld_ctx = [sem("ld_ctx0"), sem("ld_ctx1")]
        ld_xre = [sem("ld_xre0"), sem("ld_xre1")]
        ld_q = sem("ld_q")
        ld_kv = sem("ld_kv")
        ld_o = sem("ld_o")
        ld_lora = [sem("ld_lora0"), sem("ld_lora1")]
        st_out = sem("st_out")

        n_ssq, n_var, n_rstd, n_x = sem("n_ssq"), sem("n_var"), sem("n_rstd"), sem("n_x")
        n_t, n_hi, n_lo, n_bn, n_mv = sem("n_t"), sem("n_hi"), sem("n_lo"), sem("n_bn"), sem("n_mv")
        res_x, vlo_done = sem("res_x"), sem("vlo_done")
        x_add = sem("x_add")

        dt_w = sem("dt_w")
        win_h, win_l = sem("win_h"), sem("win_l")
        wout_h, wout_l = sem("wout_h"), sem("wout_l")
        gu_h, gu_l = sem("gu_h"), sem("gu_l")
        dn_h, dn_l = sem("dn_h"), sem("dn_l")
        cx_h, cx_l = sem("cx_h"), sem("cx_l")
        wq_h, wq_l = sem("wq_h"), sem("wq_l")
        wkv_h, wkv_l = sem("wkv_h"), sem("wkv_l")
        wo_h, wo_l = sem("wo_h"), sem("wo_l")

        setup_v, setup_a, setup_p = sem("setup_v"), sem("setup_a"), sem("setup_p")
        in_mm, conv_ev, conv_c, conv_th, conv_out = (sem("in_mm"), sem("conv_ev"), sem("conv_c"),
                                                     sem("conv_th"), sem("conv_out"))
        z_th, z_out = sem("z_th"), sem("z_out")
        dt_mm, dt_ev, dt_t = sem("dt_mm"), sem("dt_ev"), sem("dt_t")
        dt_a, dt_exp_done, dt_done, diag_done = sem("dt_a"), sem("dt_exp_done"), sem("dt_done"), sem("diag_done")
        md_done, xt_mm, xt_ev, cum_mm, exp_done = (sem("md_done"), sem("xt_mm"), sem("xt_ev"),
                                                   sem("cum_mm"), sem("exp_done"))
        em_done, sc_mm, att_done, y_mm, y1_done = (sem("em_done"), sem("sc_mm"), sem("att_done"),
                                                   sem("y_mm"), sem("y1_done"))
        yhi_done, ylo_done = sem("yhi_done"), sem("ylo_done")
        o_mm, o_add = sem("o_mm"), sem("o_add")
        vch = sem("vch")
        gu_mm, silu_done, h_done, hhi_done, hlo_done = (sem("gu_mm"), sem("silu_done"), sem("h_done"),
                                                        sem("hhi_done"), sem("hlo_done"))
        q_mm, q_ev, qsq_done = sem("q_mm"), sem("q_ev"), sem("qsq_done")
        ss_mm, qv_done, qr_done = sem("ss_mm"), sem("qv_done"), sem("qr_done")
        kv_mm, ksq_done, vhi_done, kraw_done = sem("kv_mm"), sem("ksq_done"), sem("vhi_done"), sem("kraw_done")
        kvar_done, kr_done, kn_done = sem("kvar_done"), sem("kr_done"), sem("kn_done")
        kt_mm, kt_ev = sem("kt_mm"), sem("kt_ev")
        s_mm, s_done, max_done, p_exp, p_rec, p_norm = (sem("s_mm"), sem("s_done"), sem("max_done"),
                                                        sem("p_exp"), sem("p_rec"), sem("p_norm"))
        pt_mm, pthi_done, ptlo_done = sem("pt_mm"), sem("pthi_done"), sem("ptlo_done")
        pv_mm, othi_done, otlo_done = sem("pv_mm"), sem("othi_done"), sem("otlo_done")
        d_mm, d_add = sem("d_mm"), sem("d_add")
        f_x2t, ra_mm, lg_done, f_exp, mid_done = (sem("f_x2t"), sem("ra_mm"), sem("lg_done"),
                                                  sem("f_exp"), sem("mid_done"))
        mt_mm, mt_ev, dl_mm, dl_add = sem("mt_mm"), sem("mt_ev"), sem("dl_mm"), sem("dl_add")

        block = ctx.enter_context(nc.Block())

        OUT_COL = 0
        DN_COL, GU_COL = 2048, 3072
        WKV_COL = 0
        WQ_COL = [1024, 1536, 3072, 3584]
        WQ_SLOT = [1, 3, 4, 5]
        WO_COL = [2048, 2560, 4096, 4608]
        RAC = NE + NE * RANK

        def mamba_raw(p):
            return raw_b[:, (p - 4) * 512:(p - 3) * 512] if 4 <= p < 8 else raw_a[:, p % 8 * 512:(p % 8 + 1) * 512]

        @block.sync
        def _(sp_eng):
            def load_x(b):
                sp_eng.dma_start(res[:, b, :], x[b]).then_inc(ld_x[b], 16)

            def load_win(p):
                if p >= 8:
                    sp_eng.wait_ge(win_l, p - 7)
                sp_eng.dma_start(mamba_raw(p), w_in[p]).then_inc(ld_win[p % 8], 16)

            load_x(0)
            sp_eng.dma_start(cst[:, :], consts).then_inc(ld_small[0], 16)
            load_x(1)
            sp_eng.dma_start(row_sb[:, :], rows.partition_broadcast(P)).then_inc(ld_small[1], 16)
            load_x(2)
            load_x(3)
            load_win(0)
            sp_eng.dma_start(wdt_raw[:, :], w_dt).then_inc(ld_small[3], 16)
            sp_eng.dma_start(chan_sb[:, :], chan).then_inc(ld_small[2], 16)
            load_win(1)
            load_win(2)
            load_win(3)
            for b in range(4, 8):
                load_win(b)
                load_x(b)
            load_win(8)
            load_win(9)
            sp_eng.wait_ge(win_l, 8)
            sp_eng.dma_start(raw_b[:, :], w_out).then_inc(ld_wout, 16)
            sp_eng.wait_ge(win_l, 10)
            sp_eng.dma_start(raw_a[:, :], w_gu[0]).then_inc(ld_gu, 16)
            sp_eng.wait_ge(wout_l, 4)
            sp_eng.dma_start(raw_b[:, 0:1024], w_dn[0]).then_inc(ld_dn, 16)

            def load_ctx(i):
                if i >= 2:
                    sp_eng.wait_ge(cx_l, i - 1)
                sp_eng.dma_start(raw_b[:, 1024 + i % 2 * 512:1536 + i % 2 * 512],
                                 ctx_t[i // 2, :, i % 2 * 512:(i % 2 + 1) * 512]).then_inc(ld_ctx[i % 2], 16)

            load_ctx(0)
            load_ctx(1)

            def load_xre(b):
                if b >= 2:
                    sp_eng.wait_ge(x_add, b - 1)
                sp_eng.dma_start(xre[:, b % 2, :], x[b]).then_inc(ld_xre[b % 2], 16)

            def next_mlp(c):
                sp_eng.wait_ge(dn_l, 2 * c + 2)
                sp_eng.dma_start(raw_b[:, 0:1024], w_dn[bass.ds(c + 1, 1)].rearrange("a p n -> (a p) n"))\
                    .then_inc(ld_dn, 16)
                sp_eng.wait_ge(gu_l, 4 * c + 4)
                sp_eng.dma_start(raw_a[:, :], w_gu[bass.ds(c + 1, 1)].rearrange("a p n -> (a p) n"))\
                    .then_inc(ld_gu, 16)

            sp_eng.wait_ge(gu_l, 4)
            sp_eng.dma_start(raw_a[:, :], w_gu[1]).then_inc(ld_gu, 16)
            sp_eng.wait_ge(o_mm, 8)
            sp_eng.wait_ge(n_x, 16)
            load_xre(0)
            load_xre(1)
            for i in range(2, 8):
                load_ctx(i)
                load_xre(i)
            sp_eng.wait_ge(dn_l, 2)
            sp_eng.dma_start(raw_b[:, 0:1024], w_dn[1]).then_inc(ld_dn, 16)
            with sp_eng.Fori(1, MLP_IT - 1) as c:
                next_mlp(c)
            sp_eng.wait_ge(gu_l, 4 * MLP_IT)
            sp_eng.dma_start(raw_a[:, :], w_q[0]).then_inc(ld_q, 16)
            sp_eng.wait_ge(dn_l, 2 * MLP_IT)
            sp_eng.dma_start(raw_b[:, 0:1024], w_kv[0]).then_inc(ld_kv, 16)
            sp_eng.wait_ge(wkv_l, 2)
            sp_eng.dma_start(raw_b[:, :], w_o[0]).then_inc(ld_o, 16)
            sp_eng.wait_ge(n_x, 24)
            sp_eng.dma_start(mask_sb[:, :], mask).then_inc(ld_small[4], 16)
            sp_eng.dma_start(ra_sb[:, :, :], w_ra).then_inc(ld_lora[0], 16)
            sp_eng.dma_start(bl_sb[:, :], w_b).then_inc(ld_lora[1], 16)

            def next_group(g):
                sp_eng.wait_ge(wq_l, 4 * g + 4)
                sp_eng.dma_start(raw_a[:, :], w_q[bass.ds(g + 1, 1)].rearrange("a p n -> (a p) n"))\
                    .then_inc(ld_q, 16)
                sp_eng.wait_ge(wo_l, 4 * g + 4)
                sp_eng.dma_start(raw_b[:, 0:1024], w_kv[bass.ds(g + 1, 1)].rearrange("a p n -> (a p) n"))\
                    .then_inc(ld_kv, 16)
                sp_eng.wait_ge(wkv_l, 2 * g + 4)
                sp_eng.dma_start(raw_b[:, :], w_o[bass.ds(g + 1, 1)].rearrange("a p n -> (a p) n"))\
                    .then_inc(ld_o, 16)

            with sp_eng.Fori(0, GROUPS - 1) as g:
                next_group(g)
            for b in range(B):
                sp_eng.wait_ge(n_x, 33 + b)
                sp_eng.dma_start(out[b], res[:, b, :]).then_inc(st_out, 16)
            sp_eng.wait_ge(st_out, 16 * B)

        @block.tensor
        def _(pe):
            mm = nc.tensor.matmul

            def mm3(o, l_hi, l_lo, r_hi, r_lo, first, last):
                mm(o, l_hi, r_hi, start=first, stop=False)
                mm(o, l_hi, r_lo, start=False, stop=False)
                return mm(o, l_lo, r_hi, start=False, stop=last)

            def norm_t(i, banks):
                pe.wait_ge(n_x, i + 1)
                if i >= 2:
                    pe.wait_ge(n_lo, i - 1)
                for k in range(KT):
                    t = nc.tensor.transpose(banks[i % 2][:, k * P:(k + 1) * P],
                                            xn[:, i % 2, k * P:(k + 1) * P], ident)
                t.then_inc(n_t, 1)

            order = [(n, p) for n in range(2) for p in range(NPIECE)]

            def in_step(f):
                n, p = order[f]
                pe.wait_ge(win_l, p + 1)
                pe.wait_ge(n_lo, 4 * n + 4)
                if f >= 2:
                    pn, pp = order[f - 2]
                    if pp < NCONV:
                        pe.wait_ge(conv_ev, NCONV * pn + pp + 1)
                    else:
                        pe.wait_ge(z_out, NH * pn + pp - NCONV + 1)
                for k in range(KT):
                    c0 = p * 512 + k * P
                    tok = slice(n * NTOK, (n + 1) * NTOK)
                    t = mm3(bank[f % 2][:, :], w_hi[:, c0:c0 + P], w_lo[:, c0:c0 + P],
                            act_hi[:, k, tok], act_lo[:, k, tok], k == 0, k == KT - 1)
                t.then_inc(in_mm, 1)

            def dt_step(n):
                pe.wait_ge(dt_w, 2)
                if n:
                    pe.wait_ge(dt_a, 1)
                for k in range(KT):
                    t = mm3(bank[7][0:NH, :], wdt_hi[:, k * NH:(k + 1) * NH], wdt_lo[:, k * NH:(k + 1) * NH],
                            act_hi[:, k, n * NTOK:(n + 1) * NTOK], act_lo[:, k, n * NTOK:(n + 1) * NTOK],
                            k == 0, k == KT - 1)
                t.then_inc(dt_mm, 1)

            def dt_turn(n):
                pe.wait_ge(dt_ev, n + 1)
                for j in range(HALF):
                    t = nc.tensor.transpose(bank[7][:, j * NH:(j + 1) * NH], dt_row[:, j * L:(j + 1) * L],
                                            ident[0:NH, 0:NH])
                t.then_inc(dt_t, 1)

            def ssm1(b):
                n, tok = b // HALF, slice(b % HALF * L, (b % HALF + 1) * L)
                pe.wait_ge(conv_out, NCONV * n + NCONV)
                if b:
                    pe.wait_ge(xt_ev, b)
                nc.tensor.transpose(bank[5][:, 0:P], xbc[:, n, 0, tok], ident).then_inc(xt_mm, 1)
                pe.wait_ge(md_done, b + 1)
                if b:
                    pe.wait_ge(exp_done, b)
                mm(bank[2][:, :], strict, md[:, b % 2, :, :], start=True, stop=True).then_inc(cum_mm, 1)
                if b:
                    pe.wait_ge(att_done, b)
                mm(bank[3][:, :], xbc[:, n, 1, tok], xbc[:, n, 2:6, tok], start=True, stop=True).then_inc(sc_mm, 1)

            def ssm2(b):
                pe.wait_ge(att_done, b + 1)
                pe.wait_ge(xt_ev, b + 1)
                if b:
                    pe.wait_ge(y1_done, b)
                mm(bank[4][:, :], xtok[:, b % 2, :], att[:, :, :], start=True, stop=True).then_inc(y_mm, 1)

            def out_step(b):
                pe.wait_ge(wout_l, 4)
                pe.wait_ge(ylo_done, b + 1)
                if b >= 2:
                    pe.wait_ge(o_add, b - 1)
                for k in range(NH):
                    c0 = OUT_COL + k * 512
                    t = mm3(bank[6 + b % 2][:, :], y_hi[:, b % 4, k, :], y_lo[:, b % 4, k, :],
                            w_hi[:, c0:c0 + 512], w_lo[:, c0:c0 + 512], k == 0, k == NH - 1)
                t.then_inc(o_mm, 1)

            pe.wait_ge(ld_small[0], 16)
            for i in range(4):
                norm_t(i, (bank[2], bank[3]))
            tb = (bank[0], bank[1])
            in_step(0)
            dt_step(0)
            in_step(1)
            dt_turn(0)
            for f in range(2, 6):
                in_step(f)
            for i in range(4, 8):
                norm_t(i, (bank[2], bank[3]))
            for f in range(6, 10):
                in_step(f)
            dt_step(1)
            in_step(10)
            dt_turn(1)
            in_step(11)
            pe.wait_ge(n_lo, 8)
            ssm1(0)
            in_step(12)
            ssm2(0)
            ssm1(1)
            in_step(13)
            ssm2(1)
            ssm1(2)
            in_step(14)
            ssm2(2)
            ssm1(3)
            in_step(15)
            ssm2(3)
            in_step(16)
            pe.wait_ge(dt_a, 2)
            in_step(17)
            out_step(0)
            ssm1(4)
            out_step(1)
            in_step(18)
            ssm2(4)
            ssm1(5)
            out_step(2)
            in_step(19)
            ssm2(5)
            ssm1(6)
            out_step(3)
            pe.wait_ge(z_out, 8)
            norm_t(8, tb)
            ssm2(6)
            ssm1(7)
            norm_t(9, tb)
            out_step(4)
            norm_t(10, tb)
            ssm2(7)
            out_step(5)
            norm_t(11, tb)
            out_step(6)
            norm_t(12, tb)
            out_step(7)
            pe.wait_ge(y1_done, 8)

            def gu_step(c, k, n):
                m_i = 2 * n + k
                pe.wait_ge(gu_l, 4 * c + 2 * k + 2)
                if not (isinstance(c, int) and 4 * c + m_i < 2):
                    pe.wait_ge(h_done, 4 * c + m_i - 1)
                tok = slice(n * NTOK, (n + 1) * NTOK)
                for which in range(2):
                    o = bank[(2, 4)[m_i % 2] + which]
                    for kk in range(KT):
                        c0 = GU_COL + (2 * k + which) * 512 + kk * P
                        t = mm3(o[:, :], w_hi[:, c0:c0 + P], w_lo[:, c0:c0 + P],
                                act_hi[:, kk, tok], act_lo[:, kk, tok], kk == 0, kk == KT - 1)
                t.then_inc(gu_mm, 1)

            def dn_step(c, b):
                pe.wait_ge(hlo_done, 4 * c + 2 * (b // HALF) + 2)
                if b == 0:
                    pe.wait_ge(dn_l, 2 * c + 2)
                pe.wait_ge(o_add, 8 + 8 * c + b - 1)
                tok = slice(b * L, (b + 1) * L)
                for k in range(2):
                    c0 = DN_COL + k * 512
                    t = mm3(bank[6 + b % 2][:, :], h_hi[:, k, tok], h_lo[:, k, tok],
                            w_hi[:, c0:c0 + 512], w_lo[:, c0:c0 + 512], k == 0, k == 1)
                t.then_inc(o_mm, 1)

            def mlp_step(c):
                first, last = (isinstance(c, int) and c == x for x in (0, MLP_IT - 1))
                if first:
                    pe.wait_ge(n_lo, 12)
                gu_step(c, 0, 0)
                if first:
                    norm_t(13, tb)
                    norm_t(14, tb)
                gu_step(c, 1, 0)
                if first:
                    norm_t(15, tb)
                    pe.wait_ge(n_lo, 16)
                gu_step(c, 0, 1)
                gu_step(c, 1, 1)
                for b in range(B):
                    dn_step(c, b)
                    if last and b >= 3:
                        norm_t(13 + b, tb)

            mlp_step(0)
            with pe.Fori(1, MLP_IT - 1) as c:
                mlp_step(c)
            mlp_step(MLP_IT - 1)

            def q_step(u, h):
                g, n = u
                hh = h
                pe.wait_ge(wq_l, 4 * g + hh + 1)
                r = 5 * n + hh
                wait_bank(g, r)
                tok = slice(n * NTOK, (n + 1) * NTOK)
                for k in range(KT):
                    c0 = WQ_COL[hh] + k * P
                    t = mm3(bank[r % 2][:, :], w_hi[:, c0:c0 + P], w_lo[:, c0:c0 + P],
                            act_hi[:, k, tok], act_lo[:, k, tok], k == 0, k == KT - 1)
                t.then_inc(q_mm, 1)

            def wait_bank(g, r):
                pr = (r - 2) % 10
                gg = g if r >= 2 else g - 1
                if isinstance(gg, int) and gg < 0:
                    return
                n, hh = pr // 5, pr % 5
                if hh < 4:
                    pe.wait_ge(qsq_done, 8 * gg + 4 * n + hh + 1)
                else:
                    pe.wait_ge(kt_ev, 2 * gg + n + 1)

            def ss_step(g, n, h):
                i = 8 * g + 4 * n + h
                pe.wait_ge(qsq_done, i + 1)
                if not (isinstance(g, int) and i == 0):
                    pe.wait_ge(qv_done, i)
                for j in range(HALF):
                    t = mm(bank[7][:, j:j + 1], qsq[:, j * L:(j + 1) * L], ones[:, :], start=True, stop=True)
                t.then_inc(ss_mm, 1)

            def kv_step(g, n, j):
                i = 8 * g + 4 * n + j
                pe.wait_ge(wkv_l, 2 * g + 2)
                if not (isinstance(g, int) and i == 0):
                    pe.wait_ge(kraw_done, i)
                tok = slice((4 * n + j) * L, (4 * n + j + 1) * L)
                for k in range(KT):
                    c0 = WKV_COL + k * 256
                    t = mm3(bank[2][:, 0:256], ctx_hi[:, k, tok], ctx_lo[:, k, tok],
                            w_hi[:, c0:c0 + 256], w_lo[:, c0:c0 + 256], k == 0, k == KT - 1)
                t.then_inc(kv_mm, 1)

            def kt_step(g, n):
                pe.wait_ge(kn_done, 2 * g + n + 1)
                wait_bank(g, 5 * n + 4)
                for j in range(HALF):
                    t = nc.tensor.transpose(bank[(5 * n + 4) % 2][:, j * P:(j + 1) * P], kraw[:, j, :], ident)
                t.then_inc(kt_mm, 1)

            def s_step(g, jj):
                n, j = jj // HALF, jj % HALF
                t_i = 8 * g + jj
                pe.wait_ge(q_ev, 8 * g + 4 * n + 4)
                pe.wait_ge(kt_ev, 2 * g + n + 1)
                if not (isinstance(g, int) and t_i == 0):
                    pe.wait_ge(s_done, t_i)
                tok = slice(j * L, (j + 1) * L)
                for h in range(GH):
                    t = mm(bank[3][:, h * L:(h + 1) * L], q_t[:, n, h, tok], k_t[:, n, tok],
                           start=True, stop=True)
                t.then_inc(s_mm, 1)

            def pt_step(g, jj):
                t_i = 8 * g + jj
                pe.wait_ge(p_norm, t_i + 1)
                if not (isinstance(g, int) and t_i == 0):
                    pe.wait_ge(ptlo_done, t_i)
                for h in range(GH):
                    t = nc.tensor.transpose(bank[4][:, h * L:(h + 1) * L], pb[:, jj % 2, h, :], ident)
                t.then_inc(pt_mm, 1)

            def pv_step(g, jj):
                t_i = 8 * g + jj
                pe.wait_ge(ptlo_done, t_i + 1)
                if not (isinstance(g, int) and t_i == 0):
                    pe.wait_ge(otlo_done, t_i)
                n, j = jj // HALF, jj % HALF
                mm3(bank[5][:, :], v_hi[:, n, j, :], v_lo[:, n, j, :], pt_hi[:, :], pt_lo[:, :], True, True)\
                    .then_inc(pv_mm, 1)

            def d_step(g, jj):
                t_i = 8 * g + jj
                pe.wait_ge(otlo_done, t_i + 1)
                if not (isinstance(g, int) and t_i == 0):
                    pe.wait_ge(d_add, t_i)
                for h in range(GH):
                    hs = slice(h * L, (h + 1) * L)
                    c0 = WO_COL[h]
                    if jj == 0:
                        pe.wait_ge(wo_l, 4 * g + h + 1)
                    t = mm3(bank[6][:, :], ot_hi[:, hs], ot_lo[:, hs], w_hi[:, c0:c0 + 512],
                            w_lo[:, c0:c0 + 512], h == 0, h == GH - 1)
                t.then_inc(d_mm, 1)

            def slot(g, jj, produce, before=True):
                n, j = jj // HALF, jj % HALF
                pg, pn = (g, 1) if n == 0 else (g + 1, 0)
                if produce:
                    if j == 0:
                        kv_step(pg, pn, 0)
                    q_step((pg, pn), j)
                    if j == 3:
                        kt_step(pg, pn)
                if j < 3:
                    s_step(g, jj + 1)
                if produce and j < 3:
                    kv_step(pg, pn, j + 1)
                pt_step(g, jj)
                if before:
                    d_step(*((g, jj - 1) if jj else (g - 1, 7)))
                if produce:
                    ss_step(pg, pn, j)
                pv_step(g, jj)
                if j == 3 and produce:
                    s_step(pg, 4 * pn)

            pe.wait_ge(h_done, 4 * MLP_IT)
            kv_step(0, 0, 0)
            norm_t(21, tb)
            kv_step(0, 0, 1)
            norm_t(22, tb)
            kv_step(0, 0, 2)
            norm_t(23, tb)
            kv_step(0, 0, 3)
            pe.wait_ge(n_lo, 24)
            pe.wait_ge(o_add, 8 + 8 * MLP_IT)
            for h in range(GH):
                q_step((0, 0), h)
                if h:
                    ss_step(0, 0, h - 1)
            kt_step(0, 0)
            ss_step(0, 0, 3)
            s_step(0, 0)
            slot(0, 0, True, before=False)
            with pe.Fori(0, GROUPS - 1) as g:
                for jj in range(1, 8):
                    slot(g, jj, True)
                slot(g + 1, 0, True)

            def lora_in(b):
                if b == 0:
                    pe.wait_ge(ld_lora[0], 16)
                pe.wait_ge(f_x2t, b + 1)
                o = bank[(2, 7)[b // 4]]
                for k in range(KT):
                    t = mm(o[:, b % 4 * RAC:(b % 4 + 1) * RAC], x2t[:, b % 2, k, :], ra_sb[:, k, :],
                           start=(k == 0), stop=(k == KT - 1))
                t.then_inc(ra_mm, 1)

            def f_norm_t(i):
                pe.wait_ge(n_x, i + 1)
                if i >= 26:
                    pe.wait_ge(f_x2t, i - 25)
                for k in range(KT):
                    t = nc.tensor.transpose(tb[i % 2][:, k * P:(k + 1) * P], res[:, i - 24, k * P:(k + 1) * P],
                                            ident)
                t.then_inc(n_t, 1)

            def mt_step(i):
                pe.wait_ge(mid_done, i + 1)
                for b in range(4 * i, 4 * i + 4):
                    t = nc.tensor.transpose(bank[(2, 7)[i]][0:NE * RANK, b % 4 * P:(b % 4 + 1) * P],
                                            mid[:, b, :, :].rearrange("p e r -> p (e r)"), ident)
                t.then_inc(mt_mm, 1)

            def dl_step(b):
                if b == 0:
                    pe.wait_ge(ld_lora[1], 16)
                    pe.wait_ge(s_done, 64)
                    pe.wait_ge(d_add, 64)
                pe.wait_ge(mt_ev, b // 4 + 1)
                if b >= 2:
                    pe.wait_ge(dl_add, b - 1)
                mm(bank[(3, 6)[b % 2]][:, :], midt[:, b, :], bl_sb[:, :], start=True, stop=True)\
                    .then_inc(dl_mm, 1)

            last = GROUPS - 1
            for jj in range(1, 4):
                slot(last, jj, True)
            pe.wait_ge(kt_ev, 16)
            pe.wait_ge(qv_done, 64)
            slot(last, 4, False)
            f_norm_t(24)
            f_norm_t(25)
            slot(last, 5, False)
            lora_in(0)
            f_norm_t(26)
            lora_in(1)
            f_norm_t(27)
            slot(last, 6, False)
            lora_in(2)
            f_norm_t(28)
            lora_in(3)
            slot(last, 7, False)
            f_norm_t(29)
            lora_in(4)
            d_step(last, 7)
            mt_step(0)
            f_norm_t(30)
            lora_in(5)
            lora_in(6)
            f_norm_t(31)
            lora_in(7)
            for b in range(4):
                dl_step(b)
            mt_step(1)
            for b in range(4, 8):
                dl_step(b)

        @block.scalar
        def _(act):
            A = nc.scalar.activation

            def square(i):
                if i < 8:
                    act.wait_ge(ld_x[i], 16)
                else:
                    act.wait_ge(o_add, i - 7)
                if i >= 1:
                    act.wait_ge(n_ssq, i)
                A(junk[:, :], res[:, i % 8, :], ACT.Square, accum_out=stat[:, i:i + 1]).then_inc(n_ssq, 1)

            def norm_hi(i, banks):
                act.wait_ge(n_t, i + 1)
                b = i % 8
                A(act_hi[:, :, b * L:(b + 1) * L], banks[i % 2][:, :].rearrange("p (k n) -> p k n", k=KT),
                  ACT.Copy).then_inc(n_hi, 1)

            def win_hi(p):
                act.wait_ge(ld_win[p % 8], 16 * (p // 8 + 1))
                A(w_hi[:, p * 512:(p + 1) * 512], mamba_raw(p), ACT.Copy).then_inc(win_h, 1)

            nb = (bank[2], bank[3])
            square(0)
            square(1)
            win_hi(0)
            norm_hi(0, nb)
            act.wait_ge(ld_small[3], 16)
            A(wdt_hi[:, :], wdt_raw[:, :], ACT.Copy).then_inc(dt_w, 1)
            square(2)
            norm_hi(1, nb)
            square(3)
            norm_hi(2, nb)
            win_hi(1)
            act.wait_ge(ld_small[1], 16)
            A(a2[:, :], row_sb[:, 2 * DM:2 * DM + NH], ACT.Exp).then_inc(setup_a, 1)
            norm_hi(3, nb)
            win_hi(2)
            win_hi(3)

            order = [(n, p) for n in range(2) for p in range(NPIECE)]

            def in_evac(f):
                n, p = order[f]
                act.wait_ge(in_mm, f + 1)
                if p < NCONV:
                    q = NCONV * n + p
                    if q == 0:
                        act.wait_ge(setup_v, 4)
                    if q >= 2:
                        act.wait_ge(conv_c, q - 1)
                    A(pre[:, q % 2, :, DCONV - 1:], bank[f % 2][:, :].rearrange("p (s n) -> p s n", s=HALF),
                      ACT.Copy)
                    if q >= 3:
                        act.wait_ge(conv_out, q - 2)
                    A(cbuf[:, q % 3, :], bank[f % 2][:, :], ACT.Identity,
                      bias=cw[:, NCONV * DCONV + p:NCONV * DCONV + p + 1],
                      scale=cw[:, p * DCONV + DCONV - 1:p * DCONV + DCONV]).then_inc(conv_ev, 1)
                else:
                    i = NH * n + p - NCONV
                    if i >= 1:
                        act.wait_ge(z_out, i)
                    A(th[:, 0, :], bank[f % 2][:, :], ACT.Tanh, scale=0.5).then_inc(z_th, 1)

            def conv_tanh(q):
                act.wait_ge(conv_c, q + 1)
                if q >= 2:
                    act.wait_ge(conv_out, q - 1)
                A(th[:, 1 + q % 2, :], cbuf[:, q % 3, :], ACT.Tanh).then_inc(conv_th, 1)

            def dt_evac(n):
                act.wait_ge(dt_mm, n + 1)
                if n:
                    act.wait_ge(dt_t, n)
                A(dt_row[:, :], bank[7][0:NH, :], ACT.Copy).then_inc(dt_ev, 1)

            def dt_exp(n):
                act.wait_ge(dt_a, n + 1)
                A(sp[:, 2, :], sp[:, 1, :], ACT.Exp).then_inc(dt_exp_done, 1)

            def x_evac(b):
                act.wait_ge(xt_mm, b + 1)
                if b >= 2:
                    act.wait_ge(y_mm, b - 1)
                A(xtok[:, b % 2, :], bank[5][:, 0:P], ACT.Copy).then_inc(xt_ev, 1)

            def decay(b):
                act.wait_ge(cum_mm, b + 1)
                if b == 0:
                    act.wait_ge(setup_v, 4)
                if b >= 2:
                    act.wait_ge(att_done, b - 1)
                for h in range(NH):
                    t = A(em[:, b % 2, h, :], bank[2][:, h * L:(h + 1) * L], ACT.Exp, scale=a2[:, h:h + 1])
                t.then_inc(exp_done, 1)

            def y_split(b):
                act.wait_ge(y1_done, b + 1)
                if b >= 4:
                    act.wait_ge(o_mm, b - 3)
                A(y_hi[:, b % 4, :, :], yb[:, b % 2, :, :], ACT.Copy).then_inc(yhi_done, 1)

            in_evac(0)
            win_hi(4)
            dt_evac(0)
            in_evac(1)
            conv_tanh(0)
            win_hi(5)
            square(4)
            in_evac(2)
            conv_tanh(1)
            win_hi(6)
            dt_exp(0)
            square(5)
            in_evac(3)
            conv_tanh(2)
            win_hi(7)
            square(6)
            in_evac(4)
            conv_tanh(3)
            win_hi(8)
            square(7)
            in_evac(5)
            conv_tanh(4)
            for i in range(4, 8):
                norm_hi(i, nb)
            win_hi(9)
            in_evac(6)
            conv_tanh(5)
            for f in range(7, 10):
                in_evac(f)
            dt_evac(1)
            in_evac(10)
            dt_exp(1)
            in_evac(11)
            conv_tanh(6)
            x_evac(0)
            decay(0)
            in_evac(12)
            conv_tanh(7)
            x_evac(1)
            decay(1)
            in_evac(13)
            conv_tanh(8)
            y_split(0)
            x_evac(2)
            decay(2)
            in_evac(14)
            conv_tanh(9)
            y_split(1)
            x_evac(3)
            decay(3)

            def wout_hi(k):
                if k == 0:
                    act.wait_ge(ld_wout, 16)
                    act.wait_ge(in_mm, 14)
                A(w_hi[:, OUT_COL + k * 512:OUT_COL + (k + 1) * 512], raw_b[:, k * 512:(k + 1) * 512],
                  ACT.Copy).then_inc(wout_h, 1)

            for k in range(2):
                wout_hi(k)
            in_evac(15)
            conv_tanh(10)
            for k in range(2, 4):
                wout_hi(k)
            y_split(2)
            in_evac(16)
            conv_tanh(11)
            y_split(3)
            in_evac(17)
            x_evac(4)
            decay(4)
            square(8)
            in_evac(18)
            x_evac(5)
            decay(5)
            in_evac(19)
            y_split(4)
            square(9)
            square(10)
            y_split(5)
            tb = (bank[0], bank[1])

            def gu_hi(c, i):
                act.wait_ge(ld_gu, 16 * c + 16)
                if isinstance(c, int) and c == 0:
                    act.wait_ge(in_mm, 20)
                else:
                    act.wait_ge(gu_mm, 4 * c)
                A(w_hi[:, GU_COL + i * 512:GU_COL + (i + 1) * 512], raw_a[:, i * 512:(i + 1) * 512],
                  ACT.Copy).then_inc(gu_h, 1)

            def dn_hi(c, i):
                act.wait_ge(ld_dn, 16 * c + 16)
                if not (isinstance(c, int) and c == 0):
                    act.wait_ge(o_mm, 8 + 8 * c)
                A(w_hi[:, DN_COL + i * 512:DN_COL + (i + 1) * 512], raw_b[:, i * 512:(i + 1) * 512],
                  ACT.Copy).then_inc(dn_h, 1)

            x_evac(6)
            decay(6)
            gu_hi(0, 0)
            square(11)
            norm_hi(8, tb)
            gu_hi(0, 1)
            y_split(6)
            x_evac(7)
            decay(7)
            norm_hi(9, tb)
            gu_hi(0, 2)
            square(12)
            norm_hi(10, tb)
            y_split(7)
            gu_hi(0, 3)
            square(13)
            norm_hi(11, tb)
            square(14)
            norm_hi(12, tb)
            square(15)

            def silu(c, m_i):
                act.wait_ge(gu_mm, 4 * c + m_i + 1)
                if not (isinstance(c, int) and 4 * c + m_i < 2):
                    act.wait_ge(h_done, 4 * c + m_i - 1)
                A(sg[:, m_i % 2, :], bank[(2, 4)[m_i % 2]][:, :], ACT.Silu).then_inc(silu_done, 1)

            def h_split(c, m_i):
                act.wait_ge(h_done, 4 * c + m_i + 1)
                if not (isinstance(c, int) and c == 0):
                    act.wait_ge(o_mm, 8 + 8 * c - 4 + 4 * (m_i // 2))
                k, n = m_i % 2, m_i // 2
                A(h_hi[:, k, n * NTOK:(n + 1) * NTOK], hb[:, m_i % 2, :], ACT.Copy).then_inc(hhi_done, 1)

            def ctx_split(i):
                act.wait_ge(ld_ctx[i % 2], 16 * (i // 2 + 1))
                if i == 0:
                    act.wait_ge(o_mm, 8)
                    act.wait_ge(n_x, 16)
                A(ctx_hi[:, i // 2, i % 2 * 512:(i % 2 + 1) * 512],
                  raw_b[:, 1024 + i % 2 * 512:1536 + i % 2 * 512], ACT.Copy).then_inc(cx_h, 1)

            def mlp_step(c):
                first, last = (isinstance(c, int) and c == x for x in (0, MLP_IT - 1))
                for m_i in range(4):
                    silu(c, m_i)
                    h_split(c, m_i)
                    if m_i == 0:
                        dn_hi(c, 0)
                        dn_hi(c, 1)
                    if first:
                        if m_i == 0:
                            norm_hi(13, tb)
                            norm_hi(14, tb)
                        if m_i == 1:
                            norm_hi(15, tb)
                        ctx_split(2 * m_i)
                        ctx_split(2 * m_i + 1)
                    if last and m_i == 1:
                        wq_hi(0, 0)
                        wq_hi(0, 1)
                        wkv_hi(0, 0)
                        wkv_hi(0, 1)
                if not last:
                    for i in range(4):
                        gu_hi(c + 1, i)

            def wkv_hi(g, i):
                act.wait_ge(ld_kv, 16 * g + 16)
                if isinstance(g, int) and g == 0:
                    act.wait_ge(o_mm, 8)
                else:
                    act.wait_ge(kv_mm, 8 * g)
                A(w_hi[:, WKV_COL + i * 512:WKV_COL + (i + 1) * 512], raw_b[:, i * 512:(i + 1) * 512],
                  ACT.Copy).then_inc(wkv_h, 1)

            def wq_hi(g, h):
                act.wait_ge(ld_q, 16 * g + 16)
                if isinstance(g, int) and g == 0:
                    act.wait_ge(*((o_mm, 8) if h < 2 else (gu_mm, 4 * MLP_IT)))
                else:
                    act.wait_ge(q_mm, 8 * g - 4 + h + 1)
                A(w_hi[:, WQ_COL[h]:WQ_COL[h] + 512], raw_a[:, h * 512:(h + 1) * 512],
                  ACT.Copy).then_inc(wq_h, 1)

            def wo_hi(g, h):
                act.wait_ge(ld_o, 16 * g + 16)
                if isinstance(g, int) and g == 0:
                    act.wait_ge(o_mm, 8 + 8 * MLP_IT)
                else:
                    act.wait_ge(d_mm, 8 * g)
                A(w_hi[:, WO_COL[h]:WO_COL[h] + 512], raw_b[:, h * 512:(h + 1) * 512], ACT.Copy)\
                    .then_inc(wo_h, 1)

            mlp_step(0)
            with act.Fori(1, MLP_IT - 1) as c:
                mlp_step(c)
            mlp_step(MLP_IT - 1)

            def q_evac(g, n, h):
                i = 8 * g + 4 * n + h
                act.wait_ge(q_mm, i + 1)
                if not (isinstance(g, int) and 8 * g + 4 * n < 8):
                    act.wait_ge(s_mm, 8 * g + 4 * n - 3)
                A(q_t[:, n, h, :], bank[(5 * n + h) % 2][:, :], ACT.Copy).then_inc(q_ev, 1)
                if not (isinstance(g, int) and i == 0):
                    act.wait_ge(ss_mm, i)
                A(qsq[:, :], bank[(5 * n + h) % 2][:, :], ACT.Square).then_inc(qsq_done, 1)

            def kv_evac(g, n, j):
                i = 8 * g + 4 * n + j
                act.wait_ge(kv_mm, i + 1)
                if not (isinstance(g, int) and i == 0):
                    act.wait_ge(ksq_done, i)
                if j == 0 and not (isinstance(g, int) and 2 * g + n == 0):
                    act.wait_ge(kvar_done, 2 * g + n)
                A(junk[:, 0:HD], bank[2][:, 0:HD], ACT.Square, accum_out=kv[:, 0, j:j + 1])\
                    .then_inc(ksq_done, 1)
                if not (isinstance(g, int) and 8 * g + 4 * n < 8):
                    act.wait_ge(pv_mm, 8 * g + 4 * n - 4 + max(0, j - 1))
                A(v_hi[:, n, j, :], bank[2][:, HD:2 * HD], ACT.Copy).then_inc(vhi_done, 1)

            def kt_evac(g, n):
                u = 2 * g + n
                act.wait_ge(kt_mm, u + 1)
                if isinstance(g, int) and u == 0:
                    act.wait_ge(setup_p, 1)
                if not (isinstance(g, int) and u < 2):
                    act.wait_ge(s_mm, 8 * g + 4 * n - 3)
                A(k_t[:, n, :], bank[(5 * n + 4) % 2][:, :], ACT.Copy, scale=qk_w[:, 0:1]).then_inc(kt_ev, 1)

            def softmax_exp(g, jj):
                t_i = 8 * g + jj
                act.wait_ge(max_done, t_i + 1)
                for h in range(GH):
                    t = A(pb[:, jj % 2, h, :], pb[:, jj % 2, h, :], ACT.Exp, bias=nmax[:, jj % 2, h:h + 1],
                          accum_out=psum_[:, jj % 2, h:h + 1])
                t.then_inc(p_exp, 1)

            def pt_evac(g, jj):
                act.wait_ge(pt_mm, 8 * g + jj + 1)
                if not (isinstance(g, int) and 8 * g + jj == 0):
                    act.wait_ge(pv_mm, 8 * g + jj)
                A(pt_hi[:, :], bank[4][:, :], ACT.Copy).then_inc(pthi_done, 1)

            def ot_evac(g, jj):
                act.wait_ge(pv_mm, 8 * g + jj + 1)
                if not (isinstance(g, int) and 8 * g + jj == 0):
                    act.wait_ge(d_mm, 8 * g + jj)
                A(ot_hi[:, :], bank[5][:, :], ACT.Copy).then_inc(othi_done, 1)

            def slot(g, jj, produce, refill=True):
                n, j = jj // HALF, jj % HALF
                pg, pn = (g, 1) if n == 0 else (g + 1, 0)
                if produce and j == 0:
                    kv_evac(pg, pn, 0)
                if j == 0:
                    softmax_exp(g, jj)
                if produce:
                    q_evac(pg, pn, j)
                    if j == 3:
                        kt_evac(pg, pn)
                if produce and j < 3:
                    kv_evac(pg, pn, j + 1)
                pt_evac(g, jj)
                if j < 3:
                    softmax_exp(g, jj + 1)
                if refill and jj in WQ_SLOT:
                    wq_hi(g + 1, WQ_SLOT.index(jj))
                if jj == 0 and not (isinstance(g, int) and g == 0):
                    for h in range(GH):
                        wo_hi(g, h)
                if refill and jj == 2:
                    wkv_hi(g + 1, 0)
                    wkv_hi(g + 1, 1)
                ot_evac(g, jj)

            def res_copy(i):
                act.wait_ge(n_x, i + 1)
                A(res[:, i - 16, :], xn[:, i % 2, :], ACT.Copy).then_inc(res_x, 1)

            for i in range(16, 21):
                res_copy(i)
                norm_hi(i, tb)
                if i == 17:
                    wq_hi(0, 2)
                    wq_hi(0, 3)
            for j in range(HALF):
                kv_evac(0, 0, j)
                if j < 3:
                    res_copy(21 + j)
                    norm_hi(21 + j, tb)
            for h in range(GH):
                q_evac(0, 0, h)
                wo_hi(0, h)
            kt_evac(0, 0)
            slot(0, 0, True)
            with act.Fori(0, GROUPS - 1) as g:
                for jj in range(1, 8):
                    slot(g, jj, True)
                slot(g + 1, 0, True, refill=False)

            def x2_evac(b):
                act.wait_ge(n_t, 25 + b)
                if b >= 2:
                    act.wait_ge(ra_mm, b - 1)
                A(x2t[:, b % 2, :, :], tb[b % 2][:, :].rearrange("p (k n) -> p k n", k=KT), ACT.Copy)\
                    .then_inc(f_x2t, 1)

            def gate_exp(i):
                act.wait_ge(lg_done, i + 1)
                A(ge[:, 4 * i:4 * i + 4, :], ge[:, 4 * i:4 * i + 4, :], ACT.Exp).then_inc(f_exp, 1)

            def mt_evac(i):
                act.wait_ge(mt_mm, i + 1)
                A(midt[:, 4 * i:4 * i + 4, :], bank[(2, 7)[i]][0:NE * RANK, :].rearrange("p (b n) -> p b n", b=4),
                  ACT.Copy).then_inc(mt_ev, 1)

            last = GROUPS - 1
            for jj in range(1, 4):
                slot(last, jj, True, refill=False)
            slot(last, 4, False, refill=False)
            x2_evac(0)
            x2_evac(1)
            slot(last, 5, False, refill=False)
            x2_evac(2)
            x2_evac(3)
            slot(last, 6, False, refill=False)
            x2_evac(4)
            slot(last, 7, False, refill=False)
            x2_evac(5)
            gate_exp(0)
            mt_evac(0)
            x2_evac(6)
            x2_evac(7)
            gate_exp(1)
            mt_evac(1)

        @block.gpsimd
        def _(pool):
            TT = nc.gpsimd.tensor_tensor

            def lo(dst, src, hi, done):
                TT(dst, src, f32(hi), ALU.subtract).then_inc(done, 1)

            def rsqrt(i):
                pool.wait_ge(n_var, i + 1)
                TT(rstd[:, i:i + 1], var[:, i:i + 1], pow_m[:, 0:1], ALU.pow).then_inc(n_rstd, 1)

            def win_rest(p):
                pool.wait_ge(win_h, p + 1)
                s = slice(p * 512, (p + 1) * 512)
                lo(w_lo[:, s], mamba_raw(p), w_hi[:, s], win_l)

            pool.wait_ge(setup_v, 2)
            nq = NCONV * DCONV + NCONV
            for i in range(4):
                rsqrt(i)
                if i == 1:
                    win_rest(0)
            win_rest(1)
            pool.wait_ge(setup_v, 4)
            pool.wait_ge(ld_small[0], 16)
            TT(diag_d[:, :, :], d2[:, :].unsqueeze(2).to_broadcast([P, NH, L]),
               ident.unsqueeze(1).to_broadcast([P, NH, L]), ALU.mult).then_inc(diag_done, 1)
            TT(qk_w[:, :], chan_sb[:, nq:nq + 1], chan_sb[:, nq + 1:nq + 2], ALU.mult).then_inc(setup_p, 1)
            for p in range(2, 6):
                win_rest(p)

            def decay_in(b):
                pool.wait_ge(dt_done, b // HALF + 1)
                if b >= 2:
                    pool.wait_ge(em_done, b - 1)
                    pool.wait_ge(cum_mm, b - 1)
                TT(md[:, b % 2, :, :], dt_sb[:, b * NH:(b + 1) * NH].unsqueeze(2).to_broadcast([P, NH, L]),
                   tri_half.unsqueeze(1).to_broadcast([P, NH, L]), ALU.mult).then_inc(md_done, 1)

            def decay_out(b):
                pool.wait_ge(exp_done, b + 1)
                TT(em[:, b % 2, :, :], em[:, b % 2, :, :], md[:, b % 2, :, :], ALU.mult).then_inc(em_done, 1)

            def y_rest(b):
                pool.wait_ge(yhi_done, b + 1)
                lo(y_lo[:, b % 4, :, :], yb[:, b % 2, :, :], y_hi[:, b % 4, :, :], ylo_done)

            for i in range(4, 8):
                rsqrt(i)
                win_rest(i + 2)
            decay_in(0)
            decay_in(1)

            def wout_rest(k):
                pool.wait_ge(wout_h, k + 1)
                s = slice(OUT_COL + k * 512, OUT_COL + (k + 1) * 512)
                lo(w_lo[:, s], raw_b[:, k * 512:(k + 1) * 512], w_hi[:, s], wout_l)

            for b in range(4):
                decay_out(b)
                decay_in(b + 2)
                if b:
                    y_rest(b - 1)
            wout_rest(0)
            wout_rest(1)
            y_rest(3)
            wout_rest(2)
            wout_rest(3)

            def gu_rest(c, i):
                pool.wait_ge(gu_h, 4 * c + i + 1)
                s = slice(GU_COL + i * 512, GU_COL + (i + 1) * 512)
                lo(w_lo[:, s], raw_a[:, i * 512:(i + 1) * 512], w_hi[:, s], gu_l)

            def dn_rest(c, i):
                pool.wait_ge(dn_h, 2 * c + i + 1)
                s = slice(DN_COL + i * 512, DN_COL + (i + 1) * 512)
                lo(w_lo[:, s], raw_b[:, i * 512:(i + 1) * 512], w_hi[:, s], dn_l)

            decay_out(4)
            decay_in(6)
            rsqrt(8)
            y_rest(4)
            decay_out(5)
            decay_in(7)
            rsqrt(9)
            rsqrt(10)
            y_rest(5)
            decay_out(6)
            gu_rest(0, 0)
            rsqrt(11)
            y_rest(6)
            decay_out(7)
            gu_rest(0, 1)
            rsqrt(12)
            gu_rest(0, 2)
            y_rest(7)
            gu_rest(0, 3)
            for i in range(13, 16):
                rsqrt(i)

            def add_x(b):
                pool.wait_ge(ld_xre[b % 2], 16 * (b // 2 + 1))
                pool.wait_ge(n_x, 9 + b)
                TT(res[:, b, :], res[:, b, :], xre[:, b % 2, :], ALU.add).then_inc(x_add, 1)

            def mlp_step(c):
                first, last = (isinstance(c, int) and c == x for x in (0, MLP_IT - 1))
                for m_i in range(4):
                    k, n = m_i % 2, m_i // 2
                    pool.wait_ge(hhi_done, 4 * c + m_i + 1)
                    tok = slice(n * NTOK, (n + 1) * NTOK)
                    lo(h_lo[:, k, tok], hb[:, m_i % 2, :], h_hi[:, k, tok], hlo_done)
                    if m_i == 0:
                        dn_rest(c, 0)
                        dn_rest(c, 1)
                    if first and m_i:
                        for b in ((), (0, 1), (2, 3, 4), (5, 6, 7))[m_i]:
                            add_x(b)
                    if last and m_i == 1:
                        wq_rest(0, 0)
                        wq_rest(0, 1)
                        wkv_rest(0, 0)
                        wkv_rest(0, 1)
                if not last:
                    for i in range(4):
                        gu_rest(c + 1, i)

            def wkv_rest(g, i):
                pool.wait_ge(wkv_h, 2 * g + i + 1)
                s = slice(WKV_COL + i * 512, WKV_COL + (i + 1) * 512)
                lo(w_lo[:, s], raw_b[:, i * 512:(i + 1) * 512], w_hi[:, s], wkv_l)

            def wq_rest(g, h):
                pool.wait_ge(wq_h, 4 * g + h + 1)
                s = slice(WQ_COL[h], WQ_COL[h] + 512)
                lo(w_lo[:, s], raw_a[:, h * 512:(h + 1) * 512], w_hi[:, s], wq_l)

            def wo_rest(g, h):
                pool.wait_ge(wo_h, 4 * g + h + 1)
                s = slice(WO_COL[h], WO_COL[h] + 512)
                lo(w_lo[:, s], raw_b[:, h * 512:(h + 1) * 512], w_hi[:, s], wo_l)

            mlp_step(0)
            with pool.Fori(1, MLP_IT - 1) as c:
                mlp_step(c)
            mlp_step(MLP_IT - 1)

            def q_rsqrt(g, n, h):
                i = 8 * g + 4 * n + h
                pool.wait_ge(qv_done, i + 1)
                if not (isinstance(g, int) and 8 * g + 4 * n < 8):
                    pool.wait_ge(s_done, 8 * g + 4 * n - 3)
                TT(qr[:, 4 * n + h, :], qv[:, 4 * n + h, :], pow_m[:, 0:HALF], ALU.pow).then_inc(qr_done, 1)

            def k_rsqrt(g, n):
                pool.wait_ge(kvar_done, 2 * g + n + 1)
                if not (isinstance(g, int) and 2 * g + n == 0):
                    pool.wait_ge(kn_done, 2 * g + n)
                TT(kv[:, 2, :], kv[:, 1, :], pow_m[:, 0:HALF], ALU.pow).then_inc(kr_done, 1)

            def p_scale(g, jj):
                pool.wait_ge(p_rec, 8 * g + jj + 1)
                TT(pb[:, jj % 2, :, :], pb[:, jj % 2, :, :],
                   prec[:, jj % 2, :].unsqueeze(2).to_broadcast([P, GH, L]), ALU.mult).then_inc(p_norm, 1)

            def slot(g, jj, produce, refill=True):
                n, j = jj // HALF, jj % HALF
                pg, pn = (g, 1) if n == 0 else (g + 1, 0)
                if j == 0:
                    p_scale(g, jj)
                if produce and j == 2:
                    k_rsqrt(pg, pn)
                if j < 3:
                    p_scale(g, jj + 1)
                if produce:
                    q_rsqrt(pg, pn, j)
                if refill and jj in WQ_SLOT:
                    wq_rest(g + 1, WQ_SLOT.index(jj))
                if jj == 0 and not (isinstance(g, int) and g == 0):
                    for h in range(GH):
                        wo_rest(g, h)
                if refill and jj == 2:
                    wkv_rest(g + 1, 0)
                    wkv_rest(g + 1, 1)

            for i in range(16, 24):
                rsqrt(i)
                if i in (17, 18):
                    wq_rest(0, i - 15)
            k_rsqrt(0, 0)
            for h in range(GH):
                q_rsqrt(0, 0, h)
                wo_rest(0, h)
            slot(0, 0, True)
            with pool.Fori(0, GROUPS - 1) as g:
                for jj in range(1, 8):
                    slot(g, jj, True)
                slot(g + 1, 0, True, refill=False)
            for jj in range(1, 8):
                slot(GROUPS - 1, jj, jj < 4, refill=False)
                rsqrt(23 + jj)
            for i in range(31, 40):
                rsqrt(i)

        @block.vector
        def _(dve):
            V = nc.vector
            TT, STT, TS = V.tensor_tensor, V.scalar_tensor_tensor, V.tensor_scalar
            count = [0]

            def link(ins):
                count[0] += 1
                ins.then_inc(vch, 1)
                dve.wait_ge(vch, count[0])

            def lo(dst, src, hi, done):
                TT(dst, src, f32(hi), ALU.subtract).then_inc(done, 1)

            def rms_var(i):
                dve.wait_ge(n_ssq, i + 1)
                TS(var[:, i:i + 1], stat[:, i:i + 1], 1.0 / DM, EPS, ALU.mult, ALU.add).then_inc(n_var, 1)

            def rms_x(i):
                dve.wait_ge(n_rstd, i + 1)
                if i == 0:
                    dve.wait_ge(ld_small[1], 16)
                if i >= 2:
                    dve.wait_ge(n_t, i - 1)
                STT(xn[:, i % 2, :], res[:, i % 8, :], rstd[:, i:i + 1],
                    row_sb[:, i // 8 * DM:(i // 8 + 1) * DM], ALU.mult, ALU.mult).then_inc(n_x, 1)

            def norm_lo(i, banks):
                dve.wait_ge(n_hi, i + 1)
                b = i % 8
                lo(act_lo[:, :, b * L:(b + 1) * L], banks[i % 2][:, :].rearrange("p (k n) -> p k n", k=KT),
                   act_hi[:, :, b * L:(b + 1) * L], n_lo)

            nb = (bank[2], bank[3])
            V.memset(ones[:, :], 1.0)
            V.memset(pre[:, :, :, :], 0.0).then_inc(setup_v, 1)
            V.memset(pow_m[:, :], -0.5).then_inc(setup_v, 1)
            rms_var(0)
            rms_var(1)
            rms_x(0)
            rms_x(1)
            norm_lo(0, nb)
            rms_var(2)
            rms_x(2)
            norm_lo(1, nb)
            dve.wait_ge(dt_w, 1)
            TT(wdt_lo[:, :], wdt_raw[:, :], f32(wdt_hi[:, :]), ALU.subtract).then_inc(dt_w, 1)
            rms_var(3)
            rms_x(3)
            norm_lo(2, nb)
            dve.wait_ge(ld_small[2], 16)
            TS(cw[:, :], chan_sb[:, 0:NCONV * DCONV + NCONV], 0.5, None, ALU.mult)
            TS(d2[:, :], row_sb[:, 2 * DM + NH:2 * DM + 2 * NH], 0.5, None, ALU.mult).then_inc(setup_v, 1)
            norm_lo(3, nb)
            dve.wait_ge(setup_a, 1)
            TS(a2[:, :], a2[:, :], -2.0, None, ALU.mult)
            V.tensor_copy(sp[:, 6, 0:NH], row_sb[:, 2 * DM + 2 * NH:2 * DM + 3 * NH]).then_inc(setup_v, 1)

            def conv(q):
                p = q % NCONV
                dve.wait_ge(conv_ev, q + 1)
                c = cbuf[:, q % 3, :].rearrange("p (s n) -> p s n", s=HALF)
                for k in (2, 1, 0):
                    t = STT(c, pre[:, q % 2, :, k:k + L], cw[:, p * DCONV + k:p * DCONV + k + 1], c,
                            ALU.mult, ALU.add)
                    if k:
                        link(t)
                    else:
                        t.then_inc(conv_c, 1)

            def conv_silu(q):
                dve.wait_ge(conv_th, q + 1)
                STT(xbc[:, q // NCONV, q % NCONV, :], th[:, 1 + q % 2, :], 1.0, cbuf[:, q % 3, :],
                    ALU.add, ALU.mult).then_inc(conv_out, 1)

            def z_silu(i):
                n, h = i // NH, i % NH
                f = NPIECE * n + NCONV + h
                dve.wait_ge(z_th, i + 1)
                STT(zt[:, h, n * NTOK:(n + 1) * NTOK], th[:, 0, :], 1.0, bank[f % 2][:, :], ALU.add, ALU.mult)\
                    .then_inc(z_out, 1)

            def dt_in(n):
                dve.wait_ge(dt_t, n + 1)
                bias = sp[:, 6, 0:NH].unsqueeze(1).to_broadcast([P, HALF, NH])
                link(TT(sp[:, 0, :].rearrange("p (b h) -> p b h", h=NH),
                        bank[7][:, 0:HALF * NH].rearrange("p (b h) -> p b h", h=NH), bias, ALU.add))
                link(TS(sp[:, 1, :], sp[:, 0, :], 0.0, None, ALU.min))
                link(TS(sp[:, 0, :], sp[:, 0, :], 0.0, None, ALU.max))
                link(TT(sp[:, 3, :], sp[:, 1, :], sp[:, 0, :], ALU.subtract))
                V.tensor_copy(sp[:, 1, :], sp[:, 3, :]).then_inc(dt_a, 1)

            def dt_out(n):
                dve.wait_ge(dt_exp_done, n + 1)
                link(TS(sp[:, 3, :], sp[:, 2, :], 2.0, None, ALU.add))
                link(V.reciprocal(sp[:, 4, :], sp[:, 3, :]))
                link(TT(sp[:, 3, :], sp[:, 2, :], sp[:, 4, :], ALU.mult))
                link(TT(sp[:, 4, :], sp[:, 3, :], sp[:, 3, :], ALU.mult))
                link(TS(sp[:, 5, :], sp[:, 4, :], 2.0 / (2 * ATANH_TERMS + 1), None, ALU.mult))
                for k in range(ATANH_TERMS - 1, 0, -1):
                    link(STT(sp[:, 5, :], sp[:, 5, :], 2.0 / (2 * k + 1), sp[:, 4, :], ALU.add, ALU.mult))
                link(STT(sp[:, 5, :], sp[:, 5, :], 2.0, sp[:, 3, :], ALU.add, ALU.mult))
                TT(dt_sb[:, n * HALF * NH:(n + 1) * HALF * NH], sp[:, 5, :], sp[:, 0, :], ALU.add)\
                    .then_inc(dt_done, 1)

            def att_mul(b):
                dve.wait_ge(em_done, b + 1)
                dve.wait_ge(sc_mm, b + 1)
                if b:
                    dve.wait_ge(y_mm, b)
                else:
                    dve.wait_ge(diag_done, 1)
                link(TT(att[:, :, :], em[:, b % 2, :, :], bank[3][:, :].rearrange("p (h n) -> p h n", h=NH),
                        ALU.mult))
                TT(att[:, :, :], att[:, :, :], diag_d[:, :, :], ALU.add).then_inc(att_done, 1)

            def y_out(b):
                dve.wait_ge(y_mm, b + 1)
                if b >= 2:
                    dve.wait_ge(ylo_done, b - 1)
                dve.wait_ge(z_out, NH * (b // HALF) + NH)
                TT(yb[:, b % 2, :, :], zt[:, :, b * L:(b + 1) * L],
                   bank[4][:, :].rearrange("p (h n) -> p h n", h=NH), ALU.mult).then_inc(y1_done, 1)

            def add_res(i, b):
                dve.wait_ge(o_mm, i + 1)
                TT(res[:, b, :], res[:, b, :], bank[6 + b % 2][:, :], ALU.add).then_inc(o_add, 1)

            tb = (bank[0], bank[1])
            conv(0)
            conv(1)
            conv_silu(0)
            dt_in(0)
            rms_var(4)
            conv(2)
            conv_silu(1)
            rms_x(4)
            rms_var(5)
            dt_out(0)
            conv(3)
            conv_silu(2)
            rms_x(5)
            rms_var(6)
            conv(4)
            conv_silu(3)
            rms_var(7)
            norm_lo(4, nb)
            rms_x(6)
            norm_lo(5, nb)
            rms_x(7)
            norm_lo(6, nb)
            conv(5)
            conv_silu(4)
            norm_lo(7, nb)
            conv_silu(5)
            for i in range(4):
                z_silu(i)
            conv(6)
            dt_in(1)
            conv(7)
            conv_silu(6)
            dt_out(1)
            att_mul(0)
            conv(8)
            conv_silu(7)
            y_out(0)
            att_mul(1)
            conv(9)
            conv_silu(8)
            y_out(1)
            att_mul(2)
            conv(10)
            conv_silu(9)
            y_out(2)
            att_mul(3)
            conv(11)
            conv_silu(10)
            y_out(3)
            z_silu(4)
            conv_silu(11)
            z_silu(5)
            add_res(0, 0)
            rms_var(8)
            att_mul(4)
            add_res(1, 1)
            rms_x(8)
            z_silu(6)
            z_silu(7)
            y_out(4)
            att_mul(5)
            rms_var(9)
            add_res(2, 2)
            rms_x(9)
            rms_var(10)
            y_out(5)
            add_res(3, 3)
            att_mul(6)
            rms_var(11)
            norm_lo(8, tb)
            rms_x(10)
            y_out(6)
            norm_lo(9, tb)
            rms_x(11)
            att_mul(7)
            add_res(4, 4)
            rms_var(12)
            norm_lo(10, tb)
            y_out(7)
            rms_x(12)
            add_res(5, 5)
            rms_var(13)
            norm_lo(11, tb)
            add_res(6, 6)
            rms_x(13)
            rms_var(14)
            norm_lo(12, tb)
            add_res(7, 7)
            rms_x(14)
            rms_var(15)

            def ln_stats(i):
                b = i % 8
                if i >= 18:
                    dve.wait_ge(n_mv, i - 17)
                V.bn_stats(bst[:, i % 2, :], res[:, b, :]).then_inc(n_bn, 1)
                dve.wait_ge(n_bn, i - 15)
                V.bn_aggr(mv[:, i, :], bst[:, i % 2, :]).then_inc(n_mv, 1)
                dve.wait_ge(n_mv, i - 15)
                TS(var[:, i:i + 1], mv[:, i, 1:2], EPS, None, ALU.add).then_inc(n_var, 1)

            def ln_x(i):
                b = i % 8
                dve.wait_ge(n_rstd, i + 1)
                dve.wait_ge(n_t, i - 1)
                TS(xn[:, i % 2, :], res[:, b, :], mv[:, i, 0:1], rstd[:, i:i + 1], ALU.subtract, ALU.mult)\
                    .then_inc(n_x, 1)

            def ctx_rest(i):
                dve.wait_ge(cx_h, i + 1)
                cs = slice(i % 2 * 512, (i % 2 + 1) * 512)
                lo(ctx_lo[:, i // 2, cs], raw_b[:, 1024 + i % 2 * 512:1536 + i % 2 * 512],
                   ctx_hi[:, i // 2, cs], cx_l)

            def mlp_step(c):
                first, last = (isinstance(c, int) and c == x for x in (0, MLP_IT - 1))
                for m_i in range(4):
                    dve.wait_ge(silu_done, 4 * c + m_i + 1)
                    dve.wait_ge(gu_mm, 4 * c + m_i + 1)
                    if not (isinstance(c, int) and 4 * c + m_i < 2):
                        dve.wait_ge(hlo_done, 4 * c + m_i - 1)
                    TT(hb[:, m_i % 2, :], sg[:, m_i % 2, :], bank[(3, 5)[m_i % 2]][:, :], ALU.mult)\
                        .then_inc(h_done, 1)
                    if first:
                        if m_i == 0:
                            norm_lo(13, tb)
                            rms_x(15)
                            norm_lo(14, tb)
                        if m_i == 1:
                            norm_lo(15, tb)
                        ctx_rest(2 * m_i)
                        ctx_rest(2 * m_i + 1)
                for b in range(B):
                    if first:
                        dve.wait_ge(x_add, b + 1)
                    add_res(8 + 8 * c + b, b)
                    if last:
                        dve.wait_ge(o_add, 9 + 8 * c + b)
                        ln_stats(16 + b)
                        if b >= 1:
                            ln_x(15 + b)
                        if b >= 2:
                            norm_lo(14 + b, tb)

            mlp_step(0)
            with dve.Fori(1, MLP_IT - 1) as c:
                mlp_step(c)
            mlp_step(MLP_IT - 1)

            def v_rest(g, n, j):
                i = 8 * g + 4 * n + j
                dve.wait_ge(vhi_done, i + 1)
                lo(v_lo[:, n, j, :], bank[2][:, HD:2 * HD], v_hi[:, n, j, :], vlo_done)
                if j == 0 and not (isinstance(g, int) and 2 * g + n == 0):
                    dve.wait_ge(kt_mm, 2 * g + n)
                V.tensor_copy(kraw[:, j, :], bank[2][:, 0:HD]).then_inc(kraw_done, 1)

            def k_var(g, n):
                u = 2 * g + n
                dve.wait_ge(ksq_done, 8 * g + 4 * n + 4)
                if not (isinstance(g, int) and u == 0):
                    dve.wait_ge(kr_done, 2 * g + n)
                TS(kv[:, 1, :], kv[:, 0, :], 1.0 / HD, EPS, ALU.mult, ALU.add).then_inc(kvar_done, 1)

            def k_norm(g, n):
                dve.wait_ge(kr_done, 2 * g + n + 1)
                dve.wait_ge(kraw_done, 8 * g + 4 * n + 4)
                TT(kraw[:, :, :], kraw[:, :, :], kv[:, 2, :].unsqueeze(2).to_broadcast([P, HALF, HD]), ALU.mult)\
                    .then_inc(kn_done, 1)

            def q_var(g, n, h):
                i = 8 * g + 4 * n + h
                dve.wait_ge(ss_mm, i + 1)
                if not (isinstance(g, int) and 8 * g + 4 * n < 8):
                    dve.wait_ge(qr_done, 8 * g + 4 * n - 3)
                TS(qv[:, 4 * n + h, :], bank[7][:, 0:HALF], HD * EPS, None, ALU.add).then_inc(qv_done, 1)

            def softmax_max(g, jj):
                n, j = jj // HALF, jj % HALF
                t_i = 8 * g + jj
                dve.wait_ge(s_mm, t_i + 1)
                dve.wait_ge(qr_done, 8 * g + 4 * n + 4)
                if not (isinstance(g, int) and t_i < 2):
                    dve.wait_ge(pt_mm, t_i - 1)
                for h in range(GH):
                    t = STT(pb[:, jj % 2, h, :], bank[3][:, h * L:(h + 1) * L], qr[:, 4 * n + h, j:j + 1],
                            mask_sb[:, :], ALU.mult, ALU.add)
                t.then_inc(s_done, 1)
                dve.wait_ge(s_done, t_i + 1)
                V.tensor_reduce(nmax[:, jj % 2, :], pb[:, jj % 2, :, :], X, ALU.max, negate=True)\
                    .then_inc(max_done, 1)

            def softmax_rec(g, jj):
                dve.wait_ge(p_exp, 8 * g + jj + 1)
                V.reciprocal(prec[:, jj % 2, :], psum_[:, jj % 2, :]).then_inc(p_rec, 1)

            def pt_rest(g, jj):
                dve.wait_ge(pthi_done, 8 * g + jj + 1)
                lo(pt_lo[:, :], bank[4][:, :], pt_hi[:, :], ptlo_done)

            def ot_rest(g, jj):
                dve.wait_ge(othi_done, 8 * g + jj + 1)
                lo(ot_lo[:, :], bank[5][:, :], ot_hi[:, :], otlo_done)

            def add_out(g, jj):
                t_i = 8 * g + jj
                dve.wait_ge(d_mm, t_i + 1)
                TT(res[:, jj, :], res[:, jj, :], bank[6][:, :], ALU.add).then_inc(d_add, 1)

            def slot(g, jj, produce, before=True):
                n, j = jj // HALF, jj % HALF
                pg, pn = (g, 1) if n == 0 else (g + 1, 0)
                if j == 0:
                    if produce:
                        v_rest(pg, pn, 0)
                    softmax_rec(g, jj)
                if j < 3:
                    softmax_max(g, jj + 1)
                    if produce:
                        v_rest(pg, pn, j + 1)
                if produce and j == 2:
                    k_var(pg, pn)
                pt_rest(g, jj)
                if j < 3:
                    softmax_rec(g, jj + 1)
                if produce and j == 2:
                    k_norm(pg, pn)
                if before:
                    add_out(*((g, jj - 1) if jj else (g - 1, 7)))
                if produce:
                    q_var(pg, pn, j)
                ot_rest(g, jj)
                if j == 3 and produce:
                    softmax_max(pg, 4 * pn)

            v_rest(0, 0, 0)
            ln_x(23)
            norm_lo(22, tb)
            v_rest(0, 0, 1)
            norm_lo(23, tb)
            v_rest(0, 0, 2)
            v_rest(0, 0, 3)
            k_var(0, 0)
            k_norm(0, 0)
            for h in range(GH):
                q_var(0, 0, h)
            dve.wait_ge(res_x, 8)
            dve.wait_ge(ld_small[4], 16)
            softmax_max(0, 0)
            slot(0, 0, True, before=False)
            with dve.Fori(0, GROUPS - 1) as g:
                for jj in range(1, 8):
                    slot(g, jj, True)
                slot(g + 1, 0, True)

            def ln2(i):
                b = i % 8
                dve.wait_ge(n_rstd, i + 1)
                TS(res[:, b, :], res[:, b, :], mv[:, i, 0:1], rstd[:, i:i + 1], ALU.subtract, ALU.mult).then_inc(n_x, 1)

            def gates_rank(i):
                tl = slice(4 * i, 4 * i + 4)
                ps = bank[(2, 7)[i]][:, 0:4 * RAC].rearrange("p (b c) -> p b c", b=4)
                dve.wait_ge(ra_mm, 4 * i + 4)
                link(V.tensor_copy(lg[:, tl, :], ps[:, :, 0:NE]))
                for b in range(4):
                    o = lg[:, 4 * i + b, :]
                    own = o.unsqueeze(2).to_broadcast([P, NE, NE])
                    other = o.unsqueeze(1).to_broadcast([P, NE, NE])
                    TT(c1[:, 4 * i + b, :, :], other, own, ALU.is_ge)
                    t = TT(c2[:, 4 * i + b, :, :], other, own, ALU.is_gt)
                link(t)
                for b in range(4):
                    TT(c1[:, 4 * i + b, :, :], c1[:, 4 * i + b, :, :], cmp_m[:, 0, :, :], ALU.mult)
                    t = TT(c2[:, 4 * i + b, :, :], c2[:, 4 * i + b, :, :], cmp_m[:, 1, :, :], ALU.mult)
                link(t)
                link(TT(c1[:, tl, :, :].rearrange("p b e f -> p (b e f)"), c1[:, tl, :, :].rearrange("p b e f -> p (b e f)"),
                        c2[:, tl, :, :].rearrange("p b e f -> p (b e f)"), ALU.add))
                V.tensor_reduce(rank_t[:, tl, :].rearrange("p b e -> p (b e)"),
                                c1[:, tl, :, :].rearrange("p b e f -> p (b e) f"), X, ALU.add)
                link(V.tensor_reduce(lmax[:, tl], lg[:, tl, :], X, ALU.max))
                TT(ge[:, tl, :], lg[:, tl, :], lmax[:, tl].unsqueeze(2).to_broadcast([P, 4, NE]), ALU.subtract)\
                    .then_inc(lg_done, 1)

            def gates_mid(i):
                tl = slice(4 * i, 4 * i + 4)
                ps = bank[(2, 7)[i]][:, 0:4 * RAC].rearrange("p (b c) -> p b c", b=4)
                dve.wait_ge(f_exp, i + 1)
                fl = ge[:, tl, :].rearrange("p b e -> p (b e)")
                link(STT(fl, rank_t[:, tl, :].rearrange("p b e -> p (b e)"), 1.5, fl, ALU.is_lt, ALU.mult))
                link(V.tensor_reduce(gsum[:, tl], ge[:, tl, :], X, ALU.add))
                link(V.reciprocal(gsum[:, tl], gsum[:, tl]))
                link(TS(gsum[:, tl], gsum[:, tl], LORA_SCALE, None, ALU.mult))
                link(TT(ge[:, tl, :], ge[:, tl, :], gsum[:, tl].unsqueeze(2).to_broadcast([P, 4, NE]), ALU.mult))
                for b in range(4):
                    t = TT(mid[:, 4 * i + b, :, :], ps[:, b, NE:].rearrange("p (e r) -> p e r", e=NE),
                           ge[:, 4 * i + b, :].unsqueeze(2).to_broadcast([P, NE, RANK]), ALU.mult)
                t.then_inc(mid_done, 1)

            def add_delta(b):
                dve.wait_ge(dl_mm, b + 1)
                TT(res[:, b, :], res[:, b, :], bank[(3, 6)[b % 2]][:, :], ALU.add).then_inc(dl_add, 1)
                dve.wait_ge(dl_add, b + 1)

            for e in range(NE):
                V.memset(cmp_m[:, 0, e, :], 0.0)
                t = V.memset(cmp_m[:, 1, e, :], 0.0)
            link(t)
            for e in range(NE):
                if e:
                    t = V.memset(cmp_m[:, 0, e, 0:e], 1.0)
                if e < NE - 1:
                    t = V.memset(cmp_m[:, 1, e, e + 1:NE], 1.0)
            link(t)

            last = GROUPS - 1
            for jj in range(1, 8):
                slot(last, jj, jj < 4)
                b = jj - 1
                dve.wait_ge(d_add, 8 * last + b + 1)
                ln_stats(24 + b)
                if b:
                    ln2(23 + b)
            add_out(last, 7)
            dve.wait_ge(d_add, 64)
            ln_stats(31)
            ln2(30)
            gates_rank(0)
            ln2(31)
            gates_mid(0)
            gates_rank(1)
            for b in range(B):
                if b == 0:
                    add_delta(0)
                    ln_stats(32)
                    gates_mid(1)
                else:
                    add_delta(b)
                    ln_stats(32 + b)
                    ln2(31 + b)
            ln2(39)


_OUT = ((B, L, DM), "float32")


def kernel(x, ctx_4096, mask_1x1xSxS2_ff0, L0_attn_w_in, L0_attn_conv_w, L0_attn_conv_b, L0_attn_A_log,
           L0_attn_D, L0_attn_dt_bias, L0_attn_w_out, L0_attn_ln1_w, L0_attn_ln2_w, L0_attn_gate_w,
           L0_attn_up_w, L0_attn_down_w, L0_xattn_Wq, L0_xattn_Wk, L0_xattn_Wv, L0_xattn_Wo,
           L0_xattn_q_norm_w, L0_xattn_k_norm_w, L0_ffn_router_w, L0_ffn_A, L0_ffn_B):
    import numpy as np
    import concourse.bacc as bacc
    from concourse.bass_utils import run_bass_kernel_spmd

    a = np.asarray

    def pieces(w, cols):
        n = w.shape[0] // cols
        return a(w).reshape(n, cols, KT, P).transpose(0, 3, 2, 1).reshape(n, P, KT * cols)

    w_in = a(L0_attn_w_in)
    cut = [0, 512, 1280, 1284]
    z, xbc, dt = (w_in[cut[i]:cut[i + 1]] for i in range(3))
    gate, up = pieces(L0_attn_gate_w, P), pieces(L0_attn_up_w, P)
    w_gu = np.stack([gate.reshape(MLP_IT, 2, P, 512), up.reshape(MLP_IT, 2, P, 512)], 2)
    w_q = pieces(L0_xattn_Wq, P).reshape(GROUPS, GH, P, 512).transpose(0, 2, 1, 3).reshape(GROUPS, P, 2048)
    wk, wv = (a(w).reshape(GROUPS, HD, KT, P).transpose(0, 3, 2, 1) for w in (L0_xattn_Wk, L0_xattn_Wv))
    w_o = a(L0_xattn_Wo).T.reshape(GROUPS, GH, HD, DM).transpose(0, 2, 1, 3).reshape(GROUPS, P, 2048)
    idx = np.arange(P)
    tri = (idx[:, None] <= idx[None, :]).astype(np.float32) * np.float32(0.5)
    strict = (idx[:, None] > idx[None, :]).astype(np.float32)
    arrays = {
        "x": a(x),
        "ctx_t": a(ctx_4096).reshape(B * L, KT, P).transpose(1, 2, 0),
        "mask": a(mask_1x1xSxS2_ff0).reshape(L, L),
        "consts": np.concatenate([np.eye(P, dtype=np.float32), tri, strict], 1),
        "chan": np.concatenate([a(L0_attn_conv_w).reshape(NCONV, P, DCONV).transpose(1, 0, 2).reshape(P, -1),
                                a(L0_attn_conv_b).reshape(NCONV, P).T,
                                a(L0_xattn_q_norm_w)[:, None], a(L0_xattn_k_norm_w)[:, None]], 1),
        "rows": np.concatenate([a(L0_attn_ln1_w), a(L0_attn_ln2_w), a(L0_attn_A_log), a(L0_attn_D),
                                a(L0_attn_dt_bias)]),
        "w_dt": dt.reshape(NH, KT, P).transpose(2, 1, 0).reshape(P, KT * NH),
        "w_in": pieces(np.concatenate([xbc, z], 0), P),
        "w_out": a(L0_attn_w_out).T.reshape(NH, P, DM).transpose(1, 0, 2).reshape(P, NH * DM),
        "w_gu": w_gu.transpose(0, 3, 1, 2, 4).reshape(MLP_IT, P, 2048),
        "w_dn": a(L0_attn_down_w).T.reshape(MLP_IT, 2, P, DM).transpose(0, 2, 1, 3).reshape(MLP_IT, P, 1024),
        "w_q": w_q,
        "w_kv": np.concatenate([wk, wv], 3).reshape(GROUPS, P, 1024),
        "w_o": w_o,
        "w_ra": np.concatenate([a(L0_ffn_router_w), a(L0_ffn_A).reshape(NE * RANK, DM)], 0)
                  .reshape(NE + NE * RANK, KT, P).transpose(2, 1, 0),
        "w_b": a(L0_ffn_B).transpose(0, 2, 1).reshape(NE * RANK, DM),
    }
    arrays = {k: np.ascontiguousarray(v) for k, v in arrays.items()}
    nc = bacc.Bacc("TRN2", target_bir_lowering=False, num_devices=1)
    args = {k: nc.dram_tensor(f"in_{k}", v.shape, mybir.dt.from_np(v.dtype), kind="ExternalInput").ap()
            for k, v in arrays.items()}
    o = nc.dram_tensor("out_0", _OUT[0], mybir.dt.float32, kind="ExternalOutput").ap()
    build_program(nc, **args, out=o)
    r = run_bass_kernel_spmd(nc, [{f"in_{k}": v for k, v in arrays.items()}], core_ids=[0])
    return r.results[0]["out_0"]
```

```python
from contextlib import ExitStack

import concourse.bass as bass
from concourse import mybir

B, L, DM = 8, 128, 512
P = 128
KT = DM // P
HALF = 4
NTOK = HALF * L
NH, DSTATE, DCONV = 4, 128, 4
NCONV = 6
NPIECE = NCONV + NH
INTER = 1792
MLP_IT = INTER // (2 * P)
GROUPS, GH, HD = 8, 4, 128
NE, RANK = 4, 16
EPS = 1e-5
LORA_SCALE = 4.0
ATANH_TERMS = 8


def build_program(nc, x, ctx_t, mask, consts, chan, rows, w_dt, w_in, w_out, w_gu, w_dn,
                  w_q, w_kv, w_o, w_ra, w_b, out):
    fp32 = mybir.dt.float32
    f32r = mybir.dt.float32r
    bf16 = mybir.dt.bfloat16
    ALU = mybir.AluOpType
    ACT = mybir.ActivationFunctionType
    X = mybir.AxisListType.X

    ctx = ExitStack()
    with ctx:
        def sb(where, name, shape, dt=fp32):
            return where.enter_context(nc.sbuf_tensor(name, shape, dt))

        def sem(name):
            return ctx.enter_context(nc.semaphore(name))

        def f32(ap):
            return ap.bitcast(fp32)

        act_hi = sb(ctx, "act_hi", [P, KT, B * L], f32r)
        act_lo = sb(ctx, "act_lo", [P, KT, B * L], f32r)
        res = sb(ctx, "res", [P, B, DM])
        w_hi = sb(ctx, "w_hi", [P, 5120], f32r)
        w_lo = sb(ctx, "w_lo", [P, 5120], f32r)
        raw_a = sb(ctx, "raw_a", [P, 2048])
        raw_b = sb(ctx, "raw_b", [P, 2048])
        cst = sb(ctx, "cst", [P, 3 * P])
        ident, tri_half, strict = cst[:, 0:P], cst[:, P:2 * P], cst[:, 2 * P:3 * P]
        chan_sb = sb(ctx, "chan_sb", [P, NCONV * DCONV + NCONV + 2])
        qk_w = sb(ctx, "qk_w", [P, 1])
        pow_m = sb(ctx, "pow_m", [P, 16])
        xn = sb(ctx, "xn", [P, 2, DM])
        junk = sb(ctx, "junk", [P, DM], bf16)
        stat = sb(ctx, "stat", [P, 32])
        var = sb(ctx, "var", [P, 48])
        rstd = sb(ctx, "rstd", [P, 48])
        bst = sb(ctx, "bst", [P, 2, 6])
        mv = sb(ctx, "mv", [P, 48, 2])

        with ExitStack() as m:
            row_sb = sb(m, "row_sb", [P, 2 * DM + 3 * NH])
            wdt_raw = sb(m, "wdt_raw", [P, KT * NH])
            wdt_hi = sb(m, "wdt_hi", [P, KT * NH], f32r)
            wdt_lo = sb(m, "wdt_lo", [P, KT * NH], f32r)
            cw = sb(m, "cw", [P, NCONV * DCONV + NCONV])
            a2 = sb(m, "a2", [P, NH])
            d2 = sb(m, "d2", [P, NH])
            dt_sb = sb(m, "dt_sb", [P, B * NH])
            sp = sb(m, "sp", [P, 7, HALF * NH])
            pre = sb(m, "pre", [P, 2, HALF, L + DCONV - 1])
            cbuf = sb(m, "cbuf", [P, 3, NTOK])
            th = sb(m, "th", [P, 3, NTOK])
            xbc = sb(m, "xbc", [P, 2, NCONV, NTOK])
            dt_row = sb(m, "dt_row", [NH, NTOK])
            diag_d = sb(m, "diag_d", [P, NH, L])
            zt = sb(m, "zt", [P, NH, B * L])
            xtok = sb(m, "xtok", [P, 2, P])
            md = sb(m, "md", [P, 2, NH, L])
            em = sb(m, "em", [P, 2, NH, L])
            att = sb(m, "att", [P, NH, L])
            yb = sb(m, "yb", [P, 2, NH, L])
            y_hi = sb(m, "y_hi", [P, 4, NH, L], f32r)
            y_lo = sb(m, "y_lo", [P, 4, NH, L], f32r)

        ctx_hi = sb(ctx, "ctx_hi", [P, KT, B * L], f32r)
        ctx_lo = sb(ctx, "ctx_lo", [P, KT, B * L], f32r)
        with ExitStack() as m:
            h_hi = sb(m, "h_hi", [P, 2, B * L], f32r)
            h_lo = sb(m, "h_lo", [P, 2, B * L], f32r)
            sg = sb(m, "sg", [P, 2, NTOK])
            hb = sb(m, "hb", [P, 2, NTOK])
            xre = sb(m, "xre", [P, B, DM])

        with ExitStack() as m:
            q_t = sb(m, "q_t", [P, 2, GH, NTOK])
            pt_hi = sb(m, "pt_hi", [P, GH * L], f32r)
            pt_lo = sb(m, "pt_lo", [P, GH * L], f32r)
            ot_hi = sb(m, "ot_hi", [P, GH * L], f32r)
            ot_lo = sb(m, "ot_lo", [P, GH * L], f32r)
            v_hi = sb(m, "v_hi", [P, 2, HALF, HD], f32r)
            v_lo = sb(m, "v_lo", [P, 2, HALF, HD], f32r)
            kraw = sb(m, "kraw", [P, HALF, HD])
            kv = sb(m, "kv", [P, 3, HALF])
            k_t = sb(m, "k_t", [P, 2, NTOK])
            pb = sb(m, "pb", [P, 2, GH, L])
            mask_sb = sb(m, "mask_sb", [P, L])
            qjunk = sb(m, "qjunk", [P, NTOK], bf16)
            qss = sb(m, "qss", [P, 2, HALF])
            qv = sb(m, "qv", [P, 2 * GH, HALF])
            qr = sb(m, "qr", [P, 2 * GH, HALF])
            nmax = sb(m, "nmax", [P, 2, GH])
            psum_ = sb(m, "psum_", [P, 2, GH])
            prec = sb(m, "prec", [P, 2, GH])

            x2t = sb(m, "x2t", [P, 2, KT, P])
            ra_sb = sb(m, "ra_sb", [P, KT, NE + NE * RANK])
            bl_sb = sb(m, "bl_sb", [NE * RANK, DM])
            cmp_m = sb(m, "cmp_m", [P, 2, NE, NE])
            lg = sb(m, "lg", [P, B, NE])
            c1 = sb(m, "c1", [P, B, NE, NE])
            c2 = sb(m, "c2", [P, B, NE, NE])
            rank_t = sb(m, "rank_t", [P, B, NE])
            lmax = sb(m, "lmax", [P, B])
            ge = sb(m, "ge", [P, B, NE])
            gsum = sb(m, "gsum", [P, B])
            mid = sb(m, "mid", [P, B, NE, RANK])
            midt = sb(m, "midt", [NE * RANK, B, P])
            mr = sb(m, "mr", [P, B])

        bank = [ctx.enter_context(nc.psum_tensor(f"bank{i}", [P, 512], fp32)) for i in range(8)]

        ld_x = [sem(f"ld_x{b}") for b in range(B)]
        ld_small = [sem(f"ld_small{i}") for i in range(7)]
        ld_win = [sem(f"ld_win{i}") for i in range(8)]
        ld_wout = sem("ld_wout")
        ld_gu = sem("ld_gu")
        ld_dn = sem("ld_dn")
        ld_ctx = [sem("ld_ctx0"), sem("ld_ctx1")]
        ld_xre = [sem("ld_xre0"), sem("ld_xre1")]
        ld_q = sem("ld_q")
        ld_kv = sem("ld_kv")
        ld_o = sem("ld_o")
        ld_lora = [sem("ld_lora0"), sem("ld_lora1")]
        st_out = sem("st_out")

        n_ssq, n_var, n_rstd, n_x = sem("n_ssq"), sem("n_var"), sem("n_rstd"), sem("n_x")
        n_t, n_hi, n_lo, n_bn, n_mv = sem("n_t"), sem("n_hi"), sem("n_lo"), sem("n_bn"), sem("n_mv")
        res_x, vlo_done = sem("res_x"), sem("vlo_done")
        x_add = sem("x_add")

        dt_w = sem("dt_w")
        win_h, win_l = sem("win_h"), sem("win_l")
        wout_h, wout_l = sem("wout_h"), sem("wout_l")
        gu_h, gu_l = sem("gu_h"), sem("gu_l")
        dn_h, dn_l = sem("dn_h"), sem("dn_l")
        cx_h, cx_l = sem("cx_h"), sem("cx_l")
        wq_h, wq_l = sem("wq_h"), sem("wq_l")
        wkv_h, wkv_l = sem("wkv_h"), sem("wkv_l")
        wo_h, wo_l = sem("wo_h"), sem("wo_l")

        setup_v, setup_a, setup_p = sem("setup_v"), sem("setup_a"), sem("setup_p")
        in_mm, conv_ev, conv_c, conv_th, conv_out = (sem("in_mm"), sem("conv_ev"), sem("conv_c"),
                                                     sem("conv_th"), sem("conv_out"))
        z_th, z_out = sem("z_th"), sem("z_out")
        dt_mm, dt_ev, dt_t = sem("dt_mm"), sem("dt_ev"), sem("dt_t")
        dt_a, dt_exp_done, dt_done, diag_done = sem("dt_a"), sem("dt_exp_done"), sem("dt_done"), sem("diag_done")
        md_done, xt_mm, xt_ev, cum_mm, exp_done = (sem("md_done"), sem("xt_mm"), sem("xt_ev"),
                                                   sem("cum_mm"), sem("exp_done"))
        em_done, sc_mm, att_done, y_mm, y1_done = (sem("em_done"), sem("sc_mm"), sem("att_done"),
                                                   sem("y_mm"), sem("y1_done"))
        yhi_done, ylo_done = sem("yhi_done"), sem("ylo_done")
        o_mm, o_add = sem("o_mm"), sem("o_add")
        vch = sem("vch")
        gu_mm, silu_done, h_done, hhi_done, hlo_done = (sem("gu_mm"), sem("silu_done"), sem("h_done"),
                                                        sem("hhi_done"), sem("hlo_done"))
        q_mm, q_ev, qsq_done = sem("q_mm"), sem("q_ev"), sem("qsq_done")
        qt_mm, qv_done, qr_done = sem("qt_mm"), sem("qv_done"), sem("qr_done")
        kv_mm, ksq_done, vhi_done, kraw_done = sem("kv_mm"), sem("ksq_done"), sem("vhi_done"), sem("kraw_done")
        kvar_done, kr_done, kn_done = sem("kvar_done"), sem("kr_done"), sem("kn_done")
        kt_mm, kt_ev = sem("kt_mm"), sem("kt_ev")
        s_mm, s_done, max_done, p_exp, p_rec, p_norm = (sem("s_mm"), sem("s_done"), sem("max_done"),
                                                        sem("p_exp"), sem("p_rec"), sem("p_norm"))
        pt_mm, pthi_done, ptlo_done = sem("pt_mm"), sem("pthi_done"), sem("ptlo_done")
        pv_mm, othi_done, otlo_done = sem("pv_mm"), sem("othi_done"), sem("otlo_done")
        d_mm, d_add = sem("d_mm"), sem("d_add")
        f_x2t, ra_mm, lg_done, f_exp, mid_done = (sem("f_x2t"), sem("ra_mm"), sem("lg_done"),
                                                  sem("f_exp"), sem("mid_done"))
        mt_mm, mt_ev, dl_mm, dl_add, mr_done = sem("mt_mm"), sem("mt_ev"), sem("dl_mm"), sem("dl_add"), sem("mr_done")

        block = ctx.enter_context(nc.Block())

        OUT_COL = 0
        DN_COL, GU_COL = 2048, 3072
        WKV_COL = 0
        WQ_COL = [1024, 1536, 3072, 3584]
        OUT_BANK = [6, 6, 6, 6, 6, 7, 6, 7]
        WQ_SLOT = [1, 3, 4, 5]
        WO_COL = [2048, 2560, 4096, 4608]
        RAC = NE + NE * RANK

        def kv_bank(g, n, j):
            return bank[2 + j % 2] if isinstance(g, int) and g == n == 0 else bank[2]

        def mamba_raw(p):
            return raw_b[:, (p - 4) * 512:(p - 3) * 512] if 4 <= p < 8 else raw_a[:, p % 8 * 512:(p % 8 + 1) * 512]

        @block.sync
        def _(sp_eng):
            def load_x(b):
                sp_eng.dma_start(res[:, b, :], x[b]).then_inc(ld_x[b], 16)

            def load_win(p):
                if p >= 8:
                    sp_eng.wait_ge(win_l, p - 7)
                sp_eng.dma_start(mamba_raw(p), w_in[p]).then_inc(ld_win[p % 8], 16)

            load_x(0)
            sp_eng.dma_start(cst[:, 0:P], consts[:, 0:P]).then_inc(ld_small[0], 16)
            sp_eng.dma_start(row_sb[:, 0:DM], rows[0:DM].partition_broadcast(P)).then_inc(ld_small[1], 16)
            load_x(1)
            load_x(2)
            load_x(3)
            load_win(0)
            sp_eng.dma_start(wdt_raw[:, :], w_dt).then_inc(ld_small[3], 16)
            sp_eng.dma_start(chan_sb[:, :], chan).then_inc(ld_small[2], 16)
            sp_eng.dma_start(row_sb[:, DM:], rows[DM:].partition_broadcast(P)).then_inc(ld_small[5], 16)
            sp_eng.dma_start(cst[:, P:], consts[:, P:]).then_inc(ld_small[6], 16)
            load_win(1)
            load_win(2)
            load_win(3)
            for b in range(4, 8):
                load_win(b)
                load_x(b)
            load_win(8)
            load_win(9)
            sp_eng.wait_ge(win_l, 8)
            sp_eng.dma_start(raw_b[:, :], w_out).then_inc(ld_wout, 16)
            sp_eng.wait_ge(win_l, 10)
            sp_eng.dma_start(raw_a[:, :], w_gu[0]).then_inc(ld_gu, 16)
            sp_eng.wait_ge(wout_l, 4)
            sp_eng.dma_start(raw_b[:, 0:1024], w_dn[0]).then_inc(ld_dn, 16)

            def load_ctx(i):
                if i >= 2:
                    sp_eng.wait_ge(cx_l, i - 1)
                sp_eng.dma_start(raw_b[:, 1024 + i % 2 * 512:1536 + i % 2 * 512],
                                 ctx_t[i // 2, :, i % 2 * 512:(i % 2 + 1) * 512]).then_inc(ld_ctx[i % 2], 16)

            load_ctx(0)
            load_ctx(1)

            def load_xre(n):
                sp_eng.dma_start(xre[:, n * HALF:(n + 1) * HALF, :],
                                 x[n * HALF:(n + 1) * HALF].rearrange("b l d -> l b d")).then_inc(ld_xre[n], 16)

            def next_mlp(c):
                sp_eng.wait_ge(dn_l, 2 * c + 2)
                sp_eng.dma_start(raw_b[:, 0:1024], w_dn[bass.ds(c + 1, 1)].rearrange("a p n -> (a p) n"))\
                    .then_inc(ld_dn, 16)
                sp_eng.wait_ge(gu_l, 4 * c + 4)
                sp_eng.dma_start(raw_a[:, :], w_gu[bass.ds(c + 1, 1)].rearrange("a p n -> (a p) n"))\
                    .then_inc(ld_gu, 16)

            sp_eng.wait_ge(gu_l, 4)
            sp_eng.dma_start(raw_a[:, :], w_gu[1]).then_inc(ld_gu, 16)
            sp_eng.wait_ge(o_mm, 8)
            sp_eng.wait_ge(n_x, 16)
            load_xre(0)
            load_ctx(2)
            load_ctx(3)
            load_xre(1)
            sp_eng.wait_ge(dn_l, 2)
            sp_eng.dma_start(raw_b[:, 0:1024], w_dn[1]).then_inc(ld_dn, 16)
            for i in range(4, 8):
                load_ctx(i)
            with sp_eng.Fori(1, MLP_IT - 1) as c:
                next_mlp(c)
            sp_eng.wait_ge(gu_l, 4 * MLP_IT)
            sp_eng.dma_start(raw_a[:, :], w_q[0]).then_inc(ld_q, 16)
            sp_eng.wait_ge(dn_l, 2 * MLP_IT)
            sp_eng.dma_start(raw_b[:, 0:1024], w_kv[0]).then_inc(ld_kv, 16)
            sp_eng.wait_ge(wkv_l, 2)
            sp_eng.dma_start(raw_b[:, :], w_o[0]).then_inc(ld_o, 16)
            sp_eng.wait_ge(n_x, 24)
            sp_eng.dma_start(mask_sb[:, :], mask).then_inc(ld_small[4], 16)
            sp_eng.dma_start(ra_sb[:, :, :], w_ra).then_inc(ld_lora[0], 16)
            sp_eng.dma_start(bl_sb[:, :], w_b).then_inc(ld_lora[1], 16)

            def next_group(g):
                sp_eng.wait_ge(wq_l, 4 * g + 4)
                sp_eng.dma_start(raw_a[:, :], w_q[bass.ds(g + 1, 1)].rearrange("a p n -> (a p) n"))\
                    .then_inc(ld_q, 16)
                sp_eng.wait_ge(wo_l, 4 * g + 4)
                sp_eng.dma_start(raw_b[:, 0:1024], w_kv[bass.ds(g + 1, 1)].rearrange("a p n -> (a p) n"))\
                    .then_inc(ld_kv, 16)
                sp_eng.wait_ge(wkv_l, 2 * g + 4)
                sp_eng.dma_start(raw_b[:, :], w_o[bass.ds(g + 1, 1)].rearrange("a p n -> (a p) n"))\
                    .then_inc(ld_o, 16)

            with sp_eng.Fori(0, GROUPS - 1) as g:
                next_group(g)
            for b in range(B):
                sp_eng.wait_ge(n_x, 33 + b)
                sp_eng.dma_start(out[b], res[:, b, :]).then_inc(st_out, 16)
            sp_eng.wait_ge(st_out, 16 * B)

        @block.tensor
        def _(pe):
            mm = nc.tensor.matmul

            def mm3(o, l_hi, l_lo, r_hi, r_lo, first, last):
                mm(o, l_hi, r_hi, start=first, stop=False)
                mm(o, l_hi, r_lo, start=False, stop=False)
                return mm(o, l_lo, r_hi, start=False, stop=last)

            def norm_t(i, banks):
                pe.wait_ge(n_x, i + 1)
                if i >= 2:
                    pe.wait_ge(n_lo, i - 1)
                for k in range(KT):
                    t = nc.tensor.transpose(banks[i % 2][:, k * P:(k + 1) * P],
                                            xn[:, i % 2, k * P:(k + 1) * P], ident)
                t.then_inc(n_t, 1)

            order = [(n, p) for n in range(2) for p in range(NPIECE)]

            def in_step(f):
                n, p = order[f]
                pe.wait_ge(win_l, p + 1)
                pe.wait_ge(n_lo, 4 * n + 4)
                if f >= 2:
                    pn, pp = order[f - 2]
                    if pp < NCONV:
                        pe.wait_ge(conv_ev, NCONV * pn + pp + 1)
                    else:
                        pe.wait_ge(z_out, NH * pn + pp - NCONV + 1)
                for k in range(KT):
                    c0 = p * 512 + k * P
                    tok = slice(n * NTOK, (n + 1) * NTOK)
                    t = mm3(bank[f % 2][:, :], w_hi[:, c0:c0 + P], w_lo[:, c0:c0 + P],
                            act_hi[:, k, tok], act_lo[:, k, tok], k == 0, k == KT - 1)
                t.then_inc(in_mm, 1)

            def dt_step(n):
                pe.wait_ge(dt_w, 2)
                pe.wait_ge(n_lo, 4 * n + 4)
                if n:
                    pe.wait_ge(dt_a, 1)
                for k in range(KT):
                    t = mm3(bank[6][0:NH, :], wdt_hi[:, k * NH:(k + 1) * NH], wdt_lo[:, k * NH:(k + 1) * NH],
                            act_hi[:, k, n * NTOK:(n + 1) * NTOK], act_lo[:, k, n * NTOK:(n + 1) * NTOK],
                            k == 0, k == KT - 1)
                t.then_inc(dt_mm, 1)

            def dt_turn(n):
                pe.wait_ge(dt_ev, n + 1)
                for j in range(HALF):
                    t = nc.tensor.transpose(bank[6][:, j * NH:(j + 1) * NH], dt_row[:, j * L:(j + 1) * L],
                                            ident[0:NH, 0:NH])
                t.then_inc(dt_t, 1)

            def ssm1(b):
                n, tok = b // HALF, slice(b % HALF * L, (b % HALF + 1) * L)
                pe.wait_ge(conv_out, NCONV * n + NCONV)
                if b:
                    pe.wait_ge(xt_ev, b)
                nc.tensor.transpose(bank[7][:, 0:P], xbc[:, n, 0, tok], ident).then_inc(xt_mm, 1)
                pe.wait_ge(md_done, b + 1)
                if b:
                    pe.wait_ge(exp_done, b)
                mm(bank[2][:, :], strict, md[:, b % 2, :, :], start=True, stop=True).then_inc(cum_mm, 1)
                if b >= 2:
                    pe.wait_ge(att_done, b - 1)
                mm(bank[3 + b % 2][:, :], xbc[:, n, 1, tok], xbc[:, n, 2:6, tok], start=True, stop=True).then_inc(sc_mm, 1)

            def ssm2(b):
                pe.wait_ge(att_done, b + 1)
                pe.wait_ge(xt_ev, b + 1)
                if b:
                    pe.wait_ge(y1_done, b)
                mm(bank[5][:, :], xtok[:, b % 2, :], att[:, :, :], start=True, stop=True).then_inc(y_mm, 1)

            def out_step(b):
                pe.wait_ge(wout_l, 4)
                pe.wait_ge(ylo_done, b + 1)
                if b == 5:
                    pe.wait_ge(xt_ev, 8)
                elif b:
                    pe.wait_ge(o_add, b if b < 6 else b - 1)
                for k in range(NH):
                    c0 = OUT_COL + k * 512
                    t = mm3(bank[OUT_BANK[b]][:, :], y_hi[:, b % 4, k, :], y_lo[:, b % 4, k, :],
                            w_hi[:, c0:c0 + 512], w_lo[:, c0:c0 + 512], k == 0, k == NH - 1)
                t.then_inc(o_mm, 1)

            pe.wait_ge(ld_small[0], 16)
            for i in range(4):
                norm_t(i, (bank[2], bank[3]))
            tb = (bank[0], bank[1])
            in_step(0)
            dt_step(0)
            in_step(1)
            dt_turn(0)
            for f in range(2, 6):
                in_step(f)
            for i in range(4, 8):
                norm_t(i, (bank[2], bank[3]))
                in_step(i + 2)
            dt_step(1)
            in_step(10)
            dt_turn(1)
            ssm1(0)
            in_step(11)
            ssm1(1)
            in_step(12)
            ssm2(0)
            ssm1(2)
            in_step(13)
            ssm2(1)
            ssm1(3)
            in_step(14)
            ssm2(2)
            in_step(15)
            ssm2(3)
            in_step(16)
            in_step(17)
            ssm1(4)
            in_step(18)
            ssm1(5)
            in_step(19)
            ssm2(4)
            pe.wait_ge(dt_a, 2)
            out_step(0)
            ssm1(6)
            ssm2(5)
            out_step(1)
            ssm1(7)
            ssm2(6)
            out_step(2)
            ssm2(7)
            out_step(3)
            pe.wait_ge(z_out, 8)
            for i in range(8, 12):
                norm_t(i, tb)
                out_step(i - 4)
            norm_t(12, tb)
            pe.wait_ge(y1_done, 8)

            def gu_step(c, k, n, turn=None):
                m_i = 2 * n + k
                pe.wait_ge(gu_l, 4 * c + 2 * k + 2)
                if not (isinstance(c, int) and 4 * c + m_i < 2):
                    pe.wait_ge(h_done, 4 * c + m_i - 1)
                tok = slice(n * NTOK, (n + 1) * NTOK)
                for which in range(2):
                    if which and turn is not None:
                        norm_t(turn, tb)
                    o = bank[(2, 4)[m_i % 2] + which]
                    for kk in range(KT):
                        c0 = GU_COL + (2 * k + which) * 512 + kk * P
                        t = mm3(o[:, :], w_hi[:, c0:c0 + P], w_lo[:, c0:c0 + P],
                                act_hi[:, kk, tok], act_lo[:, kk, tok], kk == 0, kk == KT - 1)
                t.then_inc(gu_mm, 1)

            def dn_step(c, b):
                pe.wait_ge(hlo_done, 4 * c + 2 * (b // HALF) + 2)
                if b == 0:
                    pe.wait_ge(dn_l, 2 * c + 2)
                if b == 0:
                    pe.wait_ge(o_add, 8 + 8 * c)
                elif b >= 2:
                    pe.wait_ge(o_add, 8 + 8 * c + b - 1)
                tok = slice(b * L, (b + 1) * L)
                for k in range(2):
                    c0 = DN_COL + k * 512
                    t = mm3(bank[6 + b % 2][:, :], h_hi[:, k, tok], h_lo[:, k, tok],
                            w_hi[:, c0:c0 + 512], w_lo[:, c0:c0 + 512], k == 0, k == 1)
                t.then_inc(o_mm, 1)

            def kv_step(g, n, j):
                i = 8 * g + 4 * n + j
                pe.wait_ge(wkv_l, 2 * g + 2)
                if isinstance(g, int) and g == n == 0:
                    if j >= 2:
                        pe.wait_ge(kraw_done, j - 1)
                else:
                    pe.wait_ge(kraw_done, i)
                tok = slice((4 * n + j) * L, (4 * n + j + 1) * L)
                for k in range(KT):
                    c0 = WKV_COL + k * 256
                    t = mm3(kv_bank(g, n, j)[:, 0:256], ctx_hi[:, k, tok], ctx_lo[:, k, tok],
                            w_hi[:, c0:c0 + 256], w_lo[:, c0:c0 + 256], k == 0, k == KT - 1)
                t.then_inc(kv_mm, 1)

            def mlp_step(c):
                first, last = (isinstance(c, int) and c == x for x in (0, MLP_IT - 1))
                if first:
                    pe.wait_ge(n_lo, 12)
                gu_step(c, 0, 0)
                if first:
                    norm_t(13, tb)
                    norm_t(14, tb)
                gu_step(c, 1, 0, 15 if first else None)
                if first:
                    pe.wait_ge(n_lo, 16)
                gu_step(c, 0, 1)
                gu_step(c, 1, 1)
                for b in range(B):
                    dn_step(c, b)
                    if last and b >= 3:
                        if b < 7:
                            norm_t(13 + b, tb)
                            if b == 3:
                                pe.wait_ge(h_done, 4 * MLP_IT - 1)
                            kv_step(0, 0, b - 3)

            mlp_step(0)
            with pe.Fori(1, MLP_IT - 1) as c:
                mlp_step(c)
            mlp_step(MLP_IT - 1)

            def q_step(g, n, h):
                pe.wait_ge(wq_l, 4 * g + h + 1)
                r = 5 * n + h
                wait_bank(g, r)
                tok = slice(n * NTOK, (n + 1) * NTOK)
                for k in range(KT):
                    c0 = WQ_COL[h] + k * P
                    t = mm3(bank[r % 2][:, :], w_hi[:, c0:c0 + P], w_lo[:, c0:c0 + P],
                            act_hi[:, k, tok], act_lo[:, k, tok], k == 0, k == KT - 1)
                t.then_inc(q_mm, 1)

            def wait_bank(g, r):
                pr = (r - 2) % 10
                gg = g if r >= 2 else g - 1
                if isinstance(gg, int) and gg < 0:
                    return
                n, hh = pr // 5, pr % 5
                if hh < 4:
                    pe.wait_ge(q_ev, 8 * gg + 4 * n + hh + 1)
                else:
                    pe.wait_ge(kt_ev, 2 * gg + n + 1)

            def qt_step(g, n, h):
                i = 8 * g + 4 * n + h
                pe.wait_ge(q_ev, i + 1)
                if not (isinstance(g, int) and i == 0):
                    pe.wait_ge(qsq_done, i)
                for j in range(HALF):
                    t = nc.tensor.transpose(bank[7][:, j * P:(j + 1) * P], q_t[:, n, h, j * L:(j + 1) * L], ident)
                t.then_inc(qt_mm, 1)

            def kt_step(g, n):
                pe.wait_ge(kn_done, 2 * g + n + 1)
                wait_bank(g, 5 * n + 4)
                for j in range(HALF):
                    t = nc.tensor.transpose(bank[(5 * n + 4) % 2][:, j * P:(j + 1) * P], kraw[:, j, :], ident)
                t.then_inc(kt_mm, 1)

            def s_step(g, jj):
                n, j = jj // HALF, jj % HALF
                t_i = 8 * g + jj
                pe.wait_ge(q_ev, 8 * g + 4 * n + 4)
                pe.wait_ge(kt_ev, 2 * g + n + 1)
                if not (isinstance(g, int) and t_i == 0):
                    pe.wait_ge(s_done, t_i)
                tok = slice(j * L, (j + 1) * L)
                for h in range(GH):
                    t = mm(bank[3][:, h * L:(h + 1) * L], q_t[:, n, h, tok], k_t[:, n, tok],
                           start=True, stop=True)
                t.then_inc(s_mm, 1)

            def pt_step(g, jj):
                t_i = 8 * g + jj
                pe.wait_ge(p_norm, t_i + 1)
                if not (isinstance(g, int) and t_i == 0):
                    pe.wait_ge(ptlo_done, t_i)
                for h in range(GH):
                    t = nc.tensor.transpose(bank[4][:, h * L:(h + 1) * L], pb[:, jj % 2, h, :], ident)
                t.then_inc(pt_mm, 1)

            def pv_step(g, jj):
                t_i = 8 * g + jj
                pe.wait_ge(ptlo_done, t_i + 1)
                if not (isinstance(g, int) and t_i == 0):
                    pe.wait_ge(otlo_done, t_i)
                n, j = jj // HALF, jj % HALF
                mm3(bank[5][:, :], v_hi[:, n, j, :], v_lo[:, n, j, :], pt_hi[:, :], pt_lo[:, :], True, True)\
                    .then_inc(pv_mm, 1)

            def d_step(g, jj):
                t_i = 8 * g + jj
                pe.wait_ge(otlo_done, t_i + 1)
                if not (isinstance(g, int) and t_i == 0):
                    pe.wait_ge(d_add, t_i)
                for h in range(GH):
                    hs = slice(h * L, (h + 1) * L)
                    c0 = WO_COL[h]
                    if jj == 0:
                        pe.wait_ge(wo_l, 4 * g + h + 1)
                    t = mm3(bank[6][:, :], ot_hi[:, hs], ot_lo[:, hs], w_hi[:, c0:c0 + 512],
                            w_lo[:, c0:c0 + 512], h == 0, h == GH - 1)
                t.then_inc(d_mm, 1)

            def slot(g, jj, produce, before=True):
                n, j = jj // HALF, jj % HALF
                pg, pn = (g, 1) if n == 0 else (g + 1, 0)
                if produce:
                    if j == 0:
                        kv_step(pg, pn, 0)
                    q_step(pg, pn, j)
                    if j == 3:
                        kt_step(pg, pn)
                if j < 3:
                    s_step(g, jj + 1)
                if produce and j < 3:
                    kv_step(pg, pn, j + 1)
                pt_step(g, jj)
                if produce:
                    qt_step(pg, pn, j)
                if before:
                    d_step(*((g, jj - 1) if jj else (g - 1, 7)))
                pv_step(g, jj)
                if j == 3 and produce:
                    s_step(pg, 4 * pn)

            pe.wait_ge(n_lo, 20)
            pe.wait_ge(h_done, 4 * MLP_IT)
            for h in range(GH):
                q_step(0, 0, h)
                norm_t(20 + h, (bank[4], bank[5]))
                if h:
                    if h == 1:
                        pe.wait_ge(o_add, 8 + 8 * MLP_IT)
                    qt_step(0, 0, h - 1)
            kt_step(0, 0)
            qt_step(0, 0, 3)
            s_step(0, 0)
            pe.wait_ge(n_lo, 24)
            slot(0, 0, True, before=False)
            with pe.Fori(0, GROUPS - 1) as g:
                for jj in range(1, 8):
                    slot(g, jj, True)
                slot(g + 1, 0, True)

            def lora_in(b):
                if b == 0:
                    pe.wait_ge(ld_lora[0], 16)
                pe.wait_ge(f_x2t, b + 1)
                o = bank[(2, 7)[b // 4]]
                for k in range(KT):
                    t = mm(o[:, b % 4 * RAC:(b % 4 + 1) * RAC], x2t[:, b % 2, k, :], ra_sb[:, k, :],
                           start=(k == 0), stop=(k == KT - 1))
                t.then_inc(ra_mm, 1)

            def f_norm_t(i):
                pe.wait_ge(n_x, i + 1)
                if i >= 26:
                    pe.wait_ge(f_x2t, i - 25)
                for k in range(KT):
                    t = nc.tensor.transpose(tb[i % 2][:, k * P:(k + 1) * P], res[:, i - 24, k * P:(k + 1) * P],
                                            ident)
                t.then_inc(n_t, 1)

            def mt_step(i):
                pe.wait_ge(mid_done, i + 1)
                for b in range(4 * i, 4 * i + 4):
                    t = nc.tensor.transpose(bank[(2, 7)[i]][0:NE * RANK, b % 4 * P:(b % 4 + 1) * P],
                                            mid[:, b, :, :].rearrange("p e r -> p (e r)"), ident)
                t.then_inc(mt_mm, 1)

            def dl_step(b):
                if b == 0:
                    pe.wait_ge(ld_lora[1], 16)
                    pe.wait_ge(s_done, 8 * GROUPS)
                    pe.wait_ge(ptlo_done, 8 * GROUPS)
                pe.wait_ge(mt_ev, b // 4 + 1)
                if b >= 2:
                    pe.wait_ge(dl_add, b - 1)
                mm(bank[3 + b % 2][:, :], midt[:, b, :], bl_sb[:, :], start=True, stop=True)\
                    .then_inc(dl_mm, 1)

            def last_slot(jj, fill):
                if jj == 4:
                    d_step(last, 3)
                if jj < 7:
                    s_step(last, jj + 1)
                pt_step(last, jj)
                for step, b in fill:
                    step(b)
                if jj > 4:
                    d_step(last, jj - 1)
                if jj == 7:
                    mt_step(0)
                pv_step(last, jj)

            last = GROUPS - 1
            for jj in range(1, 4):
                slot(last, jj, True)
            pe.wait_ge(kt_ev, 2 * GROUPS)
            pe.wait_ge(qsq_done, 8 * GROUPS)
            last_slot(4, ((f_norm_t, 24), (f_norm_t, 25)))
            last_slot(5, ((lora_in, 0), (f_norm_t, 26), (lora_in, 1), (f_norm_t, 27)))
            last_slot(6, ((lora_in, 2), (lora_in, 3), (f_norm_t, 28)))
            last_slot(7, ((lora_in, 4), (f_norm_t, 29)))
            dl_step(0)
            lora_in(5)
            d_step(last, 7)
            dl_step(1)
            f_norm_t(30)
            lora_in(6)
            f_norm_t(31)
            lora_in(7)
            dl_step(2)
            dl_step(3)
            mt_step(1)
            for b in range(4, 8):
                dl_step(b)

        @block.scalar
        def _(act):
            A = nc.scalar.activation

            def square(i):
                if i < 8:
                    act.wait_ge(ld_x[i], 16)
                else:
                    act.wait_ge(o_add, i - 7)
                if i >= 1:
                    act.wait_ge(n_ssq, i)
                A(junk[:, :], res[:, i % 8, :], ACT.Square, accum_out=stat[:, i:i + 1]).then_inc(n_ssq, 1)

            def norm_hi(i, banks):
                act.wait_ge(n_t, i + 1)
                b = i % 8
                A(act_hi[:, :, b * L:(b + 1) * L], banks[i % 2][:, :].rearrange("p (k n) -> p k n", k=KT),
                  ACT.Copy).then_inc(n_hi, 1)

            def win_hi(p):
                act.wait_ge(ld_win[p % 8], 16 * (p // 8 + 1))
                A(w_hi[:, p * 512:(p + 1) * 512], mamba_raw(p), ACT.Copy).then_inc(win_h, 1)

            nb = (bank[2], bank[3])
            for i in range(4):
                square(i)
            norm_hi(0, nb)
            norm_hi(1, nb)
            win_hi(0)
            norm_hi(2, nb)
            act.wait_ge(ld_small[3], 16)
            A(wdt_hi[:, :], wdt_raw[:, :], ACT.Copy).then_inc(dt_w, 1)
            norm_hi(3, nb)
            win_hi(1)
            act.wait_ge(ld_small[5], 16)
            A(a2[:, :], row_sb[:, 2 * DM:2 * DM + NH], ACT.Exp).then_inc(setup_a, 1)
            win_hi(2)
            win_hi(3)

            order = [(n, p) for n in range(2) for p in range(NPIECE)]

            def in_evac(f):
                n, p = order[f]
                act.wait_ge(in_mm, f + 1)
                if p < NCONV:
                    q = NCONV * n + p
                    if q == 0:
                        act.wait_ge(setup_v, 4)
                    if q >= 2:
                        act.wait_ge(conv_c, q - 1)
                    A(pre[:, q % 2, :, DCONV - 1:], bank[f % 2][:, :].rearrange("p (s n) -> p s n", s=HALF),
                      ACT.Copy)
                    if q >= 3:
                        act.wait_ge(conv_out, q - 2)
                    A(cbuf[:, q % 3, :], bank[f % 2][:, :], ACT.Identity,
                      bias=cw[:, NCONV * DCONV + p:NCONV * DCONV + p + 1],
                      scale=cw[:, p * DCONV + DCONV - 1:p * DCONV + DCONV]).then_inc(conv_ev, 1)
                else:
                    i = NH * n + p - NCONV
                    if i >= 1:
                        act.wait_ge(z_out, i)
                    A(th[:, 0, :], bank[f % 2][:, :], ACT.Tanh, scale=0.5).then_inc(z_th, 1)

            def conv_tanh(q):
                act.wait_ge(conv_c, q + 1)
                if q >= 2:
                    act.wait_ge(conv_out, q - 1)
                A(th[:, 1 + q % 2, :], cbuf[:, q % 3, :], ACT.Tanh).then_inc(conv_th, 1)

            def dt_evac(n):
                act.wait_ge(dt_mm, n + 1)
                if n:
                    act.wait_ge(dt_t, n)
                A(dt_row[:, :], bank[6][0:NH, :], ACT.Copy).then_inc(dt_ev, 1)

            def dt_exp(n):
                act.wait_ge(dt_a, n + 1)
                A(sp[:, 2, :], sp[:, 1, :], ACT.Exp).then_inc(dt_exp_done, 1)

            def x_evac(b):
                act.wait_ge(xt_mm, b + 1)
                if b >= 2:
                    act.wait_ge(y_mm, b - 1)
                A(xtok[:, b % 2, :], bank[7][:, 0:P], ACT.Copy).then_inc(xt_ev, 1)

            def decay(b):
                act.wait_ge(cum_mm, b + 1)
                if b == 0:
                    act.wait_ge(setup_v, 4)
                if b >= 2:
                    act.wait_ge(att_done, b - 1)
                for h in range(NH):
                    t = A(em[:, b % 2, h, :], bank[2][:, h * L:(h + 1) * L], ACT.Exp, scale=a2[:, h:h + 1])
                t.then_inc(exp_done, 1)

            def y_split(b):
                act.wait_ge(y1_done, b + 1)
                if b >= 4:
                    act.wait_ge(o_mm, b - 3)
                A(y_hi[:, b % 4, :, :], yb[:, b % 2, :, :], ACT.Copy).then_inc(yhi_done, 1)

            in_evac(0)
            win_hi(4)
            dt_evac(0)
            in_evac(1)
            conv_tanh(0)
            win_hi(5)
            square(4)
            in_evac(2)
            conv_tanh(1)
            win_hi(6)
            dt_exp(0)
            square(5)
            in_evac(3)
            conv_tanh(2)
            win_hi(7)
            square(6)
            in_evac(4)
            conv_tanh(3)
            win_hi(8)
            square(7)
            in_evac(5)
            conv_tanh(4)
            norm_hi(4, nb)
            win_hi(9)
            in_evac(6)
            conv_tanh(5)
            norm_hi(5, nb)
            in_evac(7)
            norm_hi(6, nb)
            in_evac(8)
            norm_hi(7, nb)
            in_evac(9)
            dt_evac(1)
            in_evac(10)
            x_evac(0)
            decay(0)
            conv_tanh(6)
            in_evac(11)
            x_evac(1)
            decay(1)
            dt_exp(1)
            conv_tanh(7)
            in_evac(12)
            x_evac(2)
            decay(2)
            conv_tanh(8)
            y_split(0)
            in_evac(13)
            x_evac(3)
            decay(3)
            conv_tanh(9)
            y_split(1)
            in_evac(14)
            conv_tanh(10)
            y_split(2)
            in_evac(15)

            def wout_hi(k):
                if k == 0:
                    act.wait_ge(ld_wout, 16)
                    act.wait_ge(in_mm, 14)
                A(w_hi[:, OUT_COL + k * 512:OUT_COL + (k + 1) * 512], raw_b[:, k * 512:(k + 1) * 512],
                  ACT.Copy).then_inc(wout_h, 1)

            wout_hi(0)
            wout_hi(1)
            conv_tanh(11)
            y_split(3)
            in_evac(16)
            wout_hi(2)
            wout_hi(3)
            in_evac(17)
            x_evac(4)
            decay(4)
            in_evac(18)
            x_evac(5)
            decay(5)
            in_evac(19)
            tb = (bank[0], bank[1])

            def gu_hi(c, i):
                act.wait_ge(ld_gu, 16 * c + 16)
                if isinstance(c, int) and c == 0:
                    act.wait_ge(in_mm, 20)
                else:
                    act.wait_ge(gu_mm, 4 * c)
                A(w_hi[:, GU_COL + i * 512:GU_COL + (i + 1) * 512], raw_a[:, i * 512:(i + 1) * 512],
                  ACT.Copy).then_inc(gu_h, 1)

            def dn_hi(c, i):
                act.wait_ge(ld_dn, 16 * c + 16)
                if not (isinstance(c, int) and c == 0):
                    act.wait_ge(o_mm, 8 + 8 * c)
                A(w_hi[:, DN_COL + i * 512:DN_COL + (i + 1) * 512], raw_b[:, i * 512:(i + 1) * 512],
                  ACT.Copy).then_inc(dn_h, 1)

            gu_hi(0, 0)
            y_split(4)
            square(8)
            x_evac(6)
            decay(6)
            gu_hi(0, 1)
            y_split(5)
            x_evac(7)
            decay(7)
            square(9)
            gu_hi(0, 2)
            y_split(6)
            square(10)
            y_split(7)
            gu_hi(0, 3)
            for i in range(8, 12):
                square(i + 3)
                norm_hi(i, tb)
            square(15)
            norm_hi(12, tb)

            def silu(c, m_i):
                act.wait_ge(gu_mm, 4 * c + m_i + 1)
                if not (isinstance(c, int) and 4 * c + m_i < 2):
                    act.wait_ge(h_done, 4 * c + m_i - 1)
                A(sg[:, m_i % 2, :], bank[(2, 4)[m_i % 2]][:, :], ACT.Silu).then_inc(silu_done, 1)

            def h_split(c, m_i):
                act.wait_ge(h_done, 4 * c + m_i + 1)
                if not (isinstance(c, int) and c == 0):
                    act.wait_ge(o_mm, 8 + 8 * c - 4 + 4 * (m_i // 2))
                k, n = m_i % 2, m_i // 2
                A(h_hi[:, k, n * NTOK:(n + 1) * NTOK], hb[:, m_i % 2, :], ACT.Copy).then_inc(hhi_done, 1)

            def ctx_split(i):
                act.wait_ge(ld_ctx[i % 2], 16 * (i // 2 + 1))
                if i == 0:
                    act.wait_ge(o_mm, 8)
                    act.wait_ge(n_x, 16)
                A(ctx_hi[:, i // 2, i % 2 * 512:(i % 2 + 1) * 512],
                  raw_b[:, 1024 + i % 2 * 512:1536 + i % 2 * 512], ACT.Copy).then_inc(cx_h, 1)

            def mlp_step(c):
                first, last = (isinstance(c, int) and c == x for x in (0, MLP_IT - 1))
                for m_i in range(4):
                    silu(c, m_i)
                    if first and m_i == 0:
                        norm_hi(13, tb)
                        norm_hi(14, tb)
                    h_split(c, m_i)
                    if m_i == 0:
                        dn_hi(c, 0)
                        dn_hi(c, 1)
                        if first:
                            norm_hi(15, tb)
                    if first:
                        ctx_split(2 * m_i)
                        ctx_split(2 * m_i + 1)
                    if last and m_i == 1:
                        wq_hi(0, 0)
                        wq_hi(0, 1)
                        wkv_hi(0, 0)
                        wkv_hi(0, 1)
                if not last:
                    for i in range(4):
                        gu_hi(c + 1, i)

            def wkv_hi(g, i):
                act.wait_ge(ld_kv, 16 * g + 16)
                if isinstance(g, int) and g == 0:
                    act.wait_ge(o_mm, 8)
                else:
                    act.wait_ge(kv_mm, 8 * g)
                A(w_hi[:, WKV_COL + i * 512:WKV_COL + (i + 1) * 512], raw_b[:, i * 512:(i + 1) * 512],
                  ACT.Copy).then_inc(wkv_h, 1)

            def wq_hi(g, h):
                act.wait_ge(ld_q, 16 * g + 16)
                if isinstance(g, int) and g == 0:
                    act.wait_ge(*((o_mm, 8) if h < 2 else (gu_mm, 4 * MLP_IT)))
                else:
                    act.wait_ge(q_mm, 8 * g - 4 + h + 1)
                A(w_hi[:, WQ_COL[h]:WQ_COL[h] + 512], raw_a[:, h * 512:(h + 1) * 512],
                  ACT.Copy).then_inc(wq_h, 1)

            def wo_hi(g, h):
                act.wait_ge(ld_o, 16 * g + 16)
                if isinstance(g, int) and g == 0:
                    act.wait_ge(o_mm, 8 + 8 * MLP_IT)
                else:
                    act.wait_ge(d_mm, 8 * g)
                A(w_hi[:, WO_COL[h]:WO_COL[h] + 512], raw_b[:, h * 512:(h + 1) * 512], ACT.Copy)\
                    .then_inc(wo_h, 1)

            mlp_step(0)
            with act.Fori(1, MLP_IT - 1) as c:
                mlp_step(c)
            mlp_step(MLP_IT - 1)

            def q_evac(g, n, h):
                i = 8 * g + 4 * n + h
                act.wait_ge(q_mm, i + 1)
                if not (isinstance(g, int) and 8 * g + 4 * n < 8):
                    act.wait_ge(s_mm, 8 * g + 4 * n - 3)
                A(q_t[:, n, h, :], bank[(5 * n + h) % 2][:, :], ACT.Copy).then_inc(q_ev, 1)

            def q_square(g, n, h):
                i = 8 * g + 4 * n + h
                act.wait_ge(qt_mm, i + 1)
                if not (isinstance(g, int) and i == 0):
                    act.wait_ge(qsq_done, i)
                if not (isinstance(g, int) and i < 2):
                    act.wait_ge(qv_done, i - 1)
                for j in range(HALF):
                    t = A(qjunk[:, j * P:(j + 1) * P], bank[7][:, j * P:(j + 1) * P], ACT.Square,
                          accum_out=qss[:, h % 2, j:j + 1])
                t.then_inc(qsq_done, 1)

            def kv_evac(g, n, j):
                i = 8 * g + 4 * n + j
                act.wait_ge(kv_mm, i + 1)
                if not (isinstance(g, int) and i == 0):
                    act.wait_ge(ksq_done, i)
                if j == 0 and not (isinstance(g, int) and 2 * g + n == 0):
                    act.wait_ge(kvar_done, 2 * g + n)
                A(junk[:, 0:HD], kv_bank(g, n, j)[:, 0:HD], ACT.Square, accum_out=kv[:, 0, j:j + 1])\
                    .then_inc(ksq_done, 1)
                if not (isinstance(g, int) and 8 * g + 4 * n < 8):
                    act.wait_ge(pv_mm, 8 * g + 4 * n - 4 + max(0, j - 1))
                A(v_hi[:, n, j, :], kv_bank(g, n, j)[:, HD:2 * HD], ACT.Copy).then_inc(vhi_done, 1)

            def kt_evac(g, n):
                u = 2 * g + n
                act.wait_ge(kt_mm, u + 1)
                if isinstance(g, int) and u == 0:
                    act.wait_ge(setup_p, 1)
                if not (isinstance(g, int) and u < 2):
                    act.wait_ge(s_mm, 8 * g + 4 * n - 3)
                A(k_t[:, n, :], bank[(5 * n + 4) % 2][:, :], ACT.Copy, scale=qk_w[:, 0:1]).then_inc(kt_ev, 1)

            def softmax_exp(g, jj):
                t_i = 8 * g + jj
                act.wait_ge(max_done, t_i + 1)
                for h in range(GH):
                    t = A(pb[:, jj % 2, h, :], pb[:, jj % 2, h, :], ACT.Exp, bias=nmax[:, jj % 2, h:h + 1],
                          accum_out=psum_[:, jj % 2, h:h + 1])
                t.then_inc(p_exp, 1)

            def pt_evac(g, jj):
                act.wait_ge(pt_mm, 8 * g + jj + 1)
                if not (isinstance(g, int) and 8 * g + jj == 0):
                    act.wait_ge(pv_mm, 8 * g + jj)
                A(pt_hi[:, :], bank[4][:, :], ACT.Copy).then_inc(pthi_done, 1)

            def ot_evac(g, jj):
                act.wait_ge(pv_mm, 8 * g + jj + 1)
                if not (isinstance(g, int) and 8 * g + jj == 0):
                    act.wait_ge(d_mm, 8 * g + jj)
                A(ot_hi[:, :], bank[5][:, :], ACT.Copy).then_inc(othi_done, 1)

            def slot(g, jj, produce, refill=True):
                n, j = jj // HALF, jj % HALF
                pg, pn = (g, 1) if n == 0 else (g + 1, 0)
                if produce and j == 0:
                    kv_evac(pg, pn, 0)
                if j == 0:
                    softmax_exp(g, jj)
                if produce:
                    q_evac(pg, pn, j)
                    if j == 3:
                        kt_evac(pg, pn)
                if produce and j < 3:
                    kv_evac(pg, pn, j + 1)
                pt_evac(g, jj)
                if produce:
                    q_square(pg, pn, j)
                if j < 3:
                    softmax_exp(g, jj + 1)
                if refill and jj in WQ_SLOT:
                    wq_hi(g + 1, WQ_SLOT.index(jj))
                if jj == 0 and not (isinstance(g, int) and g == 0):
                    for h in range(GH):
                        wo_hi(g, h)
                if refill and jj == 2:
                    wkv_hi(g + 1, 0)
                    wkv_hi(g + 1, 1)
                ot_evac(g, jj)

            def res_copy(i):
                act.wait_ge(n_x, i + 1)
                A(res[:, i - 16, :], xn[:, i % 2, :], ACT.Copy).then_inc(res_x, 1)

            for i in range(16, 20):
                res_copy(i)
                norm_hi(i, tb)
                kv_evac(0, 0, i - 16)
                if i in (16, 18):
                    wq_hi(0, 2 + (i - 16) // 2)
            for h in range(GH):
                res_copy(20 + h)
                q_evac(0, 0, h)
                norm_hi(20 + h, (bank[4], bank[5]))
                if h:
                    q_square(0, 0, h - 1)
            kt_evac(0, 0)
            q_square(0, 0, 3)
            for h in range(GH):
                wo_hi(0, h)
            slot(0, 0, True)
            with act.Fori(0, GROUPS - 1) as g:
                for jj in range(1, 8):
                    slot(g, jj, True)
                slot(g + 1, 0, True, refill=False)

            def x2_evac(b):
                act.wait_ge(n_t, 25 + b)
                if b >= 2:
                    act.wait_ge(ra_mm, b - 1)
                A(x2t[:, b % 2, :, :], tb[b % 2][:, :].rearrange("p (k n) -> p k n", k=KT), ACT.Copy)\
                    .then_inc(f_x2t, 1)

            def last_norm(b):
                act.wait_ge(n_rstd, 33 + b)
                act.wait_ge(mr_done, b + 1)
                A(res[:, b, :], res[:, b, :], ACT.Identity, bias=mr[:, b:b + 1], scale=rstd[:, 32 + b:33 + b])\
                    .then_inc(n_x, 1)

            def gate_exp(i):
                act.wait_ge(lg_done, i + 1)
                A(ge[:, 4 * i:4 * i + 4, :], ge[:, 4 * i:4 * i + 4, :], ACT.Exp).then_inc(f_exp, 1)

            def mt_evac(i):
                act.wait_ge(mt_mm, i + 1)
                A(midt[:, 4 * i:4 * i + 4, :], bank[(2, 7)[i]][0:NE * RANK, :].rearrange("p (b n) -> p b n", b=4),
                  ACT.Copy).then_inc(mt_ev, 1)

            last = GROUPS - 1
            for jj in range(1, 4):
                slot(last, jj, True, refill=False)

            def last_slot(jj, tiles):
                if jj == 4:
                    softmax_exp(last, 4)
                pt_evac(last, jj)
                if jj < 7:
                    softmax_exp(last, jj + 1)
                for b in tiles:
                    x2_evac(b)
                if jj == 7:
                    mt_evac(0)
                ot_evac(last, jj)

            last_slot(4, (0, 1))
            last_slot(5, (2, 3))
            last_slot(6, (4,))
            gate_exp(0)
            last_slot(7, (5,))
            x2_evac(6)
            x2_evac(7)
            gate_exp(1)
            last_norm(0)
            mt_evac(1)
            for b in range(1, B):
                last_norm(b)

        @block.gpsimd
        def _(pool):
            TT = nc.gpsimd.tensor_tensor

            def lo(dst, src, hi, done):
                TT(dst, src, f32(hi), ALU.subtract).then_inc(done, 1)

            def rsqrt(i):
                pool.wait_ge(n_var, i + 1)
                TT(rstd[:, i:i + 1], var[:, i:i + 1], pow_m[:, 0:1], ALU.pow).then_inc(n_rstd, 1)

            def win_rest(p):
                pool.wait_ge(win_h, p + 1)
                s = slice(p * 512, (p + 1) * 512)
                lo(w_lo[:, s], mamba_raw(p), w_hi[:, s], win_l)

            pool.wait_ge(setup_v, 2)
            nq = NCONV * DCONV + NCONV
            for i in range(4):
                rsqrt(i)
                if i == 3:
                    win_rest(0)
            win_rest(1)
            pool.wait_ge(setup_v, 4)
            pool.wait_ge(ld_small[0], 16)
            TT(diag_d[:, :, :], d2[:, :].unsqueeze(2).to_broadcast([P, NH, L]),
               ident.unsqueeze(1).to_broadcast([P, NH, L]), ALU.mult).then_inc(diag_done, 1)
            TT(qk_w[:, :], chan_sb[:, nq:nq + 1], chan_sb[:, nq + 1:nq + 2], ALU.mult).then_inc(setup_p, 1)
            for p in range(2, 6):
                win_rest(p)

            def decay_in(b):
                pool.wait_ge(dt_done, b // HALF + 1)
                if b == 0:
                    pool.wait_ge(ld_small[6], 16)
                if b >= 2:
                    pool.wait_ge(em_done, b - 1)
                    pool.wait_ge(cum_mm, b - 1)
                TT(md[:, b % 2, :, :], dt_sb[:, b * NH:(b + 1) * NH].unsqueeze(2).to_broadcast([P, NH, L]),
                   tri_half.unsqueeze(1).to_broadcast([P, NH, L]), ALU.mult).then_inc(md_done, 1)

            def decay_out(b):
                pool.wait_ge(exp_done, b + 1)
                TT(em[:, b % 2, :, :], em[:, b % 2, :, :], md[:, b % 2, :, :], ALU.mult).then_inc(em_done, 1)

            def y_rest(b):
                pool.wait_ge(yhi_done, b + 1)
                lo(y_lo[:, b % 4, :, :], yb[:, b % 2, :, :], y_hi[:, b % 4, :, :], ylo_done)

            for i in range(4, 8):
                rsqrt(i)
                win_rest(i + 2)
            decay_in(0)
            decay_in(1)

            def wout_rest(k):
                pool.wait_ge(wout_h, k + 1)
                s = slice(OUT_COL + k * 512, OUT_COL + (k + 1) * 512)
                lo(w_lo[:, s], raw_b[:, k * 512:(k + 1) * 512], w_hi[:, s], wout_l)

            decay_out(0)
            decay_in(2)
            decay_out(1)
            decay_in(3)
            decay_out(2)
            y_rest(0)
            decay_out(3)
            y_rest(1)
            decay_in(4)
            y_rest(2)
            wout_rest(0)
            wout_rest(1)
            decay_in(5)
            y_rest(3)
            wout_rest(2)
            wout_rest(3)

            def gu_rest(c, i):
                pool.wait_ge(gu_h, 4 * c + i + 1)
                s = slice(GU_COL + i * 512, GU_COL + (i + 1) * 512)
                lo(w_lo[:, s], raw_a[:, i * 512:(i + 1) * 512], w_hi[:, s], gu_l)

            def dn_rest(c, i):
                pool.wait_ge(dn_h, 2 * c + i + 1)
                s = slice(DN_COL + i * 512, DN_COL + (i + 1) * 512)
                lo(w_lo[:, s], raw_b[:, i * 512:(i + 1) * 512], w_hi[:, s], dn_l)

            decay_out(4)
            decay_in(6)
            decay_out(5)
            decay_in(7)
            gu_rest(0, 0)
            y_rest(4)
            decay_out(6)
            rsqrt(8)
            y_rest(5)
            decay_out(7)
            gu_rest(0, 1)
            rsqrt(9)
            gu_rest(0, 2)
            y_rest(6)
            rsqrt(10)
            y_rest(7)
            gu_rest(0, 3)
            for i in range(11, 16):
                rsqrt(i)

            def add_x(b):
                pool.wait_ge(ld_xre[b // HALF], 16)
                pool.wait_ge(n_x, 9 + b)
                TT(res[:, b, :], res[:, b, :], xre[:, b, :], ALU.add).then_inc(x_add, 1)

            def mlp_step(c):
                first, last = (isinstance(c, int) and c == x for x in (0, MLP_IT - 1))
                for m_i in range(4):
                    k, n = m_i % 2, m_i // 2
                    pool.wait_ge(hhi_done, 4 * c + m_i + 1)
                    tok = slice(n * NTOK, (n + 1) * NTOK)
                    lo(h_lo[:, k, tok], hb[:, m_i % 2, :], h_hi[:, k, tok], hlo_done)
                    if m_i == 0:
                        dn_rest(c, 0)
                        dn_rest(c, 1)
                    if first and m_i:
                        for b in ((), (0, 1), (2, 3, 4), (5, 6, 7))[m_i]:
                            add_x(b)
                    if last and m_i == 1:
                        wq_rest(0, 0)
                        wq_rest(0, 1)
                        wkv_rest(0, 0)
                        wkv_rest(0, 1)
                if not last:
                    for i in range(4):
                        gu_rest(c + 1, i)

            def wkv_rest(g, i):
                pool.wait_ge(wkv_h, 2 * g + i + 1)
                s = slice(WKV_COL + i * 512, WKV_COL + (i + 1) * 512)
                lo(w_lo[:, s], raw_b[:, i * 512:(i + 1) * 512], w_hi[:, s], wkv_l)

            def wq_rest(g, h):
                pool.wait_ge(wq_h, 4 * g + h + 1)
                s = slice(WQ_COL[h], WQ_COL[h] + 512)
                lo(w_lo[:, s], raw_a[:, h * 512:(h + 1) * 512], w_hi[:, s], wq_l)

            def wo_rest(g, h):
                pool.wait_ge(wo_h, 4 * g + h + 1)
                s = slice(WO_COL[h], WO_COL[h] + 512)
                lo(w_lo[:, s], raw_b[:, h * 512:(h + 1) * 512], w_hi[:, s], wo_l)

            mlp_step(0)
            with pool.Fori(1, MLP_IT - 1) as c:
                mlp_step(c)
            mlp_step(MLP_IT - 1)

            def q_rsqrt(g, n, h):
                i = 8 * g + 4 * n + h
                pool.wait_ge(qv_done, i + 1)
                if not (isinstance(g, int) and 8 * g + 4 * n < 8):
                    pool.wait_ge(s_done, 8 * g + 4 * n - 3)
                TT(qr[:, 4 * n + h, :], qv[:, 4 * n + h, :], pow_m[:, 0:HALF], ALU.pow).then_inc(qr_done, 1)

            def k_rsqrt(g, n):
                pool.wait_ge(kvar_done, 2 * g + n + 1)
                if not (isinstance(g, int) and 2 * g + n == 0):
                    pool.wait_ge(kn_done, 2 * g + n)
                TT(kv[:, 2, :], kv[:, 1, :], pow_m[:, 0:HALF], ALU.pow).then_inc(kr_done, 1)

            def p_scale(g, jj):
                pool.wait_ge(p_rec, 8 * g + jj + 1)
                TT(pb[:, jj % 2, :, :], pb[:, jj % 2, :, :],
                   prec[:, jj % 2, :].unsqueeze(2).to_broadcast([P, GH, L]), ALU.mult).then_inc(p_norm, 1)

            def slot(g, jj, produce, refill=True):
                n, j = jj // HALF, jj % HALF
                pg, pn = (g, 1) if n == 0 else (g + 1, 0)
                if j == 0:
                    p_scale(g, jj)
                if produce and j == 2:
                    k_rsqrt(pg, pn)
                if produce:
                    q_rsqrt(pg, pn, j)
                if j < 3:
                    p_scale(g, jj + 1)
                if refill and jj in WQ_SLOT:
                    wq_rest(g + 1, WQ_SLOT.index(jj))
                if jj == 0 and not (isinstance(g, int) and g == 0):
                    for h in range(GH):
                        wo_rest(g, h)
                if refill and jj == 2:
                    wkv_rest(g + 1, 0)
                    wkv_rest(g + 1, 1)

            for i in range(16, 24):
                rsqrt(i)
                if i in (19, 20):
                    wq_rest(0, i - 17)
                if i == 22:
                    k_rsqrt(0, 0)
            for h in range(GH):
                q_rsqrt(0, 0, h)
            for h in range(GH):
                wo_rest(0, h)
            slot(0, 0, True)
            with pool.Fori(0, GROUPS - 1) as g:
                for jj in range(1, 8):
                    slot(g, jj, True)
                slot(g + 1, 0, True, refill=False)
            last = GROUPS - 1
            for jj in range(1, 4):
                slot(last, jj, True, refill=False)
                rsqrt(23 + jj)
            for jj in range(4, 8):
                if jj == 4:
                    p_scale(last, 4)
                if jj < 7:
                    p_scale(last, jj + 1)
                rsqrt(23 + jj)
            for i in range(31, 40):
                rsqrt(i)

        @block.vector
        def _(dve):
            V = nc.vector
            TT, STT, TS = V.tensor_tensor, V.scalar_tensor_tensor, V.tensor_scalar
            count = [0]

            def link(ins):
                count[0] += 1
                ins.then_inc(vch, 1)
                dve.wait_ge(vch, count[0])

            def lo(dst, src, hi, done):
                TT(dst, src, f32(hi), ALU.subtract).then_inc(done, 1)

            def rms_var(i):
                dve.wait_ge(n_ssq, i + 1)
                TS(var[:, i:i + 1], stat[:, i:i + 1], 1.0 / DM, EPS, ALU.mult, ALU.add).then_inc(n_var, 1)

            def rms_x(i):
                dve.wait_ge(n_rstd, i + 1)
                if i == 0:
                    dve.wait_ge(ld_small[1], 16)
                if i >= 2:
                    dve.wait_ge(n_t, i - 1)
                STT(xn[:, i % 2, :], res[:, i % 8, :], rstd[:, i:i + 1],
                    row_sb[:, i // 8 * DM:(i // 8 + 1) * DM], ALU.mult, ALU.mult).then_inc(n_x, 1)

            def norm_lo(i, banks):
                dve.wait_ge(n_hi, i + 1)
                b = i % 8
                lo(act_lo[:, :, b * L:(b + 1) * L], banks[i % 2][:, :].rearrange("p (k n) -> p k n", k=KT),
                   act_hi[:, :, b * L:(b + 1) * L], n_lo)

            nb = (bank[2], bank[3])
            V.memset(pre[:, :, :, :], 0.0).then_inc(setup_v, 1)
            V.memset(pow_m[:, :], -0.5).then_inc(setup_v, 1)
            rms_var(0)
            rms_var(1)
            rms_x(0)
            rms_x(1)
            rms_var(2)
            rms_x(2)
            rms_var(3)
            norm_lo(0, nb)
            rms_x(3)
            norm_lo(1, nb)
            norm_lo(2, nb)
            dve.wait_ge(dt_w, 1)
            TT(wdt_lo[:, :], wdt_raw[:, :], f32(wdt_hi[:, :]), ALU.subtract).then_inc(dt_w, 1)
            dve.wait_ge(ld_small[2], 16)
            dve.wait_ge(ld_small[5], 16)
            TS(cw[:, :], chan_sb[:, 0:NCONV * DCONV + NCONV], 0.5, None, ALU.mult)
            TS(d2[:, :], row_sb[:, 2 * DM + NH:2 * DM + 2 * NH], 0.5, None, ALU.mult).then_inc(setup_v, 1)
            norm_lo(3, nb)
            dve.wait_ge(setup_a, 1)
            TS(a2[:, :], a2[:, :], -2.0, None, ALU.mult)
            V.tensor_copy(sp[:, 6, 0:NH], row_sb[:, 2 * DM + 2 * NH:2 * DM + 3 * NH]).then_inc(setup_v, 1)

            def conv(q, beside=None):
                p = q % NCONV
                dve.wait_ge(conv_ev, q + 1)
                c = cbuf[:, q % 3, :].rearrange("p (s n) -> p s n", s=HALF)
                for k in (2, 1, 0):
                    t = STT(c, pre[:, q % 2, :, k:k + L], cw[:, p * DCONV + k:p * DCONV + k + 1], c,
                            ALU.mult, ALU.add)
                    if k == 0:
                        t.then_inc(conv_c, 1)
                    elif k == 1 and beside:
                        count[0] += 1
                        t.then_inc(vch, 1)
                        last_tap = count[0]
                        beside[0](beside[1])
                        dve.wait_ge(vch, last_tap)
                    else:
                        link(t)

            def conv_silu(q):
                dve.wait_ge(conv_th, q + 1)
                STT(xbc[:, q // NCONV, q % NCONV, :], th[:, 1 + q % 2, :], 1.0, cbuf[:, q % 3, :],
                    ALU.add, ALU.mult).then_inc(conv_out, 1)

            def z_silu(i):
                n, h = i // NH, i % NH
                f = NPIECE * n + NCONV + h
                dve.wait_ge(z_th, i + 1)
                STT(zt[:, h, n * NTOK:(n + 1) * NTOK], th[:, 0, :], 1.0, bank[f % 2][:, :], ALU.add, ALU.mult)\
                    .then_inc(z_out, 1)

            def dt_in(n):
                dve.wait_ge(dt_t, n + 1)
                bias = sp[:, 6, 0:NH].unsqueeze(1).to_broadcast([P, HALF, NH])
                link(TT(sp[:, 0, :].rearrange("p (b h) -> p b h", h=NH),
                        bank[6][:, 0:HALF * NH].rearrange("p (b h) -> p b h", h=NH), bias, ALU.add))
                link(TS(sp[:, 1, :], sp[:, 0, :], 0.0, None, ALU.min))
                link(TS(sp[:, 0, :], sp[:, 0, :], 0.0, None, ALU.max))
                link(TT(sp[:, 3, :], sp[:, 1, :], sp[:, 0, :], ALU.subtract))
                V.tensor_copy(sp[:, 1, :], sp[:, 3, :]).then_inc(dt_a, 1)

            def dt_out(n):
                dve.wait_ge(dt_exp_done, n + 1)
                link(TS(sp[:, 3, :], sp[:, 2, :], 2.0, None, ALU.add))
                link(V.reciprocal(sp[:, 4, :], sp[:, 3, :]))
                link(TT(sp[:, 3, :], sp[:, 2, :], sp[:, 4, :], ALU.mult))
                link(TT(sp[:, 4, :], sp[:, 3, :], sp[:, 3, :], ALU.mult))
                link(TS(sp[:, 5, :], sp[:, 4, :], 2.0 / (2 * ATANH_TERMS + 1), None, ALU.mult))
                for k in range(ATANH_TERMS - 1, 0, -1):
                    link(STT(sp[:, 5, :], sp[:, 5, :], 2.0 / (2 * k + 1), sp[:, 4, :], ALU.add, ALU.mult))
                link(STT(sp[:, 5, :], sp[:, 5, :], 2.0, sp[:, 3, :], ALU.add, ALU.mult))
                TT(dt_sb[:, n * HALF * NH:(n + 1) * HALF * NH], sp[:, 5, :], sp[:, 0, :], ALU.add)\
                    .then_inc(dt_done, 1)

            def att_mul(b):
                dve.wait_ge(em_done, b + 1)
                dve.wait_ge(sc_mm, b + 1)
                if b:
                    dve.wait_ge(y_mm, b)
                else:
                    dve.wait_ge(diag_done, 1)
                link(TT(att[:, :, :], em[:, b % 2, :, :], bank[3 + b % 2][:, :].rearrange("p (h n) -> p h n", h=NH),
                        ALU.mult))
                TT(att[:, :, :], att[:, :, :], diag_d[:, :, :], ALU.add).then_inc(att_done, 1)

            def y_out(b):
                dve.wait_ge(y_mm, b + 1)
                if b >= 2:
                    dve.wait_ge(ylo_done, b - 1)
                dve.wait_ge(z_out, NH * (b // HALF) + NH)
                TT(yb[:, b % 2, :, :], zt[:, :, b * L:(b + 1) * L],
                   bank[5][:, :].rearrange("p (h n) -> p h n", h=NH), ALU.mult).then_inc(y1_done, 1)

            def add_res(i, b, o):
                dve.wait_ge(o_mm, i + 1)
                TT(res[:, b, :], res[:, b, :], bank[o][:, :], ALU.add).then_inc(o_add, 1)

            tb = (bank[0], bank[1])
            conv(0)
            conv(1)
            conv_silu(0)
            dt_in(0)
            conv(2)
            conv_silu(1)
            rms_var(4)
            conv(3)
            conv_silu(2)
            rms_x(4)
            rms_var(5)
            conv(4)
            conv_silu(3)
            rms_x(5)
            rms_var(6)
            conv(5)
            norm_lo(4, nb)
            conv_silu(4)
            rms_x(6)
            rms_var(7)
            z_silu(0)
            conv_silu(5)
            norm_lo(5, nb)
            rms_x(7)
            z_silu(1)
            norm_lo(6, nb)
            z_silu(2)
            norm_lo(7, nb)
            z_silu(3)
            dt_out(0)
            conv(6)
            dt_in(1)
            conv_silu(6)
            att_mul(0)
            conv(7)
            att_mul(1)
            conv_silu(7)
            conv(8, (y_out, 0))
            att_mul(2)
            y_out(1)
            conv_silu(8)
            conv(9)
            att_mul(3)
            y_out(2)
            conv_silu(9)
            conv(10, (y_out, 3))
            dt_out(1)
            conv_silu(10)
            conv(11)
            conv_silu(11)
            z_silu(4)
            z_silu(5)
            att_mul(4)
            z_silu(6)
            z_silu(7)
            att_mul(5)
            y_out(4)
            add_res(0, 0, OUT_BANK[0])
            rms_var(8)
            y_out(5)
            att_mul(6)
            add_res(1, 1, OUT_BANK[1])
            rms_x(8)
            rms_var(9)
            y_out(6)
            att_mul(7)
            add_res(2, 2, OUT_BANK[2])
            rms_x(9)
            rms_var(10)
            y_out(7)
            add_res(3, 3, OUT_BANK[3])
            rms_x(10)
            rms_var(11)
            norm_lo(8, tb)
            add_res(4, 4, OUT_BANK[4])
            rms_x(11)
            rms_var(12)
            norm_lo(9, tb)
            add_res(5, 5, OUT_BANK[5])
            rms_var(13)
            norm_lo(10, tb)
            rms_x(12)
            add_res(6, 6, OUT_BANK[6])
            rms_var(14)
            norm_lo(11, tb)
            rms_x(13)
            add_res(7, 7, OUT_BANK[7])
            rms_var(15)
            norm_lo(12, tb)
            rms_x(14)

            def ln_stats(i):
                b = i % 8
                if i >= 18:
                    dve.wait_ge(n_mv, i - 17)
                V.bn_stats(bst[:, i % 2, :], res[:, b, :]).then_inc(n_bn, 1)
                dve.wait_ge(n_bn, i - 15)
                V.bn_aggr(mv[:, i, :], bst[:, i % 2, :]).then_inc(n_mv, 1)
                dve.wait_ge(n_mv, i - 15)
                TS(var[:, i:i + 1], mv[:, i, 1:2], EPS, None, ALU.add).then_inc(n_var, 1)

            def ln_x(i):
                b = i % 8
                dve.wait_ge(n_rstd, i + 1)
                dve.wait_ge(n_t, i - 1)
                TS(xn[:, i % 2, :], res[:, b, :], mv[:, i, 0:1], rstd[:, i:i + 1], ALU.subtract, ALU.mult)\
                    .then_inc(n_x, 1)

            def ctx_rest(i):
                dve.wait_ge(cx_h, i + 1)
                cs = slice(i % 2 * 512, (i % 2 + 1) * 512)
                lo(ctx_lo[:, i // 2, cs], raw_b[:, 1024 + i % 2 * 512:1536 + i % 2 * 512],
                   ctx_hi[:, i // 2, cs], cx_l)

            def v_rest(g, n, j):
                i = 8 * g + 4 * n + j
                dve.wait_ge(vhi_done, i + 1)
                lo(v_lo[:, n, j, :], kv_bank(g, n, j)[:, HD:2 * HD], v_hi[:, n, j, :], vlo_done)
                if j == 0 and not (isinstance(g, int) and 2 * g + n == 0):
                    dve.wait_ge(kt_mm, 2 * g + n)
                V.tensor_copy(kraw[:, j, :], kv_bank(g, n, j)[:, 0:HD]).then_inc(kraw_done, 1)

            def mlp_step(c):
                first, last = (isinstance(c, int) and c == x for x in (0, MLP_IT - 1))
                for m_i in range(4):
                    dve.wait_ge(silu_done, 4 * c + m_i + 1)
                    dve.wait_ge(gu_mm, 4 * c + m_i + 1)
                    if not (isinstance(c, int) and 4 * c + m_i < 2):
                        dve.wait_ge(hlo_done, 4 * c + m_i - 1)
                    TT(hb[:, m_i % 2, :], sg[:, m_i % 2, :], bank[(3, 5)[m_i % 2]][:, :], ALU.mult)\
                        .then_inc(h_done, 1)
                    if first:
                        if m_i == 0:
                            norm_lo(13, tb)
                            rms_x(15)
                            norm_lo(14, tb)
                            norm_lo(15, tb)
                        if m_i < 3:
                            ctx_rest(2 * m_i)
                            ctx_rest(2 * m_i + 1)
                for b in range(B):
                    if first:
                        if b == 4:
                            ctx_rest(6)
                            ctx_rest(7)
                        dve.wait_ge(x_add, b + 1)
                    add_res(8 + 8 * c + b, b, 6 + b % 2)
                    if last:
                        dve.wait_ge(o_add, 9 + 8 * c + b)
                        ln_stats(16 + b)
                        if b >= 1:
                            ln_x(15 + b)
                        if 3 <= b < 7:
                            v_rest(0, 0, b - 3)
                        if b >= 2:
                            norm_lo(14 + b, tb if b < 6 else (bank[4], bank[5]))

            mlp_step(0)
            with dve.Fori(1, MLP_IT - 1) as c:
                mlp_step(c)
            mlp_step(MLP_IT - 1)

            def k_var(g, n):
                dve.wait_ge(ksq_done, 8 * g + 4 * n + 4)
                if not (isinstance(g, int) and g == n == 0):
                    dve.wait_ge(kr_done, 2 * g + n)
                TS(kv[:, 1, :], kv[:, 0, :], 1.0 / HD, EPS, ALU.mult, ALU.add).then_inc(kvar_done, 1)

            def k_norm(g, n):
                dve.wait_ge(kr_done, 2 * g + n + 1)
                dve.wait_ge(kraw_done, 8 * g + 4 * n + 4)
                TT(kraw[:, :, :], kraw[:, :, :], kv[:, 2, :].unsqueeze(2).to_broadcast([P, HALF, HD]), ALU.mult)\
                    .then_inc(kn_done, 1)

            def q_var(g, n, h):
                i = 8 * g + 4 * n + h
                dve.wait_ge(qsq_done, i + 1)
                if not (isinstance(g, int) and 8 * g + 4 * n < 8):
                    dve.wait_ge(qr_done, 8 * g + 4 * n - 3)
                TS(qv[:, 4 * n + h, :], qss[:, h % 2, :], HD * EPS, None, ALU.add).then_inc(qv_done, 1)

            def softmax_max(g, jj):
                n, j = jj // HALF, jj % HALF
                t_i = 8 * g + jj
                dve.wait_ge(s_mm, t_i + 1)
                dve.wait_ge(qr_done, 8 * g + 4 * n + 4)
                if not (isinstance(g, int) and t_i < 2):
                    dve.wait_ge(pt_mm, t_i - 1)
                for h in range(GH):
                    t = STT(pb[:, jj % 2, h, :], bank[3][:, h * L:(h + 1) * L], qr[:, 4 * n + h, j:j + 1],
                            mask_sb[:, :], ALU.mult, ALU.add)
                t.then_inc(s_done, 1)
                dve.wait_ge(s_done, t_i + 1)
                V.tensor_reduce(nmax[:, jj % 2, :], pb[:, jj % 2, :, :], X, ALU.max, negate=True)\
                    .then_inc(max_done, 1)

            def softmax_rec(g, jj):
                dve.wait_ge(p_exp, 8 * g + jj + 1)
                V.reciprocal(prec[:, jj % 2, :], psum_[:, jj % 2, :]).then_inc(p_rec, 1)

            def pt_rest(g, jj):
                dve.wait_ge(pthi_done, 8 * g + jj + 1)
                lo(pt_lo[:, :], bank[4][:, :], pt_hi[:, :], ptlo_done)

            def ot_rest(g, jj):
                dve.wait_ge(othi_done, 8 * g + jj + 1)
                lo(ot_lo[:, :], bank[5][:, :], ot_hi[:, :], otlo_done)

            def add_out(g, jj):
                t_i = 8 * g + jj
                dve.wait_ge(d_mm, t_i + 1)
                TT(res[:, jj, :], res[:, jj, :], bank[6][:, :], ALU.add).then_inc(d_add, 1)

            def slot(g, jj, produce, before=True):
                n, j = jj // HALF, jj % HALF
                pg, pn = (g, 1) if n == 0 else (g + 1, 0)
                if j == 0:
                    if produce:
                        v_rest(pg, pn, 0)
                    softmax_rec(g, jj)
                if j < 3:
                    softmax_max(g, jj + 1)
                    if produce:
                        v_rest(pg, pn, j + 1)
                if produce and j == 2:
                    k_var(pg, pn)
                pt_rest(g, jj)
                if produce:
                    q_var(pg, pn, j)
                if j < 3:
                    softmax_rec(g, jj + 1)
                if produce and j == 2:
                    k_norm(pg, pn)
                if before:
                    add_out(*((g, jj - 1) if jj else (g - 1, 7)))
                ot_rest(g, jj)
                if j == 3 and produce:
                    softmax_max(pg, 4 * pn)

            k_var(0, 0)
            ln_x(23)
            q_var(0, 0, 0)
            norm_lo(22, (bank[4], bank[5]))
            k_norm(0, 0)
            q_var(0, 0, 1)
            norm_lo(23, (bank[4], bank[5]))
            q_var(0, 0, 2)
            q_var(0, 0, 3)
            dve.wait_ge(res_x, 8)
            dve.wait_ge(ld_small[4], 16)
            softmax_max(0, 0)
            slot(0, 0, True, before=False)
            with dve.Fori(0, GROUPS - 1) as g:
                for jj in range(1, 8):
                    slot(g, jj, True)
                slot(g + 1, 0, True)

            def ln2(i):
                b = i % 8
                dve.wait_ge(n_rstd, i + 1)
                TS(res[:, b, :], res[:, b, :], mv[:, i, 0:1], rstd[:, i:i + 1], ALU.subtract, ALU.mult).then_inc(n_x, 1)

            def last_mean(b):
                dve.wait_ge(n_rstd, 33 + b)
                STT(mr[:, b:b + 1], mv[:, 32 + b, 0:1], -1.0, rstd[:, 32 + b:33 + b], ALU.mult, ALU.mult)\
                    .then_inc(mr_done, 1)

            def gates_rank(i):
                tl = slice(4 * i, 4 * i + 4)
                ps = bank[(2, 7)[i]][:, 0:4 * RAC].rearrange("p (b c) -> p b c", b=4)
                dve.wait_ge(ra_mm, 4 * i + 4)
                link(V.tensor_copy(lg[:, tl, :], ps[:, :, 0:NE]))
                own = lg[:, tl, :].unsqueeze(3).to_broadcast([P, 4, NE, NE])
                other = lg[:, tl, :].unsqueeze(2).to_broadcast([P, 4, NE, NE])
                TT(c1[:, tl, :, :], other, own, ALU.is_ge)
                link(TT(c2[:, tl, :, :], other, own, ALU.is_gt))
                TT(c1[:, tl, :, :], c1[:, tl, :, :], cmp_m[:, 0, :, :].unsqueeze(1).to_broadcast([P, 4, NE, NE]),
                   ALU.mult)
                link(TT(c2[:, tl, :, :], c2[:, tl, :, :],
                        cmp_m[:, 1, :, :].unsqueeze(1).to_broadcast([P, 4, NE, NE]), ALU.mult))
                link(TT(c1[:, tl, :, :].rearrange("p b e f -> p (b e f)"), c1[:, tl, :, :].rearrange("p b e f -> p (b e f)"),
                        c2[:, tl, :, :].rearrange("p b e f -> p (b e f)"), ALU.add))
                V.tensor_reduce(rank_t[:, tl, :].rearrange("p b e -> p (b e)"),
                                c1[:, tl, :, :].rearrange("p b e f -> p (b e) f"), X, ALU.add)
                link(V.tensor_reduce(lmax[:, tl], lg[:, tl, :], X, ALU.max))
                TT(ge[:, tl, :], lg[:, tl, :], lmax[:, tl].unsqueeze(2).to_broadcast([P, 4, NE]), ALU.subtract)\
                    .then_inc(lg_done, 1)

            def gates_mid(i):
                tl = slice(4 * i, 4 * i + 4)
                ps = bank[(2, 7)[i]][:, 0:4 * RAC].rearrange("p (b c) -> p b c", b=4)
                dve.wait_ge(f_exp, i + 1)
                fl = ge[:, tl, :].rearrange("p b e -> p (b e)")
                link(STT(fl, rank_t[:, tl, :].rearrange("p b e -> p (b e)"), 1.5, fl, ALU.is_lt, ALU.mult))
                link(V.tensor_reduce(gsum[:, tl], ge[:, tl, :], X, ALU.add))
                link(V.reciprocal(gsum[:, tl], gsum[:, tl]))
                link(TS(gsum[:, tl], gsum[:, tl], LORA_SCALE, None, ALU.mult))
                link(TT(ge[:, tl, :], ge[:, tl, :], gsum[:, tl].unsqueeze(2).to_broadcast([P, 4, NE]), ALU.mult))
                TT(mid[:, tl, :, :], ps[:, :, NE:].rearrange("p b (e r) -> p b e r", e=NE),
                   ge[:, tl, :].unsqueeze(3).to_broadcast([P, 4, NE, RANK]), ALU.mult).then_inc(mid_done, 1)

            def add_delta(b):
                dve.wait_ge(dl_mm, b + 1)
                TT(res[:, b, :], res[:, b, :], bank[3 + b % 2][:, :], ALU.add).then_inc(dl_add, 1)
                dve.wait_ge(dl_add, b + 1)

            for e in range(NE):
                V.memset(cmp_m[:, 0, e, :], 0.0)
                t = V.memset(cmp_m[:, 1, e, :], 0.0)
            link(t)
            for e in range(NE):
                if e:
                    t = V.memset(cmp_m[:, 0, e, 0:e], 1.0)
                if e < NE - 1:
                    t = V.memset(cmp_m[:, 1, e, e + 1:NE], 1.0)
            link(t)

            last = GROUPS - 1

            def last_slot(jj):
                b = jj - 1
                if jj == 4:
                    add_out(last, b)
                    softmax_rec(last, 4)
                if jj < 7:
                    softmax_max(last, jj + 1)
                else:
                    gates_mid(0)
                pt_rest(last, jj)
                if jj < 7:
                    softmax_rec(last, jj + 1)
                if jj > 4:
                    add_out(last, b)
                dve.wait_ge(d_add, 8 * last + b + 1)
                ln_stats(24 + b)
                ot_rest(last, jj)
                ln2(24 + b)
                if jj == 6:
                    gates_rank(0)

            for jj in range(1, 4):
                slot(last, jj, True)
                b = jj - 1
                dve.wait_ge(d_add, 8 * last + b + 1)
                ln_stats(24 + b)
                if b:
                    ln2(23 + b)
            ln2(26)
            for jj in range(4, 8):
                last_slot(jj)
            add_delta(0)
            add_out(last, 7)
            dve.wait_ge(d_add, 8 * GROUPS)
            ln_stats(31)
            ln_stats(32)
            ln2(31)
            add_delta(1)
            ln_stats(33)
            last_mean(0)
            gates_rank(1)
            add_delta(2)
            ln_stats(34)
            last_mean(1)
            gates_mid(1)
            for b in range(3, B):
                add_delta(b)
                ln_stats(32 + b)
                last_mean(b - 1)
            last_mean(7)


_OUT = ((B, L, DM), "float32")


def kernel(x, ctx_4096, mask_1x1xSxS2_ff0, L0_attn_w_in, L0_attn_conv_w, L0_attn_conv_b, L0_attn_A_log,
           L0_attn_D, L0_attn_dt_bias, L0_attn_w_out, L0_attn_ln1_w, L0_attn_ln2_w, L0_attn_gate_w,
           L0_attn_up_w, L0_attn_down_w, L0_xattn_Wq, L0_xattn_Wk, L0_xattn_Wv, L0_xattn_Wo,
           L0_xattn_q_norm_w, L0_xattn_k_norm_w, L0_ffn_router_w, L0_ffn_A, L0_ffn_B):
    import numpy as np
    import concourse.bacc as bacc
    from concourse.bass_utils import run_bass_kernel_spmd

    a = np.asarray

    def pieces(w, cols):
        n = w.shape[0] // cols
        return a(w).reshape(n, cols, KT, P).transpose(0, 3, 2, 1).reshape(n, P, KT * cols)

    w_in = a(L0_attn_w_in)
    cut = [0, 512, 1280, 1284]
    z, xbc, dt = (w_in[cut[i]:cut[i + 1]] for i in range(3))
    gate, up = pieces(L0_attn_gate_w, P), pieces(L0_attn_up_w, P)
    w_gu = np.stack([gate.reshape(MLP_IT, 2, P, 512), up.reshape(MLP_IT, 2, P, 512)], 2)
    w_q = pieces(L0_xattn_Wq, P).reshape(GROUPS, GH, P, 512).transpose(0, 2, 1, 3).reshape(GROUPS, P, 2048)
    wk, wv = (a(w).reshape(GROUPS, HD, KT, P).transpose(0, 3, 2, 1) for w in (L0_xattn_Wk, L0_xattn_Wv))
    w_o = a(L0_xattn_Wo).T.reshape(GROUPS, GH, HD, DM).transpose(0, 2, 1, 3).reshape(GROUPS, P, 2048)
    idx = np.arange(P)
    tri = (idx[:, None] <= idx[None, :]).astype(np.float32) * np.float32(0.5)
    strict = (idx[:, None] > idx[None, :]).astype(np.float32)
    arrays = {
        "x": a(x),
        "ctx_t": a(ctx_4096).reshape(B * L, KT, P).transpose(1, 2, 0),
        "mask": a(mask_1x1xSxS2_ff0).reshape(L, L),
        "consts": np.concatenate([np.eye(P, dtype=np.float32), tri, strict], 1),
        "chan": np.concatenate([a(L0_attn_conv_w).reshape(NCONV, P, DCONV).transpose(1, 0, 2).reshape(P, -1),
                                a(L0_attn_conv_b).reshape(NCONV, P).T,
                                a(L0_xattn_q_norm_w)[:, None], a(L0_xattn_k_norm_w)[:, None]], 1),
        "rows": np.concatenate([a(L0_attn_ln1_w), a(L0_attn_ln2_w), a(L0_attn_A_log), a(L0_attn_D),
                                a(L0_attn_dt_bias)]),
        "w_dt": dt.reshape(NH, KT, P).transpose(2, 1, 0).reshape(P, KT * NH),
        "w_in": pieces(np.concatenate([xbc, z], 0), P),
        "w_out": a(L0_attn_w_out).T.reshape(NH, P, DM).transpose(1, 0, 2).reshape(P, NH * DM),
        "w_gu": w_gu.transpose(0, 3, 1, 2, 4).reshape(MLP_IT, P, 2048),
        "w_dn": a(L0_attn_down_w).T.reshape(MLP_IT, 2, P, DM).transpose(0, 2, 1, 3).reshape(MLP_IT, P, 1024),
        "w_q": w_q,
        "w_kv": np.concatenate([wk, wv], 3).reshape(GROUPS, P, 1024),
        "w_o": w_o,
        "w_ra": np.concatenate([a(L0_ffn_router_w), a(L0_ffn_A).reshape(NE * RANK, DM)], 0)
                  .reshape(NE + NE * RANK, KT, P).transpose(2, 1, 0),
        "w_b": a(L0_ffn_B).transpose(0, 2, 1).reshape(NE * RANK, DM),
    }
    arrays = {k: np.ascontiguousarray(v) for k, v in arrays.items()}
    nc = bacc.Bacc("TRN2", target_bir_lowering=False, num_devices=1)
    args = {k: nc.dram_tensor(f"in_{k}", v.shape, mybir.dt.from_np(v.dtype), kind="ExternalInput").ap()
            for k, v in arrays.items()}
    o = nc.dram_tensor("out_0", _OUT[0], mybir.dt.float32, kind="ExternalOutput").ap()
    build_program(nc, **args, out=o)
    r = run_bass_kernel_spmd(nc, [{f"in_{k}": v for k, v in arrays.items()}], core_ids=[0])
    return r.results[0]["out_0"]
```
